# Optimizing a Trainium2 kernel written in Bass

```python
import numpy as np
import jax
import jax.numpy as jnp

def _softmax(x, axis=-1):
    return jax.nn.softmax(x, axis=axis)

def _gelu(x):
    return jax.nn.gelu(x, approximate=True)

def _silu(x):
    return jax.nn.silu(x)

def _sigmoid(x):
    return jax.nn.sigmoid(x)

def _layernorm(x, axis=-1, eps=1e-05):
    m = jnp.mean(x, axis=axis, keepdims=True)
    v = jnp.var(x, axis=axis, keepdims=True)
    return (x - m) / jnp.sqrt(v + eps)

def _scatter_add(tgt, idx, src, axis=0):
    return tgt.at[idx].add(src)

def _segment_sum(src, seg, n):
    return jax.ops.segment_sum(src, seg, n)
kernel_name = 'mk_sandwich_d1_jaxref_r8_4e9f6f'

def setup_inputs(seed: int=0):
    np.random.seed(seed)
    _w = jnp.asarray

    def _L0_attn_setup():
        import jax, jax.numpy as jnp
        import numpy as np
        D_MODEL = 256
        NUM_HEADS = 16
        D_Q = 192
        D_KV = 64
        BS, SL = (2, 256)

        def _lin(x, w, b):
            return jnp.einsum('...i,oi->...o', x, w) + b

        def _freqs(seq_len, dim, theta=10000.0):
            exps = jnp.arange(0, dim, 2, dtype=jnp.float32)
            tn = 1.0 / (theta ** exps / dim)
            m = jnp.arange(seq_len, dtype=jnp.float32)
            ang = jnp.outer(m, tn)
            return (jnp.cos(ang), jnp.sin(ang))

        def _rope(x, cos, sin):
            xe = x[..., 0::2]
            xo = x[..., 1::2]
            re = xe * cos - xo * sin
            im = xe * sin + xo * cos
            return jnp.stack([re, im], axis=-1).reshape(x.shape)

        def _init_linear(key, out_f, in_f):
            k1, k2 = jax.random.split(key)
            bound = 1.0 / np.sqrt(in_f)
            w = jax.random.uniform(k1, (out_f, in_f), jnp.float32, -bound, bound)
            b = jax.random.uniform(k2, (out_f,), jnp.float32, -bound, bound)
            return (w, b)
        key = jax.random.key(seed)
        ks = jax.random.split(key, 9)
        x = jax.random.normal(ks[0], (BS, SL, D_MODEL), jnp.float32)
        w_down_q, b_down_q = _init_linear(ks[1], D_Q, D_MODEL)
        w_up_q, b_up_q = _init_linear(ks[2], D_MODEL, D_Q)
        w_down_kv, b_down_kv = _init_linear(ks[3], D_KV, D_MODEL)
        w_up_k, b_up_k = _init_linear(ks[4], D_MODEL, D_KV)
        w_up_v, b_up_v = _init_linear(ks[5], D_MODEL, D_KV)
        wq_r, bq_r = _init_linear(ks[6], D_MODEL, D_Q)
        wk_r, bk_r = _init_linear(ks[7], D_MODEL, D_KV)
        wo, bo = _init_linear(ks[8], D_MODEL, D_MODEL)
        return dict(x=x, w_down_q=w_down_q, b_down_q=b_down_q, w_up_q=w_up_q, b_up_q=b_up_q, w_down_kv=w_down_kv, b_down_kv=b_down_kv, w_up_k=w_up_k, b_up_k=b_up_k, w_up_v=w_up_v, b_up_v=b_up_v, wq_r=wq_r, bq_r=bq_r, wk_r=wk_r, bk_r=bk_r, wo=wo, bo=bo)
    _L0_attn_in = _L0_attn_setup()

    def _L0_ffn_setup():
        import jax, jax.numpy as jnp
        import numpy as np
        E, H, I = (8, 256, 512)
        TOP_K = 1
        B, S = (1, 256)
        key = jax.random.key(seed)
        ks = jax.random.split(key, 7)
        std = 0.02
        return {'hidden_states': jax.random.normal(ks[0], (B, S, H), dtype=jnp.float32), 'router_w': jax.random.normal(ks[1], (E, H), dtype=jnp.float32) * std, 'gate_up_proj': jax.random.normal(ks[2], (E, H, 2 * I), dtype=jnp.float32) * std, 'down_proj': jax.random.normal(ks[3], (E, I, H), dtype=jnp.float32) * std, 'shared_gate_w': jax.random.normal(ks[4], (H, I), dtype=jnp.float32) * std, 'shared_up_w': jax.random.normal(ks[5], (H, I), dtype=jnp.float32) * std, 'shared_down_w': jax.random.normal(ks[6], (I, H), dtype=jnp.float32) * std}
    _L0_ffn_in = _L0_ffn_setup()
    _d = {'L0_attn_x': _L0_attn_in['x'], 'L0_attn_w_down_q': _L0_attn_in['w_down_q'], 'L0_attn_b_down_q': _L0_attn_in['b_down_q'], 'L0_attn_w_up_q': _L0_attn_in['w_up_q'], 'L0_attn_b_up_q': _L0_attn_in['b_up_q'], 'L0_attn_w_down_kv': _L0_attn_in['w_down_kv'], 'L0_attn_b_down_kv': _L0_attn_in['b_down_kv'], 'L0_attn_w_up_k': _L0_attn_in['w_up_k'], 'L0_attn_b_up_k': _L0_attn_in['b_up_k'], 'L0_attn_w_up_v': _L0_attn_in['w_up_v'], 'L0_attn_b_up_v': _L0_attn_in['b_up_v'], 'L0_attn_wq_r': _L0_attn_in['wq_r'], 'L0_attn_bq_r': _L0_attn_in['bq_r'], 'L0_attn_wk_r': _L0_attn_in['wk_r'], 'L0_attn_bk_r': _L0_attn_in['bk_r'], 'L0_attn_wo': _L0_attn_in['wo'], 'L0_attn_bo': _L0_attn_in['bo'], 'L0_ffn_router_w': _L0_ffn_in['router_w'], 'L0_ffn_gate_up_proj': _L0_ffn_in['gate_up_proj'], 'L0_ffn_down_proj': _L0_ffn_in['down_proj'], 'L0_ffn_shared_gate_w': _L0_ffn_in['shared_gate_w'], 'L0_ffn_shared_up_w': _L0_ffn_in['shared_up_w'], 'L0_ffn_shared_down_w': _L0_ffn_in['shared_down_w']}
    _x0 = _d['L0_attn_x']
    _d['L0_attn_x'] = jax.random.normal(jax.random.fold_in(jax.random.key(seed), 1), (8, 256, 256), dtype=_x0.dtype)
    del _x0
    return _d

def reference(L0_attn_x, L0_attn_w_down_q, L0_attn_b_down_q, L0_attn_w_up_q, L0_attn_b_up_q, L0_attn_w_down_kv, L0_attn_b_down_kv, L0_attn_w_up_k, L0_attn_b_up_k, L0_attn_w_up_v, L0_attn_b_up_v, L0_attn_wq_r, L0_attn_bq_r, L0_attn_wk_r, L0_attn_bk_r, L0_attn_wo, L0_attn_bo, L0_ffn_router_w, L0_ffn_gate_up_proj, L0_ffn_down_proj, L0_ffn_shared_gate_w, L0_ffn_shared_up_w, L0_ffn_shared_down_w):

    def _L0_attn_ref(x, w_down_q, b_down_q, w_up_q, b_up_q, w_down_kv, b_down_kv, w_up_k, b_up_k, w_up_v, b_up_v, wq_r, bq_r, wk_r, bk_r, wo, bo):
        import jax, jax.numpy as jnp
        import numpy as np
        D_MODEL = 256
        NUM_HEADS = 16
        D_Q = 192
        D_KV = 64
        BS, SL = (2, 256)

        def _lin(x, w, b):
            return jnp.einsum('...i,oi->...o', x, w) + b

        def _freqs(seq_len, dim, theta=10000.0):
            exps = jnp.arange(0, dim, 2, dtype=jnp.float32)
            tn = 1.0 / (theta ** exps / dim)
            m = jnp.arange(seq_len, dtype=jnp.float32)
            ang = jnp.outer(m, tn)
            return (jnp.cos(ang), jnp.sin(ang))

        def _rope(x, cos, sin):
            xe = x[..., 0::2]
            xo = x[..., 1::2]
            re = xe * cos - xo * sin
            im = xe * sin + xo * cos
            return jnp.stack([re, im], axis=-1).reshape(x.shape)

        def _init_linear(key, out_f, in_f):
            k1, k2 = jax.random.split(key)
            bound = 1.0 / np.sqrt(in_f)
            w = jax.random.uniform(k1, (out_f, in_f), jnp.float32, -bound, bound)
            b = jax.random.uniform(k2, (out_f,), jnp.float32, -bound, bound)
            return (w, b)
        bs, sl, dim = x.shape
        nh, hd = (NUM_HEADS, dim // NUM_HEADS)
        cos, sin = _freqs(sl, dim)
        ct_q = _lin(x, w_down_q, b_down_q)
        q_ct = _lin(ct_q, w_up_q, b_up_q)
        rope_q = _rope(_lin(ct_q, wq_r, bq_r), cos, sin)
        q = (q_ct + rope_q).reshape(bs, sl, nh, hd)
        ct_kv = _lin(x, w_down_kv, b_down_kv)
        k_ct = _lin(ct_kv, w_up_k, b_up_k)
        rope_k = _rope(_lin(ct_kv, wk_r, bk_r), cos, sin)
        k = (k_ct + rope_k).reshape(bs, sl, nh, hd)
        v = _lin(ct_kv, w_up_v, b_up_v).reshape(bs, sl, nh, hd)
        scores = jnp.einsum('bqhd,bkhd->bhqk', q, k) / np.sqrt(hd)
        probs = jax.nn.softmax(scores, axis=-1)
        a = jnp.einsum('bhqk,bkhd->bqhd', probs, v).reshape(bs, sl, nh * hd)
        return _lin(a, wo, bo)

    def _L0_ffn_ref(hidden_states, router_w, gate_up_proj, down_proj, shared_gate_w, shared_up_w, shared_down_w):
        import jax, jax.numpy as jnp
        import numpy as np
        E, H, I = (8, 256, 512)
        TOP_K = 1
        B, S = (1, 256)
        orig_shape = hidden_states.shape
        x = hidden_states.reshape(-1, H)
        T = x.shape[0]
        logits = x @ router_w.T
        top_vals, top_idx = jax.lax.top_k(logits, TOP_K)
        scores = jnp.full_like(logits, -jnp.inf)
        scores = scores.at[jnp.arange(T)[:, None], top_idx].set(top_vals)
        scores = jax.nn.sigmoid(scores.astype(jnp.float32)).astype(logits.dtype)
        xr = x[None, :, :] * scores.T[:, :, None]
        gate_up = jnp.einsum('eth,ehf->etf', xr, gate_up_proj)
        gate, up = jnp.split(gate_up, 2, axis=-1)
        routed = jnp.einsum('etf,efh->eth', up * jax.nn.silu(gate), down_proj)
        routed_sum = routed.sum(axis=0)
        shared = jax.nn.silu(x @ shared_gate_w) * (x @ shared_up_w) @ shared_down_w
        return (shared + routed_sum).reshape(orig_shape)
    x = L0_attn_x
    x = x + _layernorm(_L0_attn_ref(_layernorm(x, axis=-1), L0_attn_w_down_q, L0_attn_b_down_q, L0_attn_w_up_q, L0_attn_b_up_q, L0_attn_w_down_kv, L0_attn_b_down_kv, L0_attn_w_up_k, L0_attn_b_up_k, L0_attn_w_up_v, L0_attn_b_up_v, L0_attn_wq_r, L0_attn_bq_r, L0_attn_wk_r, L0_attn_bk_r, L0_attn_wo, L0_attn_bo), axis=-1)
    x = x + _layernorm(_L0_ffn_ref(_layernorm(x, axis=-1), L0_ffn_router_w, L0_ffn_gate_up_proj, L0_ffn_down_proj, L0_ffn_shared_gate_w, L0_ffn_shared_up_w, L0_ffn_shared_down_w), axis=-1)
    return x

_drawn_inputs = setup_inputs


def setup_inputs(seed=0):
    import zlib

    import numpy as np

    out = dict(_drawn_inputs(seed))
    spreads = {}
    factors = {'L0_attn_b_down_q': 3.386,
     'L0_attn_b_up_q': 4.062,
     'L0_attn_b_up_k': 64.0,
     'L0_attn_bq_r': 3.615,
     'L0_attn_bk_r': 36.486}
    for name, (base, spread) in spreads.items():
        noise = np.random.default_rng([zlib.crc32(name.encode()), seed]).standard_normal(out[name].shape)
        drawn = base * np.exp(spread * noise) if base else spread * noise
        out[name] = jnp.asarray(drawn.astype(out[name].dtype))
    for name, factor in factors.items():
        out[name] = (out[name] * factor).astype(out[name].dtype)
    return out
```

```python
from contextlib import ExitStack

import numpy as np

import concourse.bass as bass
from concourse import mybir

F32 = mybir.dt.float32
BF16 = mybir.dt.bfloat16
I32 = mybir.dt.int32
ALU = mybir.AluOpType
ACT = mybir.ActivationFunctionType
AX = mybir.AxisListType
ds = bass.ds

P = 128
B, S, D = 8, 256, 256
NH, HD = 16, 16
DQ, DKV = 192, 64
E, I = 8, 512
NT = B * S // P
TB = S // P
KT = D // P
NR = NT + E - 1
HALF = NT // 2
EPS = 1e-5
SCALE = 1.0 / float(np.sqrt(HD))
NPART = 3
K_SLOTS = (0, 0, 0, 1, 1, 2)
Q_SLOTS = (0, 1, 2, 0, 1, 0)
NSLOT = len(K_SLOTS)
ROWS = NSLOT * HD
MROWS = ROWS + NPART
HT = P // HD
WLEN = KT * 2 * I + (I // P) * D

C_ID, C_TRI, C_COS, C_SIN = 0, 128, 256, 512
C_DESC, C_TILE, C_LE, C_NUM = 768, 776, 792, 856
C_END = C_NUM + NR


def head_minor(a):
    return np.moveaxis(a.reshape(*a.shape[:-1], -1, HT, HD), -1, -2).reshape(a.shape)


def constants():
    t = np.zeros((P, C_END), np.float32)
    t[:, C_ID:C_ID + P] = np.eye(P)
    t[:, C_TRI:C_TRI + P] = np.triu(np.ones((P, P)), 1)
    exps = np.arange(0, D, 2, dtype=np.float32)
    inside = exps < 10
    tn = np.zeros_like(exps)
    tn[inside] = np.float32(1.0) / (np.float32(10000.0) ** exps[inside] / np.float32(D))
    assert not tn[P // 2:].any()
    ang = np.outer(np.arange(S, dtype=np.float32), tn).astype(np.float32)
    cos, sin = np.cos(ang), np.sin(ang)
    for row, f in enumerate(head_minor(np.arange(P))):
        t[row, C_COS:C_COS + S] = cos[:, f // 2]
        t[row, C_SIN:C_SIN + S] = sin[:, f // 2] * (1 if f % 2 else -1)
    t[:, C_DESC:C_DESC + E] = E - np.arange(E)
    t[:, C_TILE:C_TILE + NT] = P * np.arange(NT)
    t[:, C_LE:C_LE + E * E] = (np.arange(E)[None, :] <= np.arange(E)[:, None]).reshape(-1)
    t[:, C_NUM:C_NUM + NR] = np.arange(NR)
    return t


def program(nc, x, const, w_down, w_q, w_kv, w_out, w_router, bias_col, bias_v, bias_o,
            gate_up, down, sh_gate, sh_up, sh_down, out):
    x_tok = nc.dram_tensor("x_tok", [NT * P, D], F32, kind="Internal").ap()
    x_exp = nc.dram_tensor("x_exp", [NR * P, D], F32, kind="Internal").ap()
    y_exp = nc.dram_tensor("y_exp", [NR * P, D], F32, kind="Internal").ap()
    with ExitStack() as ctx:
        def sb(name, shape, dt=F32):
            return ctx.enter_context(nc.sbuf_tensor(name, shape, dt))

        def sem(name):
            return ctx.enter_context(nc.semaphore(name))

        wall = sb("wall", [P, E + 1, WLEN])
        x_sb = sb("x_sb", [P, NT, D])
        cst = sb("cst", [P, C_END])
        wd_sb = sb("wd_sb", [P, KT, D])
        wq_sb = sb("wq_sb", [P, KT, 2 * D])
        wkv_sb = sb("wkv_sb", [P, 3 * D])
        wo_sb = sb("wo_sb", [P, KT, D])
        wr_sb = sb("wr_sb", [P, KT, E])
        bcol = sb("bcol", [P, 12])
        bv_sb = sb("bv_sb", [P, D])
        bo_sb = sb("bo_sb", [P, D])
        stacks = sb("stacks", [P, 2, 2, NH, S], BF16)
        pv = sb("pv", [P, 4096])
        probs = pv[:, 0:2048].rearrange("p (n c) -> p n c", n=4)
        v_aug = pv[:, 2048:4096].rearrange("p (b t h c) -> p b t h c", b=2, t=TB, h=NH)
        spare = wall[:, E - 1, :]
        qf = spare[:, 0:512].rearrange("p (m c) -> p m c", m=2)
        kf = spare[:, 512:1024].rearrange("p (m c) -> p m c", m=2)
        xn = spare[:, 1024:1536].rearrange("p (t c) -> p t c", t=TB)
        xnT = spare[:, 1536:2048].rearrange("p (k c) -> p k c", k=KT)
        ctT = spare[:, 2048:2560].rearrange("p (k c) -> p k c", k=KT)
        a_sb = spare[:, 2560:3072].rearrange("p (t c) -> p t c", t=TB)
        spare2 = wall[:, E - 2, :]
        o_sb = spare2[:, 0:1024].rearrange("p (g c) -> p g c", g=4)
        aT = spare2[:, 1024:1536].rearrange("p (k c) -> p k c", k=KT)
        y_sb = spare2[:, 1536:2048].rearrange("p (t c) -> p t c", t=TB)
        xn2 = spare2[:, 2048:2560].rearrange("p (t c) -> p t c", t=TB)
        xn2T = spare2[:, 2560:3072].rearrange("p (k c) -> p k c", k=KT)
        yr = {"q": sb("yr_q", [P, S]), "k": sb("yr_k", [P, S])}
        swp = {"q": sb("swp_q", [P, S]), "k": sb("swp_k", [P, S])}
        parts = {"q": sb("parts_q", [P, NPART, 2, S], BF16), "k": sb("parts_k", [P, NPART, 2, S], BF16)}
        full = {"q": qf, "k": kf}
        nmax = sb("nmax", [P, 2, TB, NH // 2])
        nres = sb("nres", [P, 2, TB, NH // 2])
        mparts = sb("mparts", [P, TB, NPART, NH // 2], BF16)
        mT = sb("mT", [NPART * NH // 2, S], BF16)
        idb = sb("idb", [P, P], BF16)
        rec = sb("rec", [P, NH])
        stats = {n: sb(f"stats_{n}", [P, TB, 6]) for n in ("in", "at", "ff")}
        mv = {n: sb(f"mv_{n}", [P, TB, 2]) for n in ("in", "at", "ff")}
        mv2 = sb("mv2", [P, NT, 2])
        var = {n: sb(f"var_{n}", [P, TB]) for n in ("in", "at", "ff")}
        rstd = {n: sb(f"rstd_{n}", [P, TB]) for n in ("in", "at")}
        rstd2 = sb("rstd2", [P, NT])
        neg_half = sb("neg_half", [P, 1])
        zero = sb("zero", [P, D])
        logits = sb("logits", [P, NT, E])
        onehot = sb("onehot", [P, NT, E])
        work_r = sb("work_r", [P, NT, E])
        oh_bf = sb("oh_bf", [P, NT, E], BF16)
        tri_bf = sb("tri_bf", [P, P], BF16)
        ones_bf = sb("ones_bf", [P, P], BF16)
        lmax = sb("lmax", [P, NT])
        score = sb("score", [P, NT])
        gain = sb("gain", [P, NT])
        cmp_t = sb("cmp_t", [P, E, NT])
        cnt = sb("cnt", [P, 4, E])
        cmp_e = sb("cmp_e", [P, NR, E])
        eid = sb("eid", [P, NR])
        eid_i = sb("eid_i", [P, NR], I32)
        pos = sb("pos", [P, NT])
        pos_i = sb("pos_i", [P, NT], I32)
        pos_cur = sb("pos_cur", [P, 2], I32)
        ffn = stacks[:, :, :, :, :].rearrange("p a b h c -> p (a b h c)").bitcast(F32)
        xl = ffn[:, 0:512].rearrange("p (n c) -> p n c", n=2)
        xT = ffn[:, 512:768]
        sg = ffn[:, 1024:1536]
        hid = ffn[:, 1536:2048]
        hT = ffn[:, 2048:2560]
        ys = ffn[:, 2560:3072].rearrange("p (n c) -> p n c", n=2)
        z_sb = ffn[:, 3072:4096].rearrange("p (n g c) -> p n g c", n=2, g=2)
        mv_f = ffn[:, 4096:4104].rearrange("p (n g c) -> p n g c", n=2, g=2)
        rstd_f = ffn[:, 4104:4108].rearrange("p (n g) -> p n g", n=2)
        var_f = ffn[:, 4108:4112].rearrange("p (n g) -> p n g", n=2)
        stats_f = ffn[:, 4112:4136].rearrange("p (n g c) -> p n g c", n=2, g=2)
        y_first = ffn[:, 4608:4608 + HALF * D].rearrange("p (n c) -> p n c", n=HALF)
        xr = pv[:, :].rearrange("p (n c) -> p n c", n=NT)
        routed = xr

        bank = [ctx.enter_context(nc.psum_tensor(f"bank{i}", [P, 512], F32)) for i in range(8)]
        st_bank, sm_bank, av_bank, w0, w1, w2 = bank[0:2], bank[2:4], bank[4], bank[5], bank[6], bank[7]
        y_bank = bank[4], bank[7]

        def two(t):
            return t[:, :].rearrange("p (a c) -> p a c", a=2)

        names = """passed x0_in x_in attn_w const_in
            xn_ready xnT_ps xnT_sb ct_ps ct_sb k0_ps q0_ps kr_sb qr_sb k_swap q_swap k_mul q_mul k_rot
            q_rot k0_done q0_done qk1_ps qk1_sb v_ps v_ready kh qh k_res q_res km qm kl ql stacked
            sm_ps sm_max m_parts mT_ps mT_sb m_rows0 m_rows1 st_ready exp_done av_done o_copied
            avT_ps rec_ready a_ready aT_ps aT_sb wo_ps y_ready yn_ready x1_ready mv2_kept xn2_ready xn2_out
            xn2T_ps xn2T_sb rt_ps logits_sb setup_pool setup_dve bias_sum id_ready
            in_stats in_aggr in_var in_rstd at_stats at_aggr at_var at_rstd
            ff_stats ff_aggr ff_var ff_rstd out_stats out_aggr out_var out_rstd
            w_in w67_in zeroed
            rt rt_exp oh_ready rank_ps pos_ready xr_ready scattered0
            xl_in0 xl_in1 xT_ps xT_sb g_ps u_ps sg_sb h_sb hT_ps hT_sb y_ps ys_sb y_out0 y_out1
            gathered0 gathered1 gathered2 z_ready zn_ready fin_ready out_done0 out_done1""".split()
        sm = {n: sem(n) for n in names}

        def counted(value):
            return not isinstance(value, int) or value > 0

        block = ctx.enter_context(nc.Block())

        STEPS = {h: [] for h in range(NH)}
        for h, step in ((0, "A_xnT"), (1, "m1_here"), (1, "A_ct"), (2, "A_k0"), (3, "A_q0"), (4, "A_qk1"), (5, "A_v"),
                        (5, "D_avT0"), (6, "D_avT1"), (7, "D_aT"), (8, "D_wo"),
                        (11, "D_xn2T"), (12, "D_router"), (14, "m0_next")):
            STEPS[h].append(step)
        SM_AT = {9: (0, 2), 10: (2, 4), 11: (4, 6), 12: (6, 8), 13: (8, 11), 14: (11, 14), 15: (14, 16)}

        def run_slot(b, par, head, steps, first=False, last=False):
            for h in range(NH):
                head(b, par, h, first)
                for step in STEPS[h]:
                    if step == "m1_here":
                        steps["m"](b, par, 1)
                    elif step == "m0_next":
                        if not last:
                            steps["m"](b + 1, 1 - par, 0)
                    elif step[0] == "A" and not last:
                        steps[step](b + 1, 1 - par)
                    elif step[0] == "D" and not first:
                        steps[step](b - 1, 1 - par)
                if h in SM_AT and not last:
                    for u in range(*SM_AT[h]):
                        steps["SM"](b + 1, 1 - par, u)

        def run_attention(eng, head, steps, tail):
            for step in ("A_xnT", "A_ct", "A_k0", "A_q0", "A_qk1", "A_v"):
                steps[step](0, 0)
            for u in range(NH):
                steps["SM"](0, 0, u)
                if u == NH // 2 + 1:
                    steps["m"](0, 0, 0)
            run_slot(0, 0, head, steps, first=True)
            run_slot(1, 1, head, steps)
            with eng.Fori(1, B // 2 - 1) as i:
                for c in range(2):
                    run_slot(2 * i + c, c, head, steps)
            run_slot(B - 2, 0, head, steps)
            run_slot(B - 1, 1, head, steps, last=True)
            tail()

        def nothing(*_):
            return None

        ALL = ("A_xnT", "A_ct", "A_k0", "A_q0", "A_qk1", "A_v", "D_avT0", "D_avT1", "D_aT", "D_wo",
               "D_xn2T", "D_router", "m", "SM")

        LAST = NT + NR - 1
        R0, B0 = HALF, HALF + NR

        def rows_of(seq, kind):
            n = {"A": seq, "R": seq - R0, "B": seq + HALF - B0}[kind]
            return (x_exp if kind == "R" else x_tok)[ds(P * n, P), :]

        def run_ffn(eng, front, body, final=nothing, before_finals=nothing):
            front(0, 0, 0, "A")
            for c in range(2):
                body(c, 0, c, "A", "A")
            with eng.Fori(1, (HALF - 2) // 2) as i:
                for c in range(2):
                    body(2 * i + c, i, c, "A", "A")
            for s in (HALF - 2, HALF - 1):
                body(s, s // 2, s % 2, "A", "A" if s < HALF - 1 else "R")
            for s in (R0, R0 + 1):
                body(s, s // 2, s % 2, "R", "R")
            with eng.Fori(1, (NR - 1) // 2) as i:
                for c in range(2):
                    body(2 * i + R0 + c, i + R0 // 2, c, "R", "R")
            body(B0 - 1, (B0 - 1) // 2, (B0 - 1) % 2, "R", "B")
            before_finals()
            for c in range(2):
                body(B0 + c, (B0 + c) // 2, (B0 + c) % 2, "B", "B")
                final(c, 0, c)
            with eng.Fori(1, (HALF - 2) // 2) as i:
                for c in range(2):
                    body(2 * i + B0 + c, i + (B0 + c) // 2, (B0 + c) % 2, "B", "B")
                    final(2 * i + c, i, c)
            body(LAST - 1, (LAST - 1) // 2, (LAST - 1) % 2, "B", "B")
            final(HALF - 2, (HALF - 2) // 2, 0)
            body(LAST, LAST // 2, LAST % 2, "B", None)
            final(HALF - 1, (HALF - 1) // 2, 1)

        @block.sync
        def _(sp):
            x_t = x.rearrange("(n p) d -> p n d", p=P)
            sp.dma_start(x_sb[:, 0:TB, :], x_t[:, 0:TB, :]).then_inc(sm["x0_in"], 16)
            sp.dma_start(cst[:, :], const).then_inc(sm["const_in"], 16)
            loads = ((wd_sb[:, :, :], w_down.rearrange("(k p) n -> p k n", p=P)),
                     (bcol[:, :], bias_col),
                     (wkv_sb[:, :], w_kv),
                     (wq_sb[:, :, :], w_q.rearrange("(k p) n -> p k n", p=P)),
                     (bv_sb[:, :], bias_v.partition_broadcast(P)[:, 0, :]),
                     (bo_sb[:, :], bias_o.partition_broadcast(P)[:, 0, :]),
                     (wo_sb[:, :, :], w_out.rearrange("(k p) n -> p k n", p=P)),
                     (wr_sb[:, :, :], w_router.rearrange("(k p) n -> p k n", p=P)))
            assert len(loads) == 8
            for dst, src in loads:
                sp.dma_start(dst, src).then_inc(sm["attn_w"], 16)
            sp.dma_start(x_sb[:, TB:NT, :], x_t[:, TB:NT, :]).then_inc(sm["x_in"], 16)

            def stack(b, par):
                if counted(NH * (b - 1)):
                    sp.wait_ge(sm["st_ready"], NH * (b - 1))
                    sp.sem_inc(sm["passed"], 1)
                for side, key, slots, sems in ((1, "k", K_SLOTS, ("kh", "km", "kl")),
                                               (0, "q", Q_SLOTS, ("qh", "qm", "ql"))):
                    for part in range(NPART):
                        sp.wait_ge(sm[sems[part]], b + 1)
                        for r, slot in enumerate(slots):
                            if slot != part:
                                continue
                            for m in range(2):
                                sp.dma_start(
                                    stacks[HD * r:HD * r + HD, par, side, 8 * m:8 * m + 8, :],
                                    parts[key][:, part, m, :],
                                ).then_inc(sm["stacked"], 16)

            def m_rows(b, par, half):
                sp.wait_ge(sm["mT_sb"], 2 * b + half + 1)
                sp.dma_start(stacks[ROWS:MROWS, par, 0, 8 * half:8 * half + 8, :],
                             mT[:, :]).then_inc(sm[f"m_rows{half}"], 16)

            def xn2_store(b, par):
                sp.wait_ge(sm["xn2_ready"], TB * (b + 1))
                sp.dma_start(x_tok[ds(S * b, S), :].rearrange("(t p) d -> p t d", p=P),
                             xn2[:, :, :]).then_inc(sm["xn2_out"], 16)

            def weights(e, sig="w_in"):
                one = wall[:, ds(e, 1), :].rearrange("p e w -> p (e w)")
                sp.dma_start(one[:, 0:KT * 2 * I].rearrange("p (k f) -> p k f", k=KT),
                             gate_up[ds(D * e, D), :].rearrange("(k p) f -> p k f", p=P)
                             ).then_inc(sm[sig], 16)
                sp.dma_start(one[:, KT * 2 * I:WLEN].rearrange("p (k n) -> p k n", n=D),
                             down[ds(I * e, I), :].rearrange("(k p) n -> p k n", p=P)
                             ).then_inc(sm[sig], 16)

            def head(b, par, h, first):
                if h == NH - 1 and first:
                    sp.wait_ge(sm["setup_pool"], 1)
                    sp.dma_start(x_exp.rearrange("(n p) d -> p n d", p=P),
                                 zero[:, :].unsqueeze(1).to_broadcast([P, NR, D])).then_inc(sm["zeroed"], 16)
                if h == NH - 2:
                    if isinstance(b, int) and b == B - 1:
                        g = wall[:, E, 0:KT * 2 * I].rearrange("p (k f) -> p k f", k=KT)
                        sp.dma_start(g[:, :, 0:I], sh_gate.rearrange("(k p) f -> p k f", p=P)
                                     ).then_inc(sm["w_in"], 16)
                        sp.dma_start(g[:, :, I:2 * I], sh_up.rearrange("(k p) f -> p k f", p=P)
                                     ).then_inc(sm["w_in"], 16)
                        sp.dma_start(wall[:, E, KT * 2 * I:WLEN].rearrange("p (k n) -> p k n", n=D),
                                     sh_down.rearrange("(k p) n -> p k n", p=P)).then_inc(sm["w_in"], 16)
                    elif not first:
                        weights(b - 1)

            steps = dict.fromkeys(ALL, nothing)
            steps["A_v"] = stack
            steps["m"] = m_rows
            steps["D_router"] = xn2_store

            def tail():
                xn2_store(B - 1, 1)
                sp.wait_ge(sm["rt_ps"], B)
                sp.wait_ge(sm["xn2_out"], 16 * B)
                for e in (E - 2, E - 1):
                    weights(e, "w67_in")

            run_attention(sp, head, steps, tail)

            sp.wait_ge(sm["xn2_out"], 16 * B)

            def load(seq, n, p, kind):
                if counted(seq - 1):
                    sp.wait_ge(sm["xT_ps"], seq - 1)
                if kind == "R" and isinstance(seq, int) and seq == R0:
                    sp.wait_ge(sm["scattered0"], 16 * NT)
                sp.dma_start(xl[:, p, :], rows_of(seq, kind)).then_inc(sm[f"xl_in{p}"], 16)

            def body(seq, n, p, kind, then):
                if then:
                    load(seq + 1, n + p, 1 - p, then)

            def store(c, p):
                sp.wait_ge(sm["fin_ready"], c + 1)
                sp.dma_start(out.rearrange("(g r) d -> r g d", g=2)[ds(P * c, P), :, :], z_sb[:, p, :, :]
                             ).then_inc(sm[f"out_done{p}"], 16)

            def final(c, n, p):
                if not (isinstance(c, int) and c < 2):
                    store(c - 2, p)

            run_ffn(sp, load, body, final)
            store(HALF - 2, 0)
            store(HALF - 1, 1)
            sp.wait_ge(sm["out_done0"], 16 * HALF // 2)
            sp.wait_ge(sm["out_done1"], 16 * HALF // 2)

        @block.gpsimd
        def _(pool):
            pool.memset(zero[:, :], 0.0).then_inc(sm["setup_pool"], 1)
            pool.memset(neg_half[:, :], -0.5).then_inc(sm["setup_pool"], 1)
            pool.wait_ge(sm["setup_pool"], 2)

            def power(name, count, out_ap, in_ap, n):
                if counted(count):
                    pool.wait_ge(sm[f"{name}_var"], count)
                pool.tensor_tensor(out_ap, in_ap, neg_half[:, 0:1].to_broadcast([P, n]), ALU.pow
                                   ).then_inc(sm[f"{name}_rstd"], 1)

            def rotate(k, b):
                pool.wait_ge(sm[f"{k}_swap"], b + 1)
                pool.tensor_tensor(yr[k][:, :], yr[k][:, :], cst[:, C_COS:C_COS + S],
                                   ALU.mult).then_inc(sm[f"{k}_mul"], 1)
                pool.tensor_tensor(swp[k][:, :], swp[k][:, :], cst[:, C_SIN:C_SIN + S],
                                   ALU.mult).then_inc(sm[f"{k}_mul"], 1)
                pool.wait_ge(sm[f"{k}_mul"], 2 * b + 2)
                pool.tensor_tensor(yr[k][:, :], yr[k][:, :], swp[k][:, :], ALU.add
                                   ).then_inc(sm[f"{k}_rot"], 1)

            def split(k, b):
                pool.wait_ge(sm[f"{k}h"], b + 1)
                pool.tensor_tensor(full[k], full[k], parts[k][:, 0, :, :], ALU.subtract
                                   ).then_inc(sm[f"{k}_res"], 1)
                pool.wait_ge(sm[f"{k}m"], b + 1)
                pool.tensor_tensor(parts[k][:, 2, :, :], full[k], parts[k][:, 1, :, :], ALU.subtract
                                   ).then_inc(sm[f"{k}l"], 1)

            steps = dict.fromkeys(ALL, nothing)
            steps["A_xnT"] = lambda b, par: power("in", b + 1, rstd["in"][:, :], var["in"][:, :], TB)
            steps["A_k0"] = lambda b, par: rotate("k", b)
            steps["A_q0"] = lambda b, par: rotate("q", b)

            def splits(b, par):
                split("k", b)
                split("q", b)

            steps["A_v"] = splits

            def d_wo(b, par):
                power("at", b + 1, rstd["at"][:, :], var["at"][:, :], TB)
                pool.wait_ge(sm["yn_ready"], TB * (b + 1))
                tile = x_sb[:, ds(TB * b, TB), :]
                pool.tensor_tensor(tile, tile, y_sb[:, :, :], ALU.add).then_inc(sm["x1_ready"], 1)

            steps["D_wo"] = d_wo
            steps["D_xn2T"] = lambda b, par: power("ff", b + 1, rstd2[:, ds(TB * b, TB)], var["ff"][:, :], TB)

            def tail():
                d_wo(B - 1, 1)
                steps["D_xn2T"](B - 1, 1)

            run_attention(pool, nothing, steps, tail)

            pool.wait_ge(sm["pos_ready"], 1)
            pool.wait_ge(sm["zeroed"], 16)
            for j in range(NT):
                pool.wait_ge(sm["xr_ready"], j + 1)
                pool.indirect_dma_start(
                    out=x_exp, out_offset=bass.IndirectOffsetOnAxis(ap=pos_i[:, j:j + 1], axis=0),
                    in_=xr[:, j, :], in_offset=None).then_inc(sm["scattered0"], 16)

            def gather(c, name):
                for j in (HALF + c, c):
                    pool.indirect_dma_start(
                        out=routed[:, j, :], out_offset=None, in_=y_exp,
                        in_offset=bass.IndirectOffsetOnAxis(ap=pos_i[:, j:j + 1], axis=0)).then_inc(sm[name], 16)

            def before_finals():
                pool.wait_ge(sm["scattered0"], 16 * NT)
                pool.wait_ge(sm["y_out0"], 16 * ((NR + 1) // 2))
                pool.wait_ge(sm["y_out1"], 16 * (NR // 2))
                for c, name in ((0, "gathered0"), (1, "gathered1"), (2, "gathered2"), (3, "gathered2")):
                    gather(c, name)

            x_two = x_sb[:, :, :].rearrange("p (g n) d -> p n g d", g=2)

            def final(c, n, p):
                power("out", c + 1, rstd_f[:, p, :], var_f[:, p, :], 2)
                pool.wait_ge(sm["zn_ready"], 2 * c + 2)
                pool.tensor_tensor(z_sb[:, p, :, :], z_sb[:, p, :, :],
                                   x_two[:, ds(c, 1), :, :].rearrange("p a g d -> p (a g) d"), ALU.add
                                   ).then_inc(sm["fin_ready"], 1)
                if isinstance(c, int) and c == 0:
                    for rest in range(4, HALF):
                        gather(rest, "gathered2")

            run_ffn(pool, nothing, nothing, final, before_finals)

        @block.scalar
        def _(act):
            def xnT_copy(b, par):
                act.wait_ge(sm["xnT_ps"], b + 1)
                act.activation(xnT, two(w0), ACT.Copy).then_inc(sm["xnT_sb"], 1)

            def ct_copy(b, par):
                if isinstance(b, int) and b == 0:
                    act.wait_ge(sm["bias_sum"], 1)
                act.wait_ge(sm["ct_ps"], b + 1)
                if counted(b):
                    act.wait_ge(sm["v_ps"], b)
                for m in range(2):
                    act.activation(ctT[:, m, :], two(w1)[:, m, :], ACT.Identity, bias=bcol[:, m:m + 1]
                                   ).then_inc(sm["ct_sb"], 1)

            def rope_copy(k, bank_, col):
                def f(b, par):
                    act.wait_ge(sm[f"{k}0_ps"], b + 1)
                    if counted(b):
                        act.wait_ge(sm[f"{k}0_done"], b)
                    act.activation(yr[k][:, :], two(bank_)[:, 1, :], ACT.Identity,
                                   bias=bcol[:, col:col + 1]).then_inc(sm[f"{k}r_sb"], 1)
                return f

            def qk1_copy(b, par):
                act.wait_ge(sm["qk1_ps"], b + 1)
                if counted(b):
                    act.wait_ge(sm["kl"], b)
                if counted(b):
                    act.wait_ge(sm["ql"], b)
                act.activation(kf[:, 1, :], two(w0)[:, 1, :], ACT.Identity, bias=bcol[:, 7:8]
                               ).then_inc(sm["qk1_sb"], 1)
                act.activation(qf[:, 1, :], two(w0)[:, 0, :], ACT.Identity, bias=bcol[:, 3:4]
                               ).then_inc(sm["qk1_sb"], 1)

            def high_mid(b, par):
                act.wait_ge(sm["qk1_sb"], 2 * b + 2)
                if counted(16 * 4 * NSLOT * b):
                    act.wait_ge(sm["stacked"], 16 * 4 * NSLOT * b)
                for k in ("k", "q"):
                    act.wait_ge(sm[f"{k}0_done"], b + 1)
                    act.activation(parts[k][:, 0, :, :], full[k], ACT.Copy).then_inc(sm[f"{k}h"], 1)
                for k in ("k", "q"):
                    act.wait_ge(sm[f"{k}_res"], b + 1)
                    act.activation(parts[k][:, 1, :, :], full[k], ACT.Copy).then_inc(sm[f"{k}m"], 1)

            def mT_copy(b, par, half):
                act.wait_ge(sm["mT_ps"], 2 * b + half + 1)
                if half:
                    act.wait_ge(sm["m_rows0"], 16 * (b + 1))
                else:
                    if counted(16 * b):
                        act.wait_ge(sm["m_rows1"], 16 * b)
                act.activation(mT[:, :], w2[:, 0:P].bitcast(BF16)[0:NPART * NH // 2, :], ACT.Copy
                               ).then_inc(sm["mT_sb"], 1)

            def o_copy(b, half):
                act.wait_ge(sm["av_done"], NH * b + 8 * half + 8)
                if counted(2 * b):
                    act.wait_ge(sm["avT_ps"], 2 * b)
                act.activation(o_sb[:, 2 * half:2 * half + 2, :], two(av_bank), ACT.Copy
                               ).then_inc(sm["o_copied"], 1)

            def head(b, par, h, first):
                act.wait_ge(sm["st_ready"], NH * b + h + 1)
                if counted(NH * b + h - 3):
                    act.wait_ge(sm["av_done"], NH * b + h - 3)
                act.activation(probs[:, h % 4, :], st_bank[h % 2][:, :], ACT.Exp, scale=SCALE
                               ).then_inc(sm["exp_done"], 1)
                if h == 0 and not first:
                    o_copy(b - 1, 1)
                if h == 8:
                    o_copy(b, 0)

            steps = dict.fromkeys(ALL, nothing)
            steps["A_xnT"] = xnT_copy
            steps["A_ct"] = ct_copy
            steps["A_k0"] = rope_copy("k", w0, 6)
            steps["A_q0"] = rope_copy("q", w1, 2 + 2)
            steps["A_qk1"] = qk1_copy
            steps["A_v"] = high_mid
            steps["m"] = mT_copy

            def aT_copy(b, par):
                act.wait_ge(sm["aT_ps"], b + 1)
                if counted(b):
                    act.wait_ge(sm["wo_ps"], b)
                act.activation(aT[:, :, :], two(w2), ACT.Copy).then_inc(sm["aT_sb"], 1)

            def xn2T_copy(b, par):
                act.wait_ge(sm["xn2T_ps"], b + 1)
                if counted(b):
                    act.wait_ge(sm["rt_ps"], b)
                act.activation(xn2T[:, :, :], two(w2), ACT.Copy).then_inc(sm["xn2T_sb"], 1)

            steps["D_aT"] = aT_copy
            steps["D_xn2T"] = xn2T_copy

            def tail():
                o_copy(B - 1, 1)
                aT_copy(B - 1, 1)
                xn2T_copy(B - 1, 1)

            run_attention(act, head, steps, tail)

            act.wait_ge(sm["rt"], 1)
            act.activation(score[:, :], lmax[:, :], ACT.Exp, scale=-1.0).then_inc(sm["rt_exp"], 1)

            def front(seq, n, p, kind):
                act.wait_ge(sm["xT_ps"], seq + 1)
                act.activation(xT, bank[0][:, 0:KT * P], ACT.Copy).then_inc(sm["xT_sb"], 1)
                act.wait_ge(sm["g_ps"], seq + 1)
                act.activation(sg, bank[1][:, :], ACT.Silu).then_inc(sm["sg_sb"], 1)

            def body(seq, n, p, kind, then):
                if then:
                    front(seq + 1, n + p, 1 - p, then)
                if kind == "B":
                    return
                act.wait_ge(sm["y_ps"], seq + 1)
                if kind == "A":
                    act.activation(y_first[:, ds(seq, 1), :].rearrange("p a c -> p (a c)"), y_bank[p][:, 0:D],
                                   ACT.Copy).then_inc(sm["ys_sb"], 1)
                    return
                if not (isinstance(seq, int) and seq < R0 + 2):
                    if counted(16 * (n - R0 // 2)):
                        act.wait_ge(sm[f"y_out{p}"], 16 * (n - R0 // 2))
                act.activation(ys[:, p, :], y_bank[p][:, 0:D], ACT.Copy).then_inc(sm["ys_sb"], 1)
                act.wait_ge(sm["ys_sb"], seq + 1)
                act.dma_start(y_exp[ds(P * (seq - R0), P), :], ys[:, p, :]).then_inc(sm[f"y_out{p}"], 16)

            run_ffn(act, front, body)

        @block.vector
        def _(dve):
            dve.memset(ones_bf[:, :], 1.0).then_inc(sm["setup_dve"], 1)
            for par in range(2):
                dve.memset(v_aug[:, par, :, :, HD:2 * HD], 1.0).then_inc(sm["setup_dve"], 1)
                dve.memset(stacks[ROWS:MROWS, par, 1, :, :], 1.0).then_inc(sm["setup_dve"], 1)
            dve.wait_ge(sm["const_in"], 16)
            dve.tensor_copy(idb[:, :], cst[:, C_ID:C_ID + P]).then_inc(sm["setup_dve"], 1)
            dve.tensor_copy(tri_bf[:, :], cst[:, C_TRI:C_TRI + P]).then_inc(sm["setup_dve"], 1)

            def ln_head(name, b, tiles, stat, mean_var, var_ap, n):
                for t in range(n):
                    dve.bn_stats(stat[:, t, :], tiles(t)).then_inc(sm[f"{name}_stats"], 1)
                dve.wait_ge(sm[f"{name}_stats"], n * (b + 1))
                dve.sem_inc(sm["passed"], 1)
                for t in range(n):
                    dve.bn_aggr(mean_var(t), stat[:, t, :]).then_inc(sm[f"{name}_aggr"], 1)
                dve.wait_ge(sm[f"{name}_aggr"], n * (b + 1))

            def a_norm(b, par):
                if isinstance(b, int) and b <= 1:
                    dve.wait_ge(sm["x0_in" if b == 0 else "x_in"], 16)
                tiles = lambda t: x_sb[:, ds(TB * b + t, 1), :].rearrange("p a c -> p (a c)")
                ln_head("in", b, tiles, stats["in"], lambda t: mv["in"][:, t, :], var["in"], TB)
                dve.tensor_scalar(var["in"][:, :], mv["in"][:, :, 1], EPS, None, ALU.add
                                  ).then_inc(sm["in_var"], 1)
                dve.wait_ge(sm["in_rstd"], b + 1)
                if counted(b):
                    dve.wait_ge(sm["xnT_ps"], b)
                for t in range(TB):
                    dve.tensor_scalar(xn[:, t, :], tiles(t), mv["in"][:, t, 0:1], rstd["in"][:, t:t + 1],
                                      ALU.subtract, ALU.mult).then_inc(sm["xn_ready"], 1)

            SWAP = [i ^ HT for i in range(32)]

            def swap(k, col, bank_):
                def f(b, par):
                    dve.wait_ge(sm[f"{k}r_sb"], b + 1)
                    dve.sem_inc(sm["passed"], 1)
                    dve.stream_shuffle(swp[k][:, :], yr[k][:, :], SWAP).then_inc(sm[f"{k}_swap"], 1)
                return f

            def add0(k, col, bank_):
                def f(b, par):
                    dve.wait_ge(sm[f"{k}_rot"], b + 1)
                    if counted(b):
                        dve.wait_ge(sm[f"{k}l"], b)
                    dve.scalar_tensor_tensor(full[k][:, 0, :], two(bank_)[:, 0, :], bcol[:, col:col + 1],
                                             yr[k][:, :], ALU.add, ALU.add).then_inc(sm[f"{k}0_done"], 1)
                return f

            k_swap, q_swap = swap("k", 5, w0), swap("q", 2, w1)
            k_add, q_add = add0("k", 5, w0), add0("q", 2, w1)

            def v_add(b, par):
                dve.wait_ge(sm["v_ps"], b + 1)
                if counted(NH * (b - 1)):
                    dve.wait_ge(sm["av_done"], NH * (b - 1))
                dve.tensor_tensor(v_aug[:, par, :, :, 0:HD],
                                  two(w1).rearrange("p t (h d) -> p t h d", d=HD),
                                  bv_sb[:, :].rearrange("p (h d) -> p h d", d=HD).unsqueeze(1)
                                  .to_broadcast([P, TB, NH, HD]), ALU.add).then_inc(sm["v_ready"], 1)

            def sm_max(b, par, u):
                half, qt, pair = u // 8, (u // 4) % 2, u % 4
                dve.wait_ge(sm["sm_ps"], NH * b + u + 1)
                dve.tensor_reduce(nmax[:, half, qt, 2 * pair:2 * pair + 2], two(sm_bank[u % 2]), AX.X,
                                  ALU.max, negate=True).then_inc(sm["sm_max"], 1)

            def m_split(b, par, half):
                n = 8 * b + 4 * half
                dve.wait_ge(sm["sm_max"], NH * b + 8 * (half + 1))
                if counted(2 * b + half):
                    dve.wait_ge(sm["mT_ps"], 2 * b + half)
                src, res = nmax[:, half, :, :], nres[:, half, :, :]
                dve.tensor_copy(mparts[:, :, 0, :], src).then_inc(sm["m_parts"], 1)
                dve.wait_ge(sm["m_parts"], n + 1)
                dve.tensor_tensor(res, src, mparts[:, :, 0, :], ALU.subtract).then_inc(sm["m_parts"], 1)
                dve.wait_ge(sm["m_parts"], n + 2)
                dve.tensor_copy(mparts[:, :, 1, :], res).then_inc(sm["m_parts"], 1)
                dve.wait_ge(sm["m_parts"], n + 3)
                dve.tensor_tensor(mparts[:, :, 2, :], res, mparts[:, :, 1, :], ALU.subtract
                                  ).then_inc(sm["m_parts"], 1)

            def divide(t):
                def f(b, par):
                    dve.wait_ge(sm["avT_ps"], 2 * b + t + 1)
                    o = w2[:, :].rearrange("p (h c) -> p h c", c=2 * HD)
                    dve.reciprocal(rec[:, :], o[:, :, HD]).then_inc(sm["rec_ready"], 1)
                    dve.wait_ge(sm["rec_ready"], 2 * b + t + 1)
                    if counted(b):
                        dve.wait_ge(sm["aT_ps"], b)
                    dve.tensor_tensor(a_sb[:, t, :].rearrange("p (h c) -> p h c", c=HD), o[:, :, 0:HD],
                                      rec[:, :].unsqueeze(2).to_broadcast([P, NH, HD]), ALU.mult
                                      ).then_inc(sm["a_ready"], 1)
                return f

            def d_wo(b, par):
                dve.wait_ge(sm["wo_ps"], b + 1)
                if counted(b):
                    dve.wait_ge(sm["x1_ready"], b)
                dve.tensor_tensor(y_sb[:, :, :], two(w2), bo_sb[:, :].unsqueeze(1).to_broadcast([P, TB, D]),
                                  ALU.add).then_inc(sm["y_ready"], 1)
                dve.wait_ge(sm["y_ready"], b + 1)
                ln_head("at", b, lambda t: y_sb[:, t, :], stats["at"], lambda t: mv["at"][:, t, :], None, TB)
                dve.tensor_scalar(var["at"][:, :], mv["at"][:, :, 1], EPS, None, ALU.add
                                  ).then_inc(sm["at_var"], 1)
                dve.wait_ge(sm["at_rstd"], b + 1)
                for t in range(TB):
                    dve.tensor_scalar(y_sb[:, t, :], y_sb[:, t, :], mv["at"][:, t, 0:1],
                                      rstd["at"][:, t:t + 1], ALU.subtract, ALU.mult
                                      ).then_inc(sm["yn_ready"], 1)

            def d_xn2(b, par):
                dve.wait_ge(sm["x1_ready"], b + 1)
                tiles = lambda t: x_sb[:, ds(TB * b + t, 1), :].rearrange("p a c -> p (a c)")
                ln_head("ff", b, tiles, stats["ff"], lambda t: mv["ff"][:, t, :], None, TB)
                dve.tensor_copy(mv2[:, ds(TB * b, TB), :], mv["ff"][:, :, :]).then_inc(sm["mv2_kept"], 1)
                dve.tensor_scalar(var["ff"][:, :], mv["ff"][:, :, 1], EPS, None, ALU.add
                                  ).then_inc(sm["ff_var"], 1)
                dve.wait_ge(sm["ff_rstd"], b + 1)
                if counted(b):
                    dve.wait_ge(sm["xn2T_ps"], b)
                if counted(16 * b):
                    dve.wait_ge(sm["xn2_out"], 16 * b)
                for t in range(TB):
                    dve.tensor_scalar(xn2[:, t, :], tiles(t), mv["ff"][:, t, 0:1],
                                      rstd2[:, ds(TB * b + t, 1)], ALU.subtract, ALU.mult
                                      ).then_inc(sm["xn2_ready"], 1)

            def d_router(b, par):
                dve.wait_ge(sm["rt_ps"], b + 1)
                dve.tensor_copy(logits[:, ds(TB * b, TB), :],
                                w2[:, 0:TB * E].rearrange("p (t e) -> p t e", e=E)).then_inc(sm["logits_sb"], 1)

            steps = dict.fromkeys(ALL, nothing)
            steps["A_xnT"] = a_norm
            steps["A_k0"] = k_swap

            def q0_step(b, par):
                k_add(b, par)
                q_swap(b, par)

            steps["A_q0"] = q0_step
            steps["A_qk1"] = q_add
            steps["A_v"] = v_add
            steps["SM"] = sm_max
            steps["m"] = m_split
            steps["D_avT0"] = divide(0)
            steps["D_avT1"] = divide(1)
            steps["D_wo"] = d_wo
            steps["D_xn2T"] = d_xn2
            steps["D_router"] = d_router

            def bias_sums():
                if counted(16 * 8):
                    dve.wait_ge(sm["attn_w"], 16 * 8)
                dve.tensor_tensor(bcol[:, 3:4], bcol[:, 8:9], bcol[:, 9:10], ALU.add)
                dve.tensor_tensor(bcol[:, 7:8], bcol[:, 10:11], bcol[:, 11:12], ALU.add
                                  ).then_inc(sm["bias_sum"], 1)

            bias_sums()

            def tail():
                b = B - 1
                divide(0)(b, 1)
                divide(1)(b, 1)
                d_wo(b, 1)
                d_xn2(b, 1)
                d_router(b, 1)

            run_attention(dve, nothing, steps, tail)

            done = [0]

            def chain(ins):
                done[0] += 1
                ins.then_inc(sm["rt"], 1)
                if counted(done[0]):
                    dve.wait_ge(sm["rt"], done[0])

            def spread(ap, n):
                return ap.unsqueeze(2).to_broadcast([P, NT, n])

            dve.wait_ge(sm["logits_sb"], B)
            chain(dve.tensor_reduce(lmax[:, :], logits[:, :, :], AX.X, ALU.max))
            chain(dve.tensor_tensor(work_r[:, :, :], logits[:, :, :], spread(lmax[:, :], E), ALU.is_equal))
            desc = cst[:, C_DESC:C_DESC + E].unsqueeze(1).to_broadcast([P, NT, E])
            chain(dve.tensor_tensor(work_r[:, :, :], work_r[:, :, :], desc, ALU.mult))
            chain(dve.tensor_reduce(pos[:, :], work_r[:, :, :], AX.X, ALU.max))
            chain(dve.tensor_tensor(onehot[:, :, :], work_r[:, :, :], spread(pos[:, :], E), ALU.is_equal))
            dve.tensor_copy(oh_bf[:, :, :], onehot[:, :, :]).then_inc(sm["oh_ready"], 1)
            dve.wait_ge(sm["rt_exp"], 1)
            chain(dve.tensor_scalar(score[:, :], score[:, :], 1.0, None, ALU.add))
            chain(dve.reciprocal(score[:, :], score[:, :]))
            chain(dve.tensor_tensor(gain[:, :], score[:, :], rstd2[:, :], ALU.mult))
            dve.wait_ge(sm["rank_ps"], 1)
            chain(dve.tensor_copy(cnt[:, 0, :], bank[6][:, 0:E]))
            chain(dve.tensor_tensor(cmp_t[:, :, :], cnt[:, 0, :].unsqueeze(2).to_broadcast([P, E, NT]),
                                    cst[:, C_TILE:C_TILE + NT].unsqueeze(1).to_broadcast([P, E, NT]), ALU.is_gt))
            chain(dve.tensor_reduce(cnt[:, 1, :], cmp_t[:, :, :], AX.X, ALU.add))
            le = cst[:, C_LE:C_LE + E * E].rearrange("p (a b) -> p a b", a=E)
            chain(dve.tensor_tensor(cmp_t[:, :, 0:E], le, cnt[:, 1, :].unsqueeze(1).to_broadcast([P, E, E]),
                                    ALU.mult))
            chain(dve.tensor_reduce(cnt[:, 2, :], cmp_t[:, :, 0:E], AX.X, ALU.add))
            chain(dve.tensor_tensor(cnt[:, 3, :], cnt[:, 2, :], cnt[:, 1, :], ALU.subtract))
            chain(dve.tensor_scalar(cnt[:, 3, :], cnt[:, 3, :], float(P), None, ALU.mult))
            chain(dve.tensor_tensor(work_r[:, :, :], bank[5][:, 0:NT * E].rearrange("p (t e) -> p t e", e=E),
                                    cnt[:, 3, :].unsqueeze(1).to_broadcast([P, NT, E]), ALU.add))
            chain(dve.tensor_tensor(work_r[:, :, :], work_r[:, :, :], onehot[:, :, :], ALU.mult))
            chain(dve.tensor_reduce(pos[:, :], work_r[:, :, :], AX.X, ALU.add))
            dve.tensor_copy(pos_i[:, :], pos[:, :]).then_inc(sm["pos_ready"], 1)
            dve.wait_ge(sm["mv2_kept"], B)
            for j in range(NT):
                dve.tensor_scalar(xr[:, j, :], x_sb[:, j, :], mv2[:, j, 0:1], gain[:, j:j + 1],
                                  ALU.subtract, ALU.mult).then_inc(sm["xr_ready"], 1)
            chain(dve.tensor_tensor(cmp_e[:, :, :], cnt[:, 2, :].unsqueeze(1).to_broadcast([P, NR, E]),
                                    cst[:, C_NUM:C_NUM + NR].unsqueeze(2).to_broadcast([P, NR, E]), ALU.is_le))
            chain(dve.tensor_reduce(eid[:, :], cmp_e[:, :, :], AX.X, ALU.add))
            chain(dve.tensor_scalar(eid[:, :], eid[:, :], float(E - 1), None, ALU.min))
            dve.tensor_copy(eid_i[:, :], eid[:, :]).then_inc(sm["pos_ready"], 1)

            def front(seq, n, p, kind):
                dve.wait_ge(sm["sg_sb"], seq + 1)
                dve.wait_ge(sm["u_ps"], seq + 1)
                dve.tensor_tensor(hid, sg, bank[2][:, :], ALU.mult).then_inc(sm["h_sb"], 1)

            def body(seq, n, p, kind, then):
                dve.wait_ge(sm["hT_ps"], seq + 1)
                dve.tensor_copy(hT, bank[3][:, :]).then_inc(sm["hT_sb"], 1)
                if then:
                    front(seq + 1, n + p, 1 - p, then)

            def normalise(c, p):
                dve.wait_ge(sm["out_rstd"], c + 1)
                for g in range(2):
                    dve.tensor_scalar(z_sb[:, p, g, :], z_sb[:, p, g, :], mv_f[:, p, g, 0:1],
                                      rstd_f[:, p, g:g + 1], ALU.subtract, ALU.mult
                                      ).then_inc(sm["zn_ready"], 1)

            def final(c, n, p):
                if not (isinstance(c, int) and c == 0):
                    normalise(c - 1, 1 - p)
                dve.wait_ge(sm["y_ps"], c + B0 + 1)
                if isinstance(c, int) and c < 2:
                    dve.wait_ge(sm[f"gathered{c}"], 32)
                else:
                    dve.wait_ge(sm["gathered2"], 32 * (HALF - 2))
                    dve.wait_ge(sm[f"out_done{p}"], 16 * n)
                for g, y in ((1, y_bank[(B0 + p) % 2][:, 0:D]),
                             (0, y_first[:, ds(c, 1), :].rearrange("p a d -> p (a d)"))):
                    dve.tensor_tensor(z_sb[:, p, g, :], y,
                                      routed[:, ds(c + HALF * g, 1), :].rearrange("p a d -> p (a d)"), ALU.add
                                      ).then_inc(sm["z_ready"], 1)
                dve.wait_ge(sm["z_ready"], 2 * c + 2)
                dve.sem_inc(sm["passed"], 1)
                for g in range(2):
                    dve.bn_stats(stats_f[:, p, g, :], z_sb[:, p, g, :]).then_inc(sm["out_stats"], 1)
                dve.wait_ge(sm["out_stats"], 2 * c + 2)
                dve.sem_inc(sm["passed"], 1)
                for g in range(2):
                    dve.bn_aggr(mv_f[:, p, g, :], stats_f[:, p, g, :]).then_inc(sm["out_aggr"], 1)
                dve.wait_ge(sm["out_aggr"], 2 * c + 2)
                dve.tensor_scalar(var_f[:, p, :], mv_f[:, p, :, 1], EPS, None, ALU.add
                                  ).then_inc(sm["out_var"], 1)

            run_ffn(dve, front, body, final)
            normalise(HALF - 1, 1)

        @block.tensor
        def _(pe):
            ident = cst[:, C_ID:C_ID + P]

            def products(out_ap, pairs):
                for n, (lhsT, rhs) in enumerate(pairs):
                    last = pe.matmul(out_ap, lhsT, rhs, start=(n == 0), stop=(n == len(pairs) - 1))
                return last

            def turn(out_ap, in_ap):
                return pe.transpose(out_ap, in_ap, ident)

            def a_xnT(b, par):
                if isinstance(b, int) and b == 0:
                    pe.wait_ge(sm["const_in"], 16)
                pe.wait_ge(sm["xn_ready"], TB * (b + 1))
                if counted(2 * b):
                    pe.wait_ge(sm["qk1_sb"], 2 * b)
                for k in range(KT):
                    for t in range(TB):
                        last = turn(two(w0)[:, k, P * t:P * t + P], xn[:, t, P * k:P * k + P])
                last.then_inc(sm["xnT_ps"], 1)

            def a_ct(b, par):
                if isinstance(b, int) and b == 0:
                    if counted(16 * 8):
                        pe.wait_ge(sm["attn_w"], 16 * 8)
                pe.wait_ge(sm["xnT_sb"], b + 1)
                if counted(b):
                    pe.wait_ge(sm["v_ready"], b)
                for m in range(2):
                    last = products(two(w1)[:, m, :], [(wd_sb[:, k, P * m:P * m + P], xnT[:, k, :])
                                                       for k in range(KT)])
                last.then_inc(sm["ct_ps"], 1)

            def a_k0(b, par):
                pe.wait_ge(sm["ct_sb"], 2 * b + 2)
                for r in range(2):
                    last = products(two(w0)[:, r, :], [(wkv_sb[:, D * r:D * r + P], ctT[:, 1, :])])
                last.then_inc(sm["k0_ps"], 1)

            def a_q0(b, par):
                for r in range(2):
                    last = products(two(w1)[:, r, :], [(wq_sb[:, k, D * r:D * r + P], ctT[:, k, :])
                                                       for k in range(KT)])
                last.then_inc(sm["q0_ps"], 1)

            def a_qk1(b, par):
                pe.wait_ge(sm["kr_sb"], b + 1)
                pe.wait_ge(sm["k0_done"], b + 1)
                products(two(w0)[:, 0, :], [(wq_sb[:, k, D * r + P:D * r + 2 * P], ctT[:, k, :])
                                            for k in range(KT) for r in range(2)])
                products(two(w0)[:, 1, :], [(wkv_sb[:, D * r + P:D * r + 2 * P], ctT[:, 1, :])
                                            for r in range(2)]).then_inc(sm["qk1_ps"], 1)

            def a_v(b, par):
                pe.wait_ge(sm["qr_sb"], b + 1)
                pe.wait_ge(sm["q0_done"], b + 1)
                for t in range(TB):
                    last = products(two(w1)[:, t, :], [(ctT[:, 1, P * t:P * t + P], wkv_sb[:, 2 * D:3 * D])])
                last.then_inc(sm["v_ps"], 1)

            def sm_scores(b, par, u):
                half, qt, pair = u // 8, (u // 4) % 2, u % 4
                if u == 0:
                    pe.wait_ge(sm["stacked"], 16 * 4 * NSLOT * (b + 1))
                if counted(NH * b + u - 1):
                    pe.wait_ge(sm["sm_max"], NH * b + u - 1)
                for c in range(2):
                    h = 8 * half + 2 * pair + c
                    last = pe.matmul(two(sm_bank[u % 2])[:, c, :],
                                     stacks[0:ROWS, par, 0, h, P * qt:P * qt + P],
                                     stacks[0:ROWS, par, 1, h, :], start=True, stop=True)
                last.then_inc(sm["sm_ps"], 1)

            def m_turn(b, par, half):
                pe.wait_ge(sm["m_parts"], 8 * b + 4 * half + 4)
                if half:
                    pe.wait_ge(sm["mT_sb"], 2 * b + 1)
                else:
                    if counted(b - 1):
                        pe.wait_ge(sm["logits_sb"], b - 1)
                    if counted(2 * b):
                        pe.wait_ge(sm["mT_sb"], 2 * b)
                for t in range(TB):
                    last = pe.transpose(w2[:, 0:P].bitcast(BF16)[0:NPART * NH // 2, P * t:P * t + P],
                                        mparts[:, t, :, :].rearrange("p a h -> p (a h)"), idb[:, :])
                last.then_inc(sm["mT_ps"], 1)

            def probs_v(b, par, h):
                pe.wait_ge(sm["exp_done"], NH * b + h + 1)
                if h % 8 == 0:
                    if counted(2 * b + h // 8):
                        pe.wait_ge(sm["o_copied"], 2 * b + h // 8)
                if h == 0:
                    pe.wait_ge(sm["v_ready"], b + 1)
                c = h % 4
                for k in range(TB):
                    last = pe.matmul(two(av_bank)[32 * c:32 * c + 32, (h % 8) // 4, :],
                                     v_aug[:, par, k, h, :], probs[:, h % 4, S * k:S * k + S],
                                     start=(k == 0), stop=(k == TB - 1))
                last.then_inc(sm["av_done"], 1)

            def head(b, par, h, first):
                if h == 0:
                    pe.wait_ge(sm["m_rows0"], 16 * (b + 1))
                if h == 8:
                    pe.wait_ge(sm["m_rows1"], 16 * (b + 1))
                if counted(NH * b + h - 1):
                    pe.wait_ge(sm["exp_done"], NH * b + h - 1)
                for k in range(TB):
                    last = pe.matmul(two(st_bank[h % 2])[:, k, :],
                                     stacks[0:MROWS, par, 1, h, P * k:P * k + P],
                                     stacks[0:MROWS, par, 0, h, :], start=True, stop=True)
                last.then_inc(sm["st_ready"], 1)
                if h > 0:
                    probs_v(b, par, h - 1)
                elif not first:
                    probs_v(b - 1, 1 - par, NH - 1)

            def av_turn(t):
                def f(b, par):
                    if t == 0:
                        pe.wait_ge(sm["o_copied"], 2 * b + 2)
                        if isinstance(b, int) and b == B - 1:
                            if counted(b):
                                pe.wait_ge(sm["logits_sb"], b)
                        else:
                            pe.wait_ge(sm["mT_sb"], 2 * b + 4)
                    else:
                        pe.wait_ge(sm["a_ready"], 2 * b + 1)
                    for g in range(4):
                        last = turn(w2[:, P * g:P * g + P], o_sb[:, g, P * t:P * t + P])
                    last.then_inc(sm["avT_ps"], 1)
                return f

            def a_turn(b, par):
                pe.wait_ge(sm["a_ready"], 2 * b + 2)
                for k in range(KT):
                    for t in range(TB):
                        last = turn(two(w2)[:, k, P * t:P * t + P], a_sb[:, t, P * k:P * k + P])
                last.then_inc(sm["aT_ps"], 1)

            def d_wo(b, par):
                pe.wait_ge(sm["aT_sb"], b + 1)
                for t in range(TB):
                    last = products(two(w2)[:, t, :], [(aT[:, k, P * t:P * t + P], wo_sb[:, k, :])
                                                       for k in range(KT)])
                last.then_inc(sm["wo_ps"], 1)

            def d_xn2T(b, par):
                pe.wait_ge(sm["xn2_ready"], TB * (b + 1))
                for k in range(KT):
                    for t in range(TB):
                        last = turn(two(w2)[:, k, P * t:P * t + P], xn2[:, t, P * k:P * k + P])
                last.then_inc(sm["xn2T_ps"], 1)

            def d_router(b, par):
                pe.wait_ge(sm["xn2T_sb"], b + 1)
                for t in range(TB):
                    last = products(w2[:, E * t:E * t + E], [(xn2T[:, k, P * t:P * t + P], wr_sb[:, k, :])
                                                             for k in range(KT)])
                last.then_inc(sm["rt_ps"], 1)

            steps = {"A_xnT": a_xnT, "A_ct": a_ct, "A_k0": a_k0, "A_q0": a_q0, "A_qk1": a_qk1, "A_v": a_v,
                     "SM": sm_scores, "m": m_turn, "D_avT0": av_turn(0), "D_avT1": av_turn(1),
                     "D_aT": a_turn, "D_wo": d_wo, "D_xn2T": d_xn2T, "D_router": d_router}

            def tail():
                b = B - 1
                probs_v(b, 1, NH - 1)
                for step in ("D_avT0", "D_avT1", "D_aT", "D_wo", "D_xn2T", "D_router"):
                    steps[step](b, 1)

            pe.wait_ge(sm["setup_dve"], 7)
            run_attention(pe, head, steps, tail)

            pe.wait_ge(sm["oh_ready"], 1)
            flat = oh_bf[:, :, :].rearrange("p t e -> p (t e)")
            rank = bank[5][:, 0:NT * E].rearrange("p (t e) -> p t e", e=E)
            pe.matmul(bank[5][:, 0:NT * E], tri_bf[:, :], flat, start=True, stop=False, skip_group_check=True)
            for j in range(NT - 1):
                pe.matmul(rank[:, j + 1:NT, :], ones_bf[:, :],
                          oh_bf[:, j:j + 1, :].to_broadcast([P, NT - 1 - j, E]),
                          start=False, stop=(j == NT - 2), skip_group_check=True)
            for j in range(NT):
                last = pe.matmul(bank[6][:, 0:E], ones_bf[:, :], oh_bf[:, j, :],
                                 start=(j == 0), stop=(j == NT - 1))
            last.then_inc(sm["rank_ps"], 1)

            pe.wait_ge(sm["w_in"], 16 * (2 * (E - 2) + 3))

            def gate_up_of(kind, seq):
                if kind != "R":
                    return lambda k, r: wall[:, E, 2 * I * k + I * r:2 * I * k + I * r + I], \
                           lambda k: wall[:, E, KT * 2 * I + D * k:KT * 2 * I + D * k + D]
                e = pe.value_load(eid_i[0:1, ds(seq - R0, 1)], min_val=0, max_val=E - 1)
                flat_w = wall[:, :, :].rearrange("p e w -> p (e w)")
                return lambda k, r: flat_w[:, ds(e * WLEN + 2 * I * k + I * r, I)], \
                       lambda k: flat_w[:, ds(e * WLEN + KT * 2 * I + D * k, D)]

            def x_turn(seq, n, p, kind):
                pe.wait_ge(sm[f"xl_in{p}"], 16 * (n + 1))
                for k in range(KT):
                    last = turn(bank[0][:, P * k:P * k + P], xl[:, p, P * k:P * k + P])
                last.then_inc(sm["xT_ps"], 1)

            def gate_and_up(seq, n, p, kind):
                w, _ = gate_up_of(kind, seq)
                pe.wait_ge(sm["xT_sb"], seq + 1)
                for r, sig in ((0, "g_ps"), (1, "u_ps")):
                    products(bank[1 + r][:, :], [(xT[:, P * k:P * k + P], w(k, r)) for k in range(KT)]
                             ).then_inc(sm[sig], 1)

            def front(seq, n, p, kind):
                x_turn(seq, n, p, kind)
                gate_and_up(seq, n, p, kind)

            def body(seq, n, p, kind, then):
                if then:
                    x_turn(seq + 1, n + p, 1 - p, then)
                pe.wait_ge(sm["h_sb"], seq + 1)
                for k in range(I // P):
                    last = turn(bank[3][:, P * k:P * k + P], hid[:, P * k:P * k + P])
                last.then_inc(sm["hT_ps"], 1)
                if then == "R" and kind == "A":
                    pe.wait_ge(sm["pos_ready"], 2)
                    pe.wait_ge(sm["w67_in"], 64)
                if then:
                    gate_and_up(seq + 1, n + p, 1 - p, then)
                _, w = gate_up_of(kind, seq)
                pe.wait_ge(sm["hT_sb"], seq + 1)
                if kind == "B" and not (isinstance(seq, int) and seq < B0 + 2):
                    pe.wait_ge(sm["z_ready"], 2 * (seq - B0) - 3)
                else:
                    if counted(seq - 1):
                        pe.wait_ge(sm["ys_sb"], seq - 1)
                products(y_bank[p][:, 0:D], [(hT[:, P * k:P * k + P], w(k)) for k in range(I // P)]
                         ).then_inc(sm["y_ps"], 1)

            run_ffn(pe, front, body)


def kernel(**inputs):
    import concourse.bacc as bacc
    from concourse.bass_utils import run_bass_kernel_spmd

    g = {k: np.asarray(v) for k, v in inputs.items()}
    f = np.float32

    def padded(a, rows):
        return np.concatenate([np.zeros((rows, a.shape[1]), f), a], 0)

    wq = np.zeros((D, 2 * D), f)
    wq[0:DQ, 0:D] = head_minor(g["L0_attn_w_up_q"].T)
    wq[0:DQ, D:2 * D] = head_minor(g["L0_attn_wq_r"].T)
    wkv = np.concatenate([padded(head_minor(g["L0_attn_w_up_k"].T), P - DKV),
                          padded(head_minor(g["L0_attn_wk_r"].T), P - DKV),
                          padded(g["L0_attn_w_up_v"].T, P - DKV)], 1)
    col = np.zeros((P, 12), f)
    bd = np.concatenate([g["L0_attn_b_down_q"], g["L0_attn_b_down_kv"]]).reshape(2, P)
    bq, bqr, bk, bkr = (head_minor(g[f"L0_attn_{n}"]).reshape(2, P) for n in ("b_up_q", "bq_r", "b_up_k", "bk_r"))
    for c, v in ((0, bd[0]), (1, bd[1]), (2, bq[0]), (4, bqr[0]), (5, bk[0]), (6, bkr[0]),
                 (8, bq[1]), (9, bqr[1]), (10, bk[1]), (11, bkr[1])):
        col[:, c] = v
    arrays = {
        "x": g["L0_attn_x"].reshape(B * S, D),
        "const": constants(),
        "w_down": np.concatenate([g["L0_attn_w_down_q"].T, g["L0_attn_w_down_kv"].T], 1),
        "w_q": wq, "w_kv": wkv,
        "w_out": g["L0_attn_wo"].T, "w_router": g["L0_ffn_router_w"].T,
        "bias_col": col,
        "bias_v": np.zeros(0), "bias_o": np.zeros(0),
        "gate_up": g["L0_ffn_gate_up_proj"].reshape(E * D, 2 * I),
        "down": g["L0_ffn_down_proj"].reshape(E * I, D),
        "sh_gate": g["L0_ffn_shared_gate_w"], "sh_up": g["L0_ffn_shared_up_w"],
        "sh_down": g["L0_ffn_shared_down_w"],
    }
    arrays["bias_v"] = g["L0_attn_b_up_v"].reshape(1, D)
    arrays["bias_o"] = g["L0_attn_bo"].reshape(1, D)
    nc = bacc.Bacc("TRN2", target_bir_lowering=False, num_devices=1)
    aps = []
    for n in list(arrays):
        arrays[n] = np.ascontiguousarray(arrays[n])
        aps.append(nc.dram_tensor(n, list(arrays[n].shape), F32, kind="ExternalInput").ap())
    out = nc.dram_tensor("out", [B * S, D], F32, kind="ExternalOutput").ap()
    program(nc, *aps, out)
    r = run_bass_kernel_spmd(nc, [arrays], core_ids=[0])
    return r.results[0]["out"].reshape(B, S, D)
```

```python
from contextlib import ExitStack

import numpy as np

import concourse.bass as bass
from concourse import mybir

F32 = mybir.dt.float32
BF16 = mybir.dt.bfloat16
I32 = mybir.dt.int32
ALU = mybir.AluOpType
ACT = mybir.ActivationFunctionType
AX = mybir.AxisListType
ds = bass.ds

P = 128
B, S, D = 8, 256, 256
NH, HD = 16, 16
DQ, DKV = 192, 64
E, I = 8, 512
NT = B * S // P
TB = S // P
KT = D // P
NR = NT + E - 1
HALF = NT // 2
EPS = 1e-5
SCALE = 1.0 / float(np.sqrt(HD))
NPART = 3
K_SLOTS = (0, 0, 0, 1, 1, 2)
Q_SLOTS = (0, 1, 2, 0, 1, 0)
NSLOT = len(K_SLOTS)
ROWS = NSLOT * HD
MROWS = ROWS + NPART
HT = P // HD
WLEN = KT * 2 * I + (I // P) * D

C_ID, C_TRI, C_COS, C_SIN = 0, 128, 256, 512
C_DESC, C_TILE, C_LE, C_NUM = 768, 776, 792, 856
C_END = C_NUM + NR


def head_minor(a):
    return np.moveaxis(a.reshape(*a.shape[:-1], -1, HT, HD), -1, -2).reshape(a.shape)


def constants():
    t = np.zeros((P, C_END), np.float32)
    t[:, C_ID:C_ID + P] = np.eye(P)
    t[:, C_TRI:C_TRI + P] = np.triu(np.ones((P, P)), 1)
    exps = np.arange(0, D, 2, dtype=np.float32)
    inside = exps < 10
    tn = np.zeros_like(exps)
    tn[inside] = np.float32(1.0) / (np.float32(10000.0) ** exps[inside] / np.float32(D))
    assert not tn[P // 2:].any()
    ang = np.outer(np.arange(S, dtype=np.float32), tn).astype(np.float32)
    cos, sin = np.cos(ang), np.sin(ang)
    for row, f in enumerate(head_minor(np.arange(P))):
        t[row, C_COS:C_COS + S] = cos[:, f // 2]
        t[row, C_SIN:C_SIN + S] = sin[:, f // 2] * (1 if f % 2 else -1)
    t[:, C_DESC:C_DESC + E] = E - np.arange(E)
    t[:, C_TILE:C_TILE + NT] = P * np.arange(NT)
    t[:, C_LE:C_LE + E * E] = (np.arange(E)[None, :] <= np.arange(E)[:, None]).reshape(-1)
    t[:, C_NUM:C_NUM + NR] = np.arange(NR)
    return t


def program(nc, x, const, w_down, w_q, w_kv, w_out, w_router, bias_col, bias_v, bias_o,
            gate_up, down, sh_gate, sh_up, sh_down, out):
    x_tok = nc.dram_tensor("x_tok", [NT * P, D], F32, kind="Internal").ap()
    x_exp = nc.dram_tensor("x_exp", [NR * P, D], F32, kind="Internal").ap()
    y_exp = nc.dram_tensor("y_exp", [NR * P, D], F32, kind="Internal").ap()
    with ExitStack() as ctx:
        def sb(name, shape, dt=F32):
            return ctx.enter_context(nc.sbuf_tensor(name, shape, dt))

        def sem(name):
            return ctx.enter_context(nc.semaphore(name))

        wall = sb("wall", [P, E + 1, WLEN])
        x_sb = sb("x_sb", [P, NT, D])
        cst = sb("cst", [P, C_END])
        wd_sb = sb("wd_sb", [P, KT, D])
        wq_sb = sb("wq_sb", [P, KT, 2 * D])
        wkv_sb = sb("wkv_sb", [P, 3 * D])
        wo_sb = sb("wo_sb", [P, KT, D])
        wr_sb = sb("wr_sb", [P, KT, E])
        bcol = sb("bcol", [P, 12])
        bv_sb = sb("bv_sb", [P, D])
        bo_sb = sb("bo_sb", [P, D])
        stacks = sb("stacks", [P, 2, 2, NH, S], BF16)
        pv = sb("pv", [P, 4096])
        probs = pv[:, 0:2048].rearrange("p (n c) -> p n c", n=4)
        v_aug = pv[:, 2048:4096].rearrange("p (b t h c) -> p b t h c", b=2, t=TB, h=NH)
        spare = wall[:, E - 1, :]
        qf = spare[:, 0:512].rearrange("p (m c) -> p m c", m=2)
        kf = spare[:, 512:1024].rearrange("p (m c) -> p m c", m=2)
        xn = spare[:, 1024:1536].rearrange("p (t c) -> p t c", t=TB)
        xnT = spare[:, 1536:2048].rearrange("p (k c) -> p k c", k=KT)
        ctT = spare[:, 2048:2560].rearrange("p (k c) -> p k c", k=KT)
        a_sb = spare[:, 2560:3072].rearrange("p (t c) -> p t c", t=TB)
        spare2 = wall[:, E - 2, :]
        o_sb = spare2[:, 0:1024].rearrange("p (g c) -> p g c", g=4)
        aT = spare2[:, 1024:1536].rearrange("p (k c) -> p k c", k=KT)
        y_sb = spare2[:, 1536:2048].rearrange("p (t c) -> p t c", t=TB)
        xn2 = spare2[:, 2048:2560].rearrange("p (t c) -> p t c", t=TB)
        xn2T = spare2[:, 2560:3072].rearrange("p (k c) -> p k c", k=KT)
        yr = {"q": sb("yr_q", [P, S]), "k": sb("yr_k", [P, S])}
        swp = {"q": sb("swp_q", [P, S]), "k": sb("swp_k", [P, S])}
        parts = {"q": sb("parts_q", [P, NPART, 2, S], BF16), "k": sb("parts_k", [P, NPART, 2, S], BF16)}
        full = {"q": qf, "k": kf}
        nmax = sb("nmax", [P, 2, TB, NH // 2])
        nres = sb("nres", [P, 2, TB, NH // 2])
        mparts = sb("mparts", [P, TB, NPART, NH // 2], BF16)
        mT = sb("mT", [NPART * NH // 2, S], BF16)
        idb = sb("idb", [P, P], BF16)
        rec = sb("rec", [P, NH])
        stats = {n: sb(f"stats_{n}", [P, TB, 6]) for n in ("in", "at", "ff")}
        mv = {n: sb(f"mv_{n}", [P, TB, 2]) for n in ("in", "at", "ff")}
        mv2 = sb("mv2", [P, NT, 2])
        var = {n: sb(f"var_{n}", [P, TB]) for n in ("in", "at", "ff")}
        rstd = {n: sb(f"rstd_{n}", [P, TB]) for n in ("in", "at")}
        rstd2 = sb("rstd2", [P, NT])
        neg_half = sb("neg_half", [P, 1])
        zero = sb("zero", [P, D])
        logits = sb("logits", [P, NT, E])
        onehot = sb("onehot", [P, NT, E])
        work_r = sb("work_r", [P, NT, E])
        oh_bf = sb("oh_bf", [P, NT, E], BF16)
        tri_bf = sb("tri_bf", [P, P], BF16)
        ones_bf = sb("ones_bf", [P, P], BF16)
        lmax = sb("lmax", [P, NT])
        score = sb("score", [P, NT])
        gain = sb("gain", [P, NT])
        cmp_t = sb("cmp_t", [P, E, NT])
        cnt = sb("cnt", [P, 4, E])
        cmp_e = sb("cmp_e", [P, NR, E])
        eid = sb("eid", [P, NR])
        eid_i = sb("eid_i", [P, NR], I32)
        pos = sb("pos", [P, NT])
        pos_i = sb("pos_i", [P, NT], I32)
        pos_cur = sb("pos_cur", [P, 2], I32)
        ffn = stacks[:, :, :, :, :].rearrange("p a b h c -> p (a b h c)").bitcast(F32)
        xl = ffn[:, 0:512].rearrange("p (n c) -> p n c", n=2)
        xT = ffn[:, 512:1024].rearrange("p (n c) -> p n c", n=2)
        sg = ffn[:, 1024:1536]
        hid = ffn[:, 1536:2048]
        hT = ffn[:, 2048:2560]
        ys = ffn[:, 2560:3072].rearrange("p (n c) -> p n c", n=2)
        z_sb = ffn[:, 3072:4096].rearrange("p (n g c) -> p n g c", n=2, g=2)
        mv_f = ffn[:, 4096:4104].rearrange("p (n g c) -> p n g c", n=2, g=2)
        rstd_f = ffn[:, 4104:4108].rearrange("p (n g) -> p n g", n=2)
        var_f = ffn[:, 4108:4112].rearrange("p (n g) -> p n g", n=2)
        stats_f = ffn[:, 4112:4136].rearrange("p (n g c) -> p n g c", n=2, g=2)
        y_first = ffn[:, 4608:4608 + HALF * D].rearrange("p (n c) -> p n c", n=HALF)
        xr = pv[:, :].rearrange("p (n c) -> p n c", n=NT)
        routed = xr

        bank = [ctx.enter_context(nc.psum_tensor(f"bank{i}", [P, 512], F32)) for i in range(8)]
        st_bank, sm_bank, av_bank, w0, w1, w2 = bank[0:2], bank[2:4], bank[4], bank[5], bank[6], bank[7]
        y_bank = bank[4], bank[7]

        def two(t):
            return t[:, :].rearrange("p (a c) -> p a c", a=2)

        names = """passed x0_in x_in attn_w const_in
            xn_ready xnT_ps xnT_sb ct_ps ct_sb k0_ps q0_ps kr_sb qr_sb k_swap q_swap k_mul q_mul k_rot
            q_rot k0_done q0_done qk1_ps qk1_sb v_ps v_ready kh qh k_res q_res km qm kl ql stacked0 stacked1
            sm_ps sm_max m_parts mT_ps mT_sb m_rows0 m_rows1 st_ready exp_done av_done o_copied
            avT_ps rec_ready a_ready aT_ps aT_sb wo_ps y_ready yn_ready x1_ready mv2_kept xn2_ready xn2_out
            xn2T_ps xn2T_sb rt_ps logits_sb setup_pool setup_dve bias_sum id_ready
            in_stats in_aggr in_var in_rstd at_stats at_aggr at_var at_rstd
            ff_stats ff_aggr ff_var ff_rstd out_stats out_aggr out_var out_rstd
            w_in w67_in zeroed
            rt rt_exp oh_ready rank_ps pos_ready xr_ready scattered0
            xl_in0 xl_in1 xT_ps xT_sb g_ps u_ps sg_sb h_sb hT_ps hT_sb y_ps ys_sb y_out0 y_out1
            gathered0 gathered1 gathered2 z_ready zn_ready fin_ready out_done0 out_done1""".split()
        sm = {n: sem(n) for n in names}

        def counted(value):
            return not isinstance(value, int) or value > 0

        block = ctx.enter_context(nc.Block())

        AHEAD = {"A": 2, "N": 1, "M0": 1, "M1": 0, "D": -1}

        def exists(b):
            return not isinstance(b, int) or 0 <= b < B

        def step_of(steps, name, b, par):
            ahead = AHEAD[name.split("_")[0]]
            if exists(b + ahead):
                steps[name](b + ahead, (par + ahead) % 2)

        def run_slot(b, par, head, steps, order, behind):
            for h in range(NH):
                head(b, par, h)
                if exists(b + 1):
                    steps["SM"](b + 1, 1 - par, h)
                for name in order.get(h, ()):
                    step_of(steps, name, b, par)
                behind(b, par, h)

        def run_attention(eng, head, steps, order, tail, behind=lambda *_: None):
            in_order = [name for h in range(NH) for name in order.get(h, ())]
            for name in in_order:
                if name[0] == "A":
                    steps[name](0, 0)
            for name in in_order:
                if name[0] == "N":
                    steps[name](0, 0)
            for name in in_order:
                if name[0] == "A":
                    steps[name](1, 1)
            for u in range(NH):
                steps["SM"](0, 0, u)
                if u == NH // 2 + 1 and "M0" in steps:
                    steps["M0"](0, 0)
            for b in (0, 1):
                run_slot(b, b, head, steps, order, behind)
            with eng.Fori(1, B // 2 - 1) as i:
                for c in range(2):
                    run_slot(2 * i + c, c, head, steps, order, behind)
            for b in (B - 2, B - 1):
                run_slot(b, b % 2, head, steps, order, behind)
            tail()

        def nothing(*_):
            return None

        LAST = NT + NR - 1
        R0, B0 = HALF, HALF + NR

        def rows_of(seq, kind):
            n = {"A": seq, "R": seq - R0, "B": seq + HALF - B0}[kind]
            return (x_exp if kind == "R" else x_tok)[ds(P * n, P), :]

        def run_ffn(eng, front, body, final=nothing, before_finals=nothing):
            kinds = "A" * HALF + "R" * NR + "B" * HALF

            def single(s):
                body(s, s // 2, s % 2, kinds[s:s + 3])

            front()
            for s in (0, 1):
                single(s)
            with eng.Fori(1, (HALF - 2) // 2) as i:
                for c in range(2):
                    body(2 * i + c, i, c, "AAA")
            for s in (HALF - 2, HALF - 1, R0, R0 + 1):
                single(s)
            with eng.Fori(1, (NR - 1) // 2 - 1) as i:
                for c in range(2):
                    body(2 * i + R0 + c, i + R0 // 2, c, "RRR")
            for s in (B0 - 3, B0 - 2, B0 - 1):
                single(s)
            before_finals()
            for c in range(2):
                single(B0 + c)
                final(c, 0, c)
            with eng.Fori(1, (HALF - 2) // 2) as i:
                for c in range(2):
                    body(2 * i + B0 + c, i + (B0 + c) // 2, (B0 + c) % 2, "BBB")
                    final(2 * i + c, i, c)
            for c in (HALF - 2, HALF - 1):
                single(B0 + c)
                final(c, c // 2, c % 2)

        @block.sync
        def _(sp):
            x_t = x.rearrange("(n p) d -> p n d", p=P)
            sp.dma_start(x_sb[:, 0:TB, :], x_t[:, 0:TB, :]).then_inc(sm["x0_in"], 16)
            sp.dma_start(cst[:, :], const).then_inc(sm["const_in"], 16)
            loads = ((wd_sb[:, :, :], w_down.rearrange("(k p) n -> p k n", p=P)),
                     (bcol[:, :], bias_col),
                     (wkv_sb[:, :], w_kv),
                     (wq_sb[:, :, :], w_q.rearrange("(k p) n -> p k n", p=P)),
                     (bv_sb[:, :], bias_v.partition_broadcast(P)[:, 0, :]),
                     (bo_sb[:, :], bias_o.partition_broadcast(P)[:, 0, :]),
                     (wo_sb[:, :, :], w_out.rearrange("(k p) n -> p k n", p=P)),
                     (wr_sb[:, :, :], w_router.rearrange("(k p) n -> p k n", p=P)))
            assert len(loads) == 8
            for dst, src in loads:
                sp.dma_start(dst, src).then_inc(sm["attn_w"], 16)
            sp.dma_start(x_sb[:, TB:NT, :], x_t[:, TB:NT, :]).then_inc(sm["x_in"], 16)

            def stack(m):
                def f(b, par):
                    before = NH * (b - 2) + 8 * (m + 1)
                    if counted(before):
                        sp.wait_ge(sm["st_ready"], before)
                        sp.sem_inc(sm["passed"], 1)
                    for side, key, slots, sems in ((1, "k", K_SLOTS, ("kh", "km", "kl")),
                                                   (0, "q", Q_SLOTS, ("qh", "qm", "ql"))):
                        for part in range(NPART):
                            sp.wait_ge(sm[sems[part]], b + 1)
                            for r, slot in enumerate(slots):
                                if slot == part:
                                    sp.dma_start(
                                        stacks[HD * r:HD * r + HD, par, side, 8 * m:8 * m + 8, :],
                                        parts[key][:, part, m, :],
                                    ).then_inc(sm[f"stacked{m}"], 16)
                return f

            def xn2_store(b, par):
                sp.wait_ge(sm["xn2_ready"], TB * (b + 1))
                sp.dma_start(x_tok[ds(S * b, S), :].rearrange("(t p) d -> p t d", p=P),
                             xn2[:, :, :]).then_inc(sm["xn2_out"], 16)

            def weights(e, sig="w_in"):
                one = wall[:, ds(e, 1), :].rearrange("p e w -> p (e w)")
                sp.dma_start(one[:, 0:KT * 2 * I].rearrange("p (k f) -> p k f", k=KT),
                             gate_up[ds(D * e, D), :].rearrange("(k p) f -> p k f", p=P)
                             ).then_inc(sm[sig], 16)
                sp.dma_start(one[:, KT * 2 * I:WLEN].rearrange("p (k n) -> p k n", n=D),
                             down[ds(I * e, I), :].rearrange("(k p) n -> p k n", p=P)
                             ).then_inc(sm[sig], 16)

            def head(b, par, h):
                if h == NH - 1 and isinstance(b, int) and b == 0:
                    sp.wait_ge(sm["setup_pool"], 1)
                    sp.dma_start(x_exp.rearrange("(n p) d -> p n d", p=P),
                                 zero[:, :].unsqueeze(1).to_broadcast([P, NR, D])).then_inc(sm["zeroed"], 16)
                if h == 3:
                    if isinstance(b, int) and b == B - 1:
                        g = wall[:, E, 0:KT * 2 * I].rearrange("p (k f) -> p k f", k=KT)
                        sp.dma_start(g[:, :, 0:I], sh_gate.rearrange("(k p) f -> p k f", p=P)
                                     ).then_inc(sm["w_in"], 16)
                        sp.dma_start(g[:, :, I:2 * I], sh_up.rearrange("(k p) f -> p k f", p=P)
                                     ).then_inc(sm["w_in"], 16)
                        sp.dma_start(wall[:, E, KT * 2 * I:WLEN].rearrange("p (k n) -> p k n", n=D),
                                     sh_down.rearrange("(k p) n -> p k n", p=P)).then_inc(sm["w_in"], 16)
                    elif not (isinstance(b, int) and b == 0):
                        weights(b - 1)

            steps = {"A_stack": stack(0), "N_stack": stack(1), "D_store": xn2_store, "SM": nothing}
            order = {0: ("N_stack",), 8: ("A_stack",), 15: ("D_store",)}

            def tail():
                xn2_store(B - 1, 1)
                sp.wait_ge(sm["rt_ps"], B)
                sp.wait_ge(sm["xn2_out"], 16 * B)
                for e in (E - 2, E - 1):
                    weights(e, "w67_in")

            run_attention(sp, head, steps, order, tail)

            sp.wait_ge(sm["xn2_out"], 16 * B)

            def load(seq, n, p, kind):
                if counted(seq - 1):
                    sp.wait_ge(sm["xT_ps"], seq - 1)
                if kind == "R" and isinstance(seq, int) and seq == R0:
                    sp.wait_ge(sm["scattered0"], 16 * NT)
                sp.dma_start(xl[:, p, :], rows_of(seq, kind)).then_inc(sm[f"xl_in{p}"], 16)

            def front():
                load(0, 0, 0, "A")
                load(1, 0, 1, "A")

            def body(seq, n, p, kinds):
                if kinds[2:]:
                    load(seq + 2, n + 1, p, kinds[2])

            def store(c, p):
                sp.wait_ge(sm["fin_ready"], c + 1)
                sp.dma_start(out.rearrange("(g r) d -> r g d", g=2)[ds(P * c, P), :, :], z_sb[:, p, :, :]
                             ).then_inc(sm[f"out_done{p}"], 16)

            def final(c, n, p):
                if not (isinstance(c, int) and c < 2):
                    store(c - 2, p)

            run_ffn(sp, front, body, final)
            store(HALF - 2, 0)
            store(HALF - 1, 1)
            sp.wait_ge(sm["out_done0"], 16 * HALF // 2)
            sp.wait_ge(sm["out_done1"], 16 * HALF // 2)

        @block.gpsimd
        def _(pool):
            pool.memset(zero[:, :], 0.0).then_inc(sm["setup_pool"], 1)
            pool.memset(neg_half[:, :], -0.5).then_inc(sm["setup_pool"], 1)
            pool.wait_ge(sm["setup_pool"], 2)

            def power(name, count, out_ap, in_ap, n):
                if counted(count):
                    pool.wait_ge(sm[f"{name}_var"], count)
                pool.tensor_tensor(out_ap, in_ap, neg_half[:, 0:1].to_broadcast([P, n]), ALU.pow
                                   ).then_inc(sm[f"{name}_rstd"], 1)

            def rotate(k, b):
                pool.wait_ge(sm[f"{k}_swap"], b + 1)
                pool.tensor_tensor(yr[k][:, :], yr[k][:, :], cst[:, C_COS:C_COS + S],
                                   ALU.mult).then_inc(sm[f"{k}_mul"], 1)
                pool.tensor_tensor(swp[k][:, :], swp[k][:, :], cst[:, C_SIN:C_SIN + S],
                                   ALU.mult).then_inc(sm[f"{k}_mul"], 1)
                pool.wait_ge(sm[f"{k}_mul"], 2 * b + 2)
                pool.tensor_tensor(yr[k][:, :], yr[k][:, :], swp[k][:, :], ALU.add
                                   ).then_inc(sm[f"{k}_rot"], 1)

            def residual(k, b):
                pool.wait_ge(sm[f"{k}h"], b + 1)
                pool.tensor_tensor(full[k], full[k], parts[k][:, 0, :, :], ALU.subtract
                                   ).then_inc(sm[f"{k}_res"], 1)

            def low(k, b):
                pool.wait_ge(sm[f"{k}m"], b + 1)
                pool.tensor_tensor(parts[k][:, 2, :, :], full[k], parts[k][:, 1, :, :], ALU.subtract
                                   ).then_inc(sm[f"{k}l"], 1)

            def add_x(b, par):
                pool.wait_ge(sm["yn_ready"], TB * (b + 1))
                tile = x_sb[:, ds(TB * b, TB), :]
                pool.tensor_tensor(tile, tile, y_sb[:, :, :], ALU.add).then_inc(sm["x1_ready"], 1)

            steps = {
                "A_power": lambda b, par: power("in", b + 1, rstd["in"][:, :], var["in"][:, :], TB),
                "A_krot": lambda b, par: rotate("k", b), "A_qrot": lambda b, par: rotate("q", b),
                "A_kres": lambda b, par: residual("k", b), "A_qres": lambda b, par: residual("q", b),
                "A_klow": lambda b, par: low("k", b), "A_qlow": lambda b, par: low("q", b),
                "D_power": lambda b, par: power("at", b + 1, rstd["at"][:, :], var["at"][:, :], TB),
                "D_x1": add_x,
                "D_power2": lambda b, par: power("ff", b + 1, rstd2[:, ds(TB * b, TB)], var["ff"][:, :], TB),
                "SM": nothing}
            order = {0: ("A_power",), 4: ("A_krot",), 5: ("A_qrot",), 7: ("D_power",), 8: ("A_kres", "A_qres", "D_x1"),
                     9: ("A_klow",), 10: ("A_qlow",), 11: ("D_power2",)}

            def tail():
                for name in ("D_power", "D_x1", "D_power2"):
                    steps[name](B - 1, 1)

            run_attention(pool, nothing, steps, order, tail)

            pool.wait_ge(sm["pos_ready"], 1)
            pool.wait_ge(sm["zeroed"], 16)
            for j in range(NT):
                pool.wait_ge(sm["xr_ready"], j + 1)
                pool.indirect_dma_start(
                    out=x_exp, out_offset=bass.IndirectOffsetOnAxis(ap=pos_i[:, j:j + 1], axis=0),
                    in_=xr[:, j, :], in_offset=None).then_inc(sm["scattered0"], 16)

            def gather(c, name):
                for j in (HALF + c, c):
                    pool.indirect_dma_start(
                        out=routed[:, j, :], out_offset=None, in_=y_exp,
                        in_offset=bass.IndirectOffsetOnAxis(ap=pos_i[:, j:j + 1], axis=0)).then_inc(sm[name], 16)

            def before_finals():
                pool.wait_ge(sm["scattered0"], 16 * NT)
                pool.wait_ge(sm["y_out0"], 16 * ((NR + 1) // 2))
                pool.wait_ge(sm["y_out1"], 16 * (NR // 2))
                for c, name in ((0, "gathered0"), (1, "gathered1"), (2, "gathered2"), (3, "gathered2")):
                    gather(c, name)

            x_two = x_sb[:, :, :].rearrange("p (g n) d -> p n g d", g=2)

            def final(c, n, p):
                power("out", c + 1, rstd_f[:, p, :], var_f[:, p, :], 2)
                pool.wait_ge(sm["zn_ready"], 2 * c + 2)
                pool.tensor_tensor(z_sb[:, p, :, :], z_sb[:, p, :, :],
                                   x_two[:, ds(c, 1), :, :].rearrange("p a g d -> p (a g) d"), ALU.add
                                   ).then_inc(sm["fin_ready"], 1)
                if isinstance(c, int) and c == 0:
                    for rest in range(4, HALF):
                        gather(rest, "gathered2")

            run_ffn(pool, nothing, nothing, final, before_finals)

        @block.scalar
        def _(act):
            def xnT_copy(b, par):
                act.wait_ge(sm["xnT_ps"], b + 1)
                act.activation(xnT, two(w0), ACT.Copy).then_inc(sm["xnT_sb"], 1)

            def ct_copy(b, par):
                if isinstance(b, int) and b == 0:
                    act.wait_ge(sm["bias_sum"], 1)
                act.wait_ge(sm["ct_ps"], b + 1)
                if counted(b):
                    act.wait_ge(sm["v_ps"], b)
                for m in range(2):
                    act.activation(ctT[:, m, :], two(w1)[:, m, :], ACT.Identity, bias=bcol[:, m:m + 1]
                                   ).then_inc(sm["ct_sb"], 1)

            def rope_copy(k, bank_, col):
                def f(b, par):
                    act.wait_ge(sm[f"{k}0_ps"], b + 1)
                    if counted(b):
                        act.wait_ge(sm[f"{k}0_done"], b)
                    act.activation(yr[k][:, :], two(bank_)[:, 1, :], ACT.Identity,
                                   bias=bcol[:, col:col + 1]).then_inc(sm[f"{k}r_sb"], 1)
                return f

            def qk1_copy(b, par):
                act.wait_ge(sm["qk1_ps"], b + 1)
                if counted(b):
                    act.wait_ge(sm["kl"], b)
                if counted(b):
                    act.wait_ge(sm["ql"], b)
                act.activation(kf[:, 1, :], two(w0)[:, 1, :], ACT.Identity, bias=bcol[:, 7:8]
                               ).then_inc(sm["qk1_sb"], 1)
                act.activation(qf[:, 1, :], two(w0)[:, 0, :], ACT.Identity, bias=bcol[:, 3:4]
                               ).then_inc(sm["qk1_sb"], 1)

            def high_parts(b, par):
                act.wait_ge(sm["qk1_sb"], 2 * b + 2)
                if counted(16 * 2 * NSLOT * b):
                    act.wait_ge(sm["stacked0"], 16 * 2 * NSLOT * b)
                if counted(16 * 2 * NSLOT * b):
                    act.wait_ge(sm["stacked1"], 16 * 2 * NSLOT * b)
                for k in ("k", "q"):
                    act.wait_ge(sm[f"{k}0_done"], b + 1)
                    act.activation(parts[k][:, 0, :, :], full[k], ACT.Copy).then_inc(sm[f"{k}h"], 1)

            def mid_parts(b, par):
                for k in ("k", "q"):
                    act.wait_ge(sm[f"{k}_res"], b + 1)
                    act.activation(parts[k][:, 1, :, :], full[k], ACT.Copy).then_inc(sm[f"{k}m"], 1)

            def mT_out(b, par, half):
                act.wait_ge(sm["mT_ps"], 2 * b + half + 1)
                if half:
                    act.wait_ge(sm["m_rows0"], 16 * (b + 1))
                else:
                    if counted(16 * b):
                        act.wait_ge(sm["m_rows1"], 16 * b)
                act.activation(mT[:, :], w2[:, 0:P].bitcast(BF16)[0:NPART * NH // 2, :], ACT.Copy
                               ).then_inc(sm["mT_sb"], 1)
                act.wait_ge(sm["mT_sb"], 2 * b + half + 1)
                act.dma_start(stacks[ROWS:MROWS, par, 0, 8 * half:8 * half + 8, :],
                              mT[:, :]).then_inc(sm[f"m_rows{half}"], 16)

            def o_copy(b, half):
                act.wait_ge(sm["av_done"], NH * b + 8 * half + 8)
                if counted(2 * b):
                    act.wait_ge(sm["avT_ps"], 2 * b)
                act.activation(o_sb[:, 2 * half:2 * half + 2, :], two(av_bank), ACT.Copy
                               ).then_inc(sm["o_copied"], 1)

            def head(b, par, h):
                act.wait_ge(sm["st_ready"], NH * b + h + 1)
                if counted(NH * b + h - 3):
                    act.wait_ge(sm["av_done"], NH * b + h - 3)
                act.activation(probs[:, h % 4, :], st_bank[h % 2][:, :], ACT.Exp, scale=SCALE
                               ).then_inc(sm["exp_done"], 1)

            def aT_copy(b, par):
                act.wait_ge(sm["aT_ps"], b + 1)
                if counted(b):
                    act.wait_ge(sm["wo_ps"], b)
                act.activation(aT[:, :, :], two(w2), ACT.Copy).then_inc(sm["aT_sb"], 1)

            def xn2T_copy(b, par):
                act.wait_ge(sm["xn2T_ps"], b + 1)
                if counted(b):
                    act.wait_ge(sm["rt_ps"], b)
                act.activation(xn2T[:, :, :], two(w2), ACT.Copy).then_inc(sm["xn2T_sb"], 1)

            steps = {
                "A_xnT": xnT_copy, "A_ct": ct_copy, "A_k0": rope_copy("k", w0, 6), "A_q0": rope_copy("q", w1, 4),
                "A_qk1": qk1_copy, "A_high": high_parts, "A_mid": mid_parts,
                "M0": lambda b, par: mT_out(b, par, 0), "M1": lambda b, par: mT_out(b, par, 1),
                "M1_o0": lambda b, par: o_copy(b, 0), "D_o1": lambda b, par: o_copy(b, 1),
                "D_aT": aT_copy, "D_xn2T": xn2T_copy, "SM": nothing}
            order = {0: ("D_o1",), 1: ("M1",), 2: ("A_xnT",), 3: ("A_ct",), 4: ("A_k0",), 5: ("A_q0", "D_aT"),
                     7: ("A_qk1",), 8: ("M1_o0", "A_high",), 10: ("A_mid",), 11: ("M0",), 13: ("D_xn2T",)}

            def tail():
                for name in ("D_o1", "D_aT", "D_xn2T"):
                    steps[name](B - 1, 1)

            run_attention(act, head, steps, order, tail)

            act.wait_ge(sm["rt"], 1)
            act.activation(score[:, :], lmax[:, :], ACT.Exp, scale=-1.0).then_inc(sm["rt_exp"], 1)

            def xT_copy(seq, p):
                act.wait_ge(sm["xT_ps"], seq + 1)
                act.activation(xT[:, p, :], bank[0][:, 0:KT * P], ACT.Copy).then_inc(sm["xT_sb"], 1)

            def silu(seq):
                act.wait_ge(sm["g_ps"], seq + 1)
                act.activation(sg, bank[1][:, :], ACT.Silu).then_inc(sm["sg_sb"], 1)

            def front():
                xT_copy(0, 0)
                silu(0)
                xT_copy(1, 1)

            def body(seq, n, p, kinds):
                kind = kinds[0]
                if kinds[1:]:
                    silu(seq + 1)
                if kinds[2:]:
                    xT_copy(seq + 2, p)
                if kind == "B":
                    return
                act.wait_ge(sm["y_ps"], seq + 1)
                if kind == "A":
                    act.activation(y_first[:, ds(seq, 1), :].rearrange("p a c -> p (a c)"), y_bank[p][:, 0:D],
                                   ACT.Copy).then_inc(sm["ys_sb"], 1)
                    return
                if not (isinstance(seq, int) and seq < R0 + 2):
                    if counted(16 * (n - R0 // 2)):
                        act.wait_ge(sm[f"y_out{p}"], 16 * (n - R0 // 2))
                act.activation(ys[:, p, :], y_bank[p][:, 0:D], ACT.Copy).then_inc(sm["ys_sb"], 1)
                act.wait_ge(sm["ys_sb"], seq + 1)
                act.dma_start(y_exp[ds(P * (seq - R0), P), :], ys[:, p, :]).then_inc(sm[f"y_out{p}"], 16)

            run_ffn(act, front, body)

        @block.vector
        def _(dve):
            dve.memset(ones_bf[:, :], 1.0).then_inc(sm["setup_dve"], 1)
            for par in range(2):
                dve.memset(v_aug[:, par, :, :, HD:2 * HD], 1.0).then_inc(sm["setup_dve"], 1)
                dve.memset(stacks[ROWS:MROWS, par, 1, :, :], 1.0).then_inc(sm["setup_dve"], 1)
            dve.wait_ge(sm["const_in"], 16)
            dve.tensor_copy(idb[:, :], cst[:, C_ID:C_ID + P]).then_inc(sm["setup_dve"], 1)
            dve.tensor_copy(tri_bf[:, :], cst[:, C_TRI:C_TRI + P]).then_inc(sm["setup_dve"], 1)

            def ln_head(name, b, tiles, stat, mean_var, var_ap, n):
                for t in range(n):
                    dve.bn_stats(stat[:, t, :], tiles(t)).then_inc(sm[f"{name}_stats"], 1)
                dve.wait_ge(sm[f"{name}_stats"], n * (b + 1))
                dve.sem_inc(sm["passed"], 1)
                for t in range(n):
                    dve.bn_aggr(mean_var(t), stat[:, t, :]).then_inc(sm[f"{name}_aggr"], 1)
                dve.wait_ge(sm[f"{name}_aggr"], n * (b + 1))

            def a_stats(b, par):
                if isinstance(b, int) and b <= 1:
                    dve.wait_ge(sm["x0_in" if b == 0 else "x_in"], 16)
                tiles = lambda t: x_sb[:, ds(TB * b + t, 1), :].rearrange("p a c -> p (a c)")
                ln_head("in", b, tiles, stats["in"], lambda t: mv["in"][:, t, :], var["in"], TB)
                dve.tensor_scalar(var["in"][:, :], mv["in"][:, :, 1], EPS, None, ALU.add
                                  ).then_inc(sm["in_var"], 1)

            def a_norm(b, par):
                tiles = lambda t: x_sb[:, ds(TB * b + t, 1), :].rearrange("p a c -> p (a c)")
                dve.wait_ge(sm["in_rstd"], b + 1)
                if counted(b):
                    dve.wait_ge(sm["xnT_ps"], b)
                for t in range(TB):
                    dve.tensor_scalar(xn[:, t, :], tiles(t), mv["in"][:, t, 0:1], rstd["in"][:, t:t + 1],
                                      ALU.subtract, ALU.mult).then_inc(sm["xn_ready"], 1)

            SWAP = [i ^ HT for i in range(32)]

            def swap(k, col, bank_):
                def f(b, par):
                    dve.wait_ge(sm[f"{k}r_sb"], b + 1)
                    dve.sem_inc(sm["passed"], 1)
                    dve.stream_shuffle(swp[k][:, :], yr[k][:, :], SWAP).then_inc(sm[f"{k}_swap"], 1)
                return f

            def add0(k, col, bank_):
                def f(b, par):
                    dve.wait_ge(sm[f"{k}_rot"], b + 1)
                    if counted(b):
                        dve.wait_ge(sm[f"{k}l"], b)
                    dve.scalar_tensor_tensor(full[k][:, 0, :], two(bank_)[:, 0, :], bcol[:, col:col + 1],
                                             yr[k][:, :], ALU.add, ALU.add).then_inc(sm[f"{k}0_done"], 1)
                return f

            k_swap, q_swap = swap("k", 5, w0), swap("q", 2, w1)
            k_add, q_add = add0("k", 5, w0), add0("q", 2, w1)

            def v_add(b, par):
                dve.wait_ge(sm["v_ps"], b + 1)
                if counted(NH * (b - 1)):
                    dve.wait_ge(sm["av_done"], NH * (b - 1))
                dve.tensor_tensor(v_aug[:, par, :, :, 0:HD],
                                  two(w1).rearrange("p t (h d) -> p t h d", d=HD),
                                  bv_sb[:, :].rearrange("p (h d) -> p h d", d=HD).unsqueeze(1)
                                  .to_broadcast([P, TB, NH, HD]), ALU.add).then_inc(sm["v_ready"], 1)

            def sm_max(b, par, u):
                half, qt, pair = u // 8, (u // 4) % 2, u % 4
                dve.wait_ge(sm["sm_ps"], NH * b + u + 1)
                dve.tensor_reduce(nmax[:, half, qt, 2 * pair:2 * pair + 2], two(sm_bank[u % 2]), AX.X,
                                  ALU.max, negate=True).then_inc(sm["sm_max"], 1)

            def m_split(b, par, half):
                n = 8 * b + 4 * half
                dve.wait_ge(sm["sm_max"], NH * b + 8 * (half + 1))
                if counted(2 * b + half):
                    dve.wait_ge(sm["mT_ps"], 2 * b + half)
                src, res = nmax[:, half, :, :], nres[:, half, :, :]
                dve.tensor_copy(mparts[:, :, 0, :], src).then_inc(sm["m_parts"], 1)
                dve.wait_ge(sm["m_parts"], n + 1)
                dve.tensor_tensor(res, src, mparts[:, :, 0, :], ALU.subtract).then_inc(sm["m_parts"], 1)
                dve.wait_ge(sm["m_parts"], n + 2)
                dve.tensor_copy(mparts[:, :, 1, :], res).then_inc(sm["m_parts"], 1)
                dve.wait_ge(sm["m_parts"], n + 3)
                dve.tensor_tensor(mparts[:, :, 2, :], res, mparts[:, :, 1, :], ALU.subtract
                                  ).then_inc(sm["m_parts"], 1)

            def divide(t):
                def f(b, par):
                    dve.wait_ge(sm["avT_ps"], 2 * b + t + 1)
                    o = w2[:, :].rearrange("p (h c) -> p h c", c=2 * HD)
                    dve.reciprocal(rec[:, :], o[:, :, HD]).then_inc(sm["rec_ready"], 1)
                    dve.wait_ge(sm["rec_ready"], 2 * b + t + 1)
                    if counted(b):
                        dve.wait_ge(sm["aT_ps"], b)
                    dve.tensor_tensor(a_sb[:, t, :].rearrange("p (h c) -> p h c", c=HD), o[:, :, 0:HD],
                                      rec[:, :].unsqueeze(2).to_broadcast([P, NH, HD]), ALU.mult
                                      ).then_inc(sm["a_ready"], 1)
                return f

            def d_wo(b, par):
                dve.wait_ge(sm["wo_ps"], b + 1)
                if counted(b):
                    dve.wait_ge(sm["x1_ready"], b)
                dve.tensor_tensor(y_sb[:, :, :], two(w2), bo_sb[:, :].unsqueeze(1).to_broadcast([P, TB, D]),
                                  ALU.add).then_inc(sm["y_ready"], 1)
                dve.wait_ge(sm["y_ready"], b + 1)
                ln_head("at", b, lambda t: y_sb[:, t, :], stats["at"], lambda t: mv["at"][:, t, :], None, TB)
                dve.tensor_scalar(var["at"][:, :], mv["at"][:, :, 1], EPS, None, ALU.add
                                  ).then_inc(sm["at_var"], 1)

            def d_yn(b, par):
                dve.wait_ge(sm["at_rstd"], b + 1)
                for t in range(TB):
                    dve.tensor_scalar(y_sb[:, t, :], y_sb[:, t, :], mv["at"][:, t, 0:1],
                                      rstd["at"][:, t:t + 1], ALU.subtract, ALU.mult
                                      ).then_inc(sm["yn_ready"], 1)

            def d_stats(b, par):
                dve.wait_ge(sm["x1_ready"], b + 1)
                tiles = lambda t: x_sb[:, ds(TB * b + t, 1), :].rearrange("p a c -> p (a c)")
                ln_head("ff", b, tiles, stats["ff"], lambda t: mv["ff"][:, t, :], None, TB)
                dve.tensor_copy(mv2[:, ds(TB * b, TB), :], mv["ff"][:, :, :]).then_inc(sm["mv2_kept"], 1)
                dve.tensor_scalar(var["ff"][:, :], mv["ff"][:, :, 1], EPS, None, ALU.add
                                  ).then_inc(sm["ff_var"], 1)

            def d_xn2(b, par):
                tiles = lambda t: x_sb[:, ds(TB * b + t, 1), :].rearrange("p a c -> p (a c)")
                dve.wait_ge(sm["ff_rstd"], b + 1)
                if counted(b):
                    dve.wait_ge(sm["xn2T_ps"], b)
                if counted(16 * b):
                    dve.wait_ge(sm["xn2_out"], 16 * b)
                for t in range(TB):
                    dve.tensor_scalar(xn2[:, t, :], tiles(t), mv["ff"][:, t, 0:1],
                                      rstd2[:, ds(TB * b + t, 1)], ALU.subtract, ALU.mult
                                      ).then_inc(sm["xn2_ready"], 1)

            def d_router(b, par):
                dve.wait_ge(sm["rt_ps"], b + 1)
                dve.tensor_copy(logits[:, ds(TB * b, TB), :],
                                w2[:, 0:TB * E].rearrange("p (t e) -> p t e", e=E)).then_inc(sm["logits_sb"], 1)

            steps = {
                "A_stats": a_stats, "A_norm": a_norm, "A_kswap": k_swap, "A_kadd": k_add, "A_qswap": q_swap,
                "A_qadd": q_add, "N_v": v_add, "SM": sm_max,
                "M0": lambda b, par: m_split(b, par, 0), "M1": lambda b, par: m_split(b, par, 1),
                "D_div0": divide(0), "D_div1": divide(1), "D_y": d_wo, "D_yn": d_yn, "D_stats": d_stats,
                "D_xn2": d_xn2, "D_router": d_router}
            order = {0: ("A_stats", "M1", "N_v"), 1: ("A_norm",), 2: ("D_div0",), 3: ("D_div1",), 4: ("A_kswap",),
                     5: ("A_qswap",), 6: ("A_kadd",), 7: ("A_qadd", "D_y"), 8: ("D_yn",),
                     9: ("M0",), 11: ("D_stats",), 12: ("D_xn2",), 15: ("D_router",)}

            def bias_sums():
                if counted(16 * 8):
                    dve.wait_ge(sm["attn_w"], 16 * 8)
                dve.tensor_tensor(bcol[:, 3:4], bcol[:, 8:9], bcol[:, 9:10], ALU.add)
                dve.tensor_tensor(bcol[:, 7:8], bcol[:, 10:11], bcol[:, 11:12], ALU.add
                                  ).then_inc(sm["bias_sum"], 1)

            bias_sums()

            def tail():
                for name in ("D_div0", "D_div1", "D_y", "D_yn", "D_stats", "D_xn2", "D_router"):
                    steps[name](B - 1, 1)

            run_attention(dve, nothing, steps, order, tail)

            done = [0]

            def chain(ins):
                done[0] += 1
                ins.then_inc(sm["rt"], 1)
                if counted(done[0]):
                    dve.wait_ge(sm["rt"], done[0])

            def spread(ap, n):
                return ap.unsqueeze(2).to_broadcast([P, NT, n])

            dve.wait_ge(sm["logits_sb"], B)
            chain(dve.tensor_reduce(lmax[:, :], logits[:, :, :], AX.X, ALU.max))
            chain(dve.tensor_tensor(work_r[:, :, :], logits[:, :, :], spread(lmax[:, :], E), ALU.is_equal))
            desc = cst[:, C_DESC:C_DESC + E].unsqueeze(1).to_broadcast([P, NT, E])
            chain(dve.tensor_tensor(work_r[:, :, :], work_r[:, :, :], desc, ALU.mult))
            chain(dve.tensor_reduce(pos[:, :], work_r[:, :, :], AX.X, ALU.max))
            chain(dve.tensor_tensor(onehot[:, :, :], work_r[:, :, :], spread(pos[:, :], E), ALU.is_equal))
            dve.tensor_copy(oh_bf[:, :, :], onehot[:, :, :]).then_inc(sm["oh_ready"], 1)
            dve.wait_ge(sm["rt_exp"], 1)
            chain(dve.tensor_scalar(score[:, :], score[:, :], 1.0, None, ALU.add))
            chain(dve.reciprocal(score[:, :], score[:, :]))
            chain(dve.tensor_tensor(gain[:, :], score[:, :], rstd2[:, :], ALU.mult))
            dve.wait_ge(sm["rank_ps"], 1)
            chain(dve.tensor_copy(cnt[:, 0, :], bank[6][:, 0:E]))
            chain(dve.tensor_tensor(cmp_t[:, :, :], cnt[:, 0, :].unsqueeze(2).to_broadcast([P, E, NT]),
                                    cst[:, C_TILE:C_TILE + NT].unsqueeze(1).to_broadcast([P, E, NT]), ALU.is_gt))
            chain(dve.tensor_reduce(cnt[:, 1, :], cmp_t[:, :, :], AX.X, ALU.add))
            le = cst[:, C_LE:C_LE + E * E].rearrange("p (a b) -> p a b", a=E)
            chain(dve.tensor_tensor(cmp_t[:, :, 0:E], le, cnt[:, 1, :].unsqueeze(1).to_broadcast([P, E, E]),
                                    ALU.mult))
            chain(dve.tensor_reduce(cnt[:, 2, :], cmp_t[:, :, 0:E], AX.X, ALU.add))
            chain(dve.tensor_tensor(cnt[:, 3, :], cnt[:, 2, :], cnt[:, 1, :], ALU.subtract))
            chain(dve.tensor_scalar(cnt[:, 3, :], cnt[:, 3, :], float(P), None, ALU.mult))
            chain(dve.tensor_tensor(work_r[:, :, :], bank[5][:, 0:NT * E].rearrange("p (t e) -> p t e", e=E),
                                    cnt[:, 3, :].unsqueeze(1).to_broadcast([P, NT, E]), ALU.add))
            chain(dve.tensor_tensor(work_r[:, :, :], work_r[:, :, :], onehot[:, :, :], ALU.mult))
            chain(dve.tensor_reduce(pos[:, :], work_r[:, :, :], AX.X, ALU.add))
            dve.tensor_copy(pos_i[:, :], pos[:, :]).then_inc(sm["pos_ready"], 1)
            dve.wait_ge(sm["mv2_kept"], B)
            for j in range(NT):
                dve.tensor_scalar(xr[:, j, :], x_sb[:, j, :], mv2[:, j, 0:1], gain[:, j:j + 1],
                                  ALU.subtract, ALU.mult).then_inc(sm["xr_ready"], 1)
            chain(dve.tensor_tensor(cmp_e[:, :, :], cnt[:, 2, :].unsqueeze(1).to_broadcast([P, NR, E]),
                                    cst[:, C_NUM:C_NUM + NR].unsqueeze(2).to_broadcast([P, NR, E]), ALU.is_le))
            chain(dve.tensor_reduce(eid[:, :], cmp_e[:, :, :], AX.X, ALU.add))
            chain(dve.tensor_scalar(eid[:, :], eid[:, :], float(E - 1), None, ALU.min))
            dve.tensor_copy(eid_i[:, :], eid[:, :]).then_inc(sm["pos_ready"], 1)

            def hidden(seq):
                dve.wait_ge(sm["sg_sb"], seq + 1)
                dve.wait_ge(sm["u_ps"], seq + 1)
                dve.tensor_tensor(hid, sg, bank[2][:, :], ALU.mult).then_inc(sm["h_sb"], 1)

            def front():
                hidden(0)

            def body(seq, n, p, kinds):
                dve.wait_ge(sm["hT_ps"], seq + 1)
                dve.tensor_copy(hT, bank[3][:, :]).then_inc(sm["hT_sb"], 1)
                if kinds[1:]:
                    hidden(seq + 1)

            def normalise(c, p):
                dve.wait_ge(sm["out_rstd"], c + 1)
                for g in range(2):
                    dve.tensor_scalar(z_sb[:, p, g, :], z_sb[:, p, g, :], mv_f[:, p, g, 0:1],
                                      rstd_f[:, p, g:g + 1], ALU.subtract, ALU.mult
                                      ).then_inc(sm["zn_ready"], 1)

            def final(c, n, p):
                if not (isinstance(c, int) and c == 0):
                    normalise(c - 1, 1 - p)
                dve.wait_ge(sm["y_ps"], c + B0 + 1)
                if isinstance(c, int) and c < 2:
                    dve.wait_ge(sm[f"gathered{c}"], 32)
                else:
                    dve.wait_ge(sm["gathered2"], 32 * (HALF - 2))
                    dve.wait_ge(sm[f"out_done{p}"], 16 * n)
                for g, y in ((1, y_bank[(B0 + p) % 2][:, 0:D]),
                             (0, y_first[:, ds(c, 1), :].rearrange("p a d -> p (a d)"))):
                    dve.tensor_tensor(z_sb[:, p, g, :], y,
                                      routed[:, ds(c + HALF * g, 1), :].rearrange("p a d -> p (a d)"), ALU.add
                                      ).then_inc(sm["z_ready"], 1)
                dve.wait_ge(sm["z_ready"], 2 * c + 2)
                dve.sem_inc(sm["passed"], 1)
                for g in range(2):
                    dve.bn_stats(stats_f[:, p, g, :], z_sb[:, p, g, :]).then_inc(sm["out_stats"], 1)
                dve.wait_ge(sm["out_stats"], 2 * c + 2)
                dve.sem_inc(sm["passed"], 1)
                for g in range(2):
                    dve.bn_aggr(mv_f[:, p, g, :], stats_f[:, p, g, :]).then_inc(sm["out_aggr"], 1)
                dve.wait_ge(sm["out_aggr"], 2 * c + 2)
                dve.tensor_scalar(var_f[:, p, :], mv_f[:, p, :, 1], EPS, None, ALU.add
                                  ).then_inc(sm["out_var"], 1)

            run_ffn(dve, front, body, final)
            normalise(HALF - 1, 1)

        @block.tensor
        def _(pe):
            ident = cst[:, C_ID:C_ID + P]

            def products(out_ap, pairs):
                for n, (lhsT, rhs) in enumerate(pairs):
                    last = pe.matmul(out_ap, lhsT, rhs, start=(n == 0), stop=(n == len(pairs) - 1))
                return last

            def turn(out_ap, in_ap):
                return pe.transpose(out_ap, in_ap, ident)

            def a_xnT(b, par):
                if isinstance(b, int) and b == 0:
                    pe.wait_ge(sm["const_in"], 16)
                pe.wait_ge(sm["xn_ready"], TB * (b + 1))
                if counted(2 * b):
                    pe.wait_ge(sm["qk1_sb"], 2 * b)
                for k in range(KT):
                    for t in range(TB):
                        last = turn(two(w0)[:, k, P * t:P * t + P], xn[:, t, P * k:P * k + P])
                last.then_inc(sm["xnT_ps"], 1)

            def a_ct(b, par):
                if isinstance(b, int) and b == 0:
                    if counted(16 * 8):
                        pe.wait_ge(sm["attn_w"], 16 * 8)
                pe.wait_ge(sm["xnT_sb"], b + 1)
                if counted(b):
                    pe.wait_ge(sm["v_ready"], b)
                for m in range(2):
                    last = products(two(w1)[:, m, :], [(wd_sb[:, k, P * m:P * m + P], xnT[:, k, :])
                                                       for k in range(KT)])
                last.then_inc(sm["ct_ps"], 1)

            def a_k0(b, par):
                pe.wait_ge(sm["ct_sb"], 2 * b + 2)
                for r in range(2):
                    last = products(two(w0)[:, r, :], [(wkv_sb[:, D * r:D * r + P], ctT[:, 1, :])])
                last.then_inc(sm["k0_ps"], 1)

            def a_q0(b, par):
                for r in range(2):
                    last = products(two(w1)[:, r, :], [(wq_sb[:, k, D * r:D * r + P], ctT[:, k, :])
                                                       for k in range(KT)])
                last.then_inc(sm["q0_ps"], 1)

            def a_qk1(b, par):
                pe.wait_ge(sm["kr_sb"], b + 1)
                pe.wait_ge(sm["k0_done"], b + 1)
                products(two(w0)[:, 0, :], [(wq_sb[:, k, D * r + P:D * r + 2 * P], ctT[:, k, :])
                                            for k in range(KT) for r in range(2)])
                products(two(w0)[:, 1, :], [(wkv_sb[:, D * r + P:D * r + 2 * P], ctT[:, 1, :])
                                            for r in range(2)]).then_inc(sm["qk1_ps"], 1)

            def a_v(b, par):
                pe.wait_ge(sm["qr_sb"], b + 1)
                pe.wait_ge(sm["q0_done"], b + 1)
                for t in range(TB):
                    last = products(two(w1)[:, t, :], [(ctT[:, 1, P * t:P * t + P], wkv_sb[:, 2 * D:3 * D])])
                last.then_inc(sm["v_ps"], 1)

            def sm_scores(b, par, u):
                half, qt, pair = u // 8, (u // 4) % 2, u % 4
                if u % 8 == 0:
                    pe.wait_ge(sm[f"stacked{half}"], 16 * 2 * NSLOT * (b + 1))
                if counted(NH * b + u - 1):
                    pe.wait_ge(sm["sm_max"], NH * b + u - 1)
                for c in range(2):
                    h = 8 * half + 2 * pair + c
                    last = pe.matmul(two(sm_bank[u % 2])[:, c, :],
                                     stacks[0:ROWS, par, 0, h, P * qt:P * qt + P],
                                     stacks[0:ROWS, par, 1, h, :], start=True, stop=True)
                last.then_inc(sm["sm_ps"], 1)

            def m_turn(b, par, half):
                pe.wait_ge(sm["m_parts"], 8 * b + 4 * half + 4)
                if half:
                    pe.wait_ge(sm["mT_sb"], 2 * b + 1)
                    if counted(b - 1):
                        pe.wait_ge(sm["logits_sb"], b - 1)
                else:
                    if counted(b - 1):
                        pe.wait_ge(sm["y_ready"], b - 1)
                    if counted(2 * b):
                        pe.wait_ge(sm["mT_sb"], 2 * b)
                for t in range(TB):
                    last = pe.transpose(w2[:, 0:P].bitcast(BF16)[0:NPART * NH // 2, P * t:P * t + P],
                                        mparts[:, t, :, :].rearrange("p a h -> p (a h)"), idb[:, :])
                last.then_inc(sm["mT_ps"], 1)

            def probs_v(b, par, h):
                pe.wait_ge(sm["exp_done"], NH * b + h + 1)
                if h % 8 == 0:
                    if counted(2 * b + h // 8):
                        pe.wait_ge(sm["o_copied"], 2 * b + h // 8)
                if h == 0:
                    pe.wait_ge(sm["v_ready"], b + 1)
                c = h % 4
                for k in range(TB):
                    last = pe.matmul(two(av_bank)[32 * c:32 * c + 32, (h % 8) // 4, :],
                                     v_aug[:, par, k, h, :], probs[:, h % 4, S * k:S * k + S],
                                     start=(k == 0), stop=(k == TB - 1))
                last.then_inc(sm["av_done"], 1)

            def head(b, par, h):
                if h == 0:
                    pe.wait_ge(sm["m_rows0"], 16 * (b + 1))
                if h == 8:
                    pe.wait_ge(sm["m_rows1"], 16 * (b + 1))
                if counted(NH * b + h - 1):
                    pe.wait_ge(sm["exp_done"], NH * b + h - 1)
                for k in range(TB):
                    last = pe.matmul(two(st_bank[h % 2])[:, k, :],
                                     stacks[0:MROWS, par, 1, h, P * k:P * k + P],
                                     stacks[0:MROWS, par, 0, h, :], start=True, stop=True)
                last.then_inc(sm["st_ready"], 1)

            def behind(b, par, h):
                if h > 0:
                    probs_v(b, par, h - 1)
                elif exists(b - 1):
                    probs_v(b - 1, 1 - par, NH - 1)

            def av_turn(t):
                def f(b, par):
                    if t == 0:
                        pe.wait_ge(sm["o_copied"], 2 * b + 2)
                        if isinstance(b, int) and b == B - 1:
                            if counted(b):
                                pe.wait_ge(sm["logits_sb"], b)
                        else:
                            pe.wait_ge(sm["mT_sb"], 2 * b + 4)
                    else:
                        pe.wait_ge(sm["a_ready"], 2 * b + 1)
                    for g in range(4):
                        last = turn(w2[:, P * g:P * g + P], o_sb[:, g, P * t:P * t + P])
                    last.then_inc(sm["avT_ps"], 1)
                return f

            def a_turn(b, par):
                pe.wait_ge(sm["a_ready"], 2 * b + 2)
                for k in range(KT):
                    for t in range(TB):
                        last = turn(two(w2)[:, k, P * t:P * t + P], a_sb[:, t, P * k:P * k + P])
                last.then_inc(sm["aT_ps"], 1)

            def d_wo(b, par):
                pe.wait_ge(sm["aT_sb"], b + 1)
                for t in range(TB):
                    last = products(two(w2)[:, t, :], [(aT[:, k, P * t:P * t + P], wo_sb[:, k, :])
                                                       for k in range(KT)])
                last.then_inc(sm["wo_ps"], 1)

            def d_xn2T(b, par):
                pe.wait_ge(sm["xn2_ready"], TB * (b + 1))
                if exists(b + 2):
                    pe.wait_ge(sm["mT_sb"], 2 * b + 5)
                for k in range(KT):
                    for t in range(TB):
                        last = turn(two(w2)[:, k, P * t:P * t + P], xn2[:, t, P * k:P * k + P])
                last.then_inc(sm["xn2T_ps"], 1)

            def d_router(b, par):
                pe.wait_ge(sm["xn2T_sb"], b + 1)
                for t in range(TB):
                    last = products(w2[:, E * t:E * t + E], [(xn2T[:, k, P * t:P * t + P], wr_sb[:, k, :])
                                                             for k in range(KT)])
                last.then_inc(sm["rt_ps"], 1)

            steps = {"A_xnT": a_xnT, "A_ct": a_ct, "A_k0": a_k0, "A_q0": a_q0, "A_qk1": a_qk1, "A_v": a_v,
                     "SM": sm_scores, "M0": lambda b, par: m_turn(b, par, 0),
                     "M1": lambda b, par: m_turn(b, par, 1), "D_avT0": av_turn(0), "D_avT1": av_turn(1),
                     "D_aT": a_turn, "D_wo": d_wo, "D_xn2T": d_xn2T, "D_router": d_router}
            order = {1: ("M1",), 2: ("A_xnT", "D_avT0"), 3: ("A_ct", "D_avT1"), 4: ("A_k0", "D_aT"),
                     5: ("A_q0",), 6: ("D_wo",), 7: ("A_qk1",), 8: ("A_v",),
                     11: ("M0",), 13: ("D_xn2T",), 14: ("D_router",)}

            def tail():
                b = B - 1
                probs_v(b, 1, NH - 1)
                for step in ("D_avT0", "D_avT1", "D_aT", "D_wo", "D_xn2T", "D_router"):
                    steps[step](b, 1)

            pe.wait_ge(sm["setup_dve"], 7)
            run_attention(pe, head, steps, order, tail, behind)

            pe.wait_ge(sm["oh_ready"], 1)
            flat = oh_bf[:, :, :].rearrange("p t e -> p (t e)")
            rank = bank[5][:, 0:NT * E].rearrange("p (t e) -> p t e", e=E)
            pe.matmul(bank[5][:, 0:NT * E], tri_bf[:, :], flat, start=True, stop=False, skip_group_check=True)
            for j in range(NT - 1):
                pe.matmul(rank[:, j + 1:NT, :], ones_bf[:, :],
                          oh_bf[:, j:j + 1, :].to_broadcast([P, NT - 1 - j, E]),
                          start=False, stop=(j == NT - 2), skip_group_check=True)
            for j in range(NT):
                last = pe.matmul(bank[6][:, 0:E], ones_bf[:, :], oh_bf[:, j, :],
                                 start=(j == 0), stop=(j == NT - 1))
            last.then_inc(sm["rank_ps"], 1)

            pe.wait_ge(sm["w_in"], 16 * (2 * (E - 2) + 3))

            def gate_up_of(kind, seq):
                if kind != "R":
                    return lambda k, r: wall[:, E, 2 * I * k + I * r:2 * I * k + I * r + I], \
                           lambda k: wall[:, E, KT * 2 * I + D * k:KT * 2 * I + D * k + D]
                e = pe.value_load(eid_i[0:1, ds(seq - R0, 1)], min_val=0, max_val=E - 1)
                flat_w = wall[:, :, :].rearrange("p e w -> p (e w)")
                return lambda k, r: flat_w[:, ds(e * WLEN + 2 * I * k + I * r, I)], \
                       lambda k: flat_w[:, ds(e * WLEN + KT * 2 * I + D * k, D)]

            def x_turn(seq, n, p):
                pe.wait_ge(sm[f"xl_in{p}"], 16 * (n + 1))
                for k in range(KT):
                    last = turn(bank[0][:, P * k:P * k + P], xl[:, p, P * k:P * k + P])
                last.then_inc(sm["xT_ps"], 1)

            def gate_and_up(seq, p, kind):
                w, _ = gate_up_of(kind, seq)
                pe.wait_ge(sm["xT_sb"], seq + 1)
                for r, sig in ((0, "g_ps"), (1, "u_ps")):
                    products(bank[1 + r][:, :], [(xT[:, p, P * k:P * k + P], w(k, r)) for k in range(KT)]
                             ).then_inc(sm[sig], 1)

            def front():
                x_turn(0, 0, 0)
                gate_and_up(0, 0, "A")
                x_turn(1, 0, 1)

            def body(seq, n, p, kinds):
                kind, then = kinds[0], kinds[1:2]
                pe.wait_ge(sm["h_sb"], seq + 1)
                for k in range(I // P):
                    last = turn(bank[3][:, P * k:P * k + P], hid[:, P * k:P * k + P])
                last.then_inc(sm["hT_ps"], 1)
                if then == "R" and kind == "A":
                    pe.wait_ge(sm["pos_ready"], 2)
                    pe.wait_ge(sm["w67_in"], 64)
                if then:
                    gate_and_up(seq + 1, 1 - p, then)
                if kinds[2:]:
                    x_turn(seq + 2, n + 1, p)
                _, w = gate_up_of(kind, seq)
                pe.wait_ge(sm["hT_sb"], seq + 1)
                if kind == "B" and not (isinstance(seq, int) and seq < B0 + 2):
                    pe.wait_ge(sm["z_ready"], 2 * (seq - B0) - 3)
                else:
                    if counted(seq - 1):
                        pe.wait_ge(sm["ys_sb"], seq - 1)
                products(y_bank[p][:, 0:D], [(hT[:, P * k:P * k + P], w(k)) for k in range(I // P)]
                         ).then_inc(sm["y_ps"], 1)

            run_ffn(pe, front, body)


def kernel(**inputs):
    import concourse.bacc as bacc
    from concourse.bass_utils import run_bass_kernel_spmd

    g = {k: np.asarray(v) for k, v in inputs.items()}
    f = np.float32

    def padded(a, rows):
        return np.concatenate([np.zeros((rows, a.shape[1]), f), a], 0)

    wq = np.zeros((D, 2 * D), f)
    wq[0:DQ, 0:D] = head_minor(g["L0_attn_w_up_q"].T)
    wq[0:DQ, D:2 * D] = head_minor(g["L0_attn_wq_r"].T)
    wkv = np.concatenate([padded(head_minor(g["L0_attn_w_up_k"].T), P - DKV),
                          padded(head_minor(g["L0_attn_wk_r"].T), P - DKV),
                          padded(g["L0_attn_w_up_v"].T, P - DKV)], 1)
    col = np.zeros((P, 12), f)
    bd = np.concatenate([g["L0_attn_b_down_q"], g["L0_attn_b_down_kv"]]).reshape(2, P)
    bq, bqr, bk, bkr = (head_minor(g[f"L0_attn_{n}"]).reshape(2, P) for n in ("b_up_q", "bq_r", "b_up_k", "bk_r"))
    for c, v in ((0, bd[0]), (1, bd[1]), (2, bq[0]), (4, bqr[0]), (5, bk[0]), (6, bkr[0]),
                 (8, bq[1]), (9, bqr[1]), (10, bk[1]), (11, bkr[1])):
        col[:, c] = v
    arrays = {
        "x": g["L0_attn_x"].reshape(B * S, D),
        "const": constants(),
        "w_down": np.concatenate([g["L0_attn_w_down_q"].T, g["L0_attn_w_down_kv"].T], 1),
        "w_q": wq, "w_kv": wkv,
        "w_out": g["L0_attn_wo"].T, "w_router": g["L0_ffn_router_w"].T,
        "bias_col": col,
        "bias_v": np.zeros(0), "bias_o": np.zeros(0),
        "gate_up": g["L0_ffn_gate_up_proj"].reshape(E * D, 2 * I),
        "down": g["L0_ffn_down_proj"].reshape(E * I, D),
        "sh_gate": g["L0_ffn_shared_gate_w"], "sh_up": g["L0_ffn_shared_up_w"],
        "sh_down": g["L0_ffn_shared_down_w"],
    }
    arrays["bias_v"] = g["L0_attn_b_up_v"].reshape(1, D)
    arrays["bias_o"] = g["L0_attn_bo"].reshape(1, D)
    nc = bacc.Bacc("TRN2", target_bir_lowering=False, num_devices=1)
    aps = []
    for n in list(arrays):
        arrays[n] = np.ascontiguousarray(arrays[n])
        aps.append(nc.dram_tensor(n, list(arrays[n].shape), F32, kind="ExternalInput").ap())
    out = nc.dram_tensor("out", [B * S, D], F32, kind="ExternalOutput").ap()
    program(nc, *aps, out)
    r = run_bass_kernel_spmd(nc, [arrays], core_ids=[0])
    return r.results[0]["out"].reshape(B, S, D)
```

```python
from contextlib import ExitStack

import numpy as np

import concourse.bass as bass
from concourse import mybir

F32 = mybir.dt.float32
BF16 = mybir.dt.bfloat16
I32 = mybir.dt.int32
ALU = mybir.AluOpType
ACT = mybir.ActivationFunctionType
AX = mybir.AxisListType
ds = bass.ds

P = 128
B, S, D = 8, 256, 256
NH, HD = 16, 16
DQ, DKV = 192, 64
E, I = 8, 512
NT = B * S // P
TB = S // P
KT = D // P
NR = NT + E - 1
HALF = NT // 2
EPS = 1e-5
SCALE = 1.0 / float(np.sqrt(HD))
NPART = 3
K_SLOTS = (0, 0, 0, 1, 1, 2)
Q_SLOTS = (0, 1, 2, 0, 1, 0)
NSLOT = len(K_SLOTS)
ROWS = NSLOT * HD
MROWS = ROWS + NPART
HT = P // HD
WLEN = KT * 2 * I + (I // P) * D

C_ID, C_TRI, C_COS, C_SIN = 0, 128, 256, 512
C_DESC, C_TILE, C_LE, C_NUM = 768, 776, 792, 856
C_END = C_NUM + NR


def head_minor(a):
    return np.moveaxis(a.reshape(*a.shape[:-1], -1, HT, HD), -1, -2).reshape(a.shape)


def constants():
    t = np.zeros((P, C_END), np.float32)
    t[:, C_ID:C_ID + P] = np.eye(P)
    t[:, C_TRI:C_TRI + P] = np.triu(np.ones((P, P)), 1)
    exps = np.arange(0, D, 2, dtype=np.float32)
    inside = exps < 10
    tn = np.zeros_like(exps)
    tn[inside] = np.float32(1.0) / (np.float32(10000.0) ** exps[inside] / np.float32(D))
    assert not tn[P // 2:].any()
    ang = np.outer(np.arange(S, dtype=np.float32), tn).astype(np.float32)
    cos, sin = np.cos(ang), np.sin(ang)
    for row, f in enumerate(head_minor(np.arange(P))):
        t[row, C_COS:C_COS + S] = cos[:, f // 2]
        t[row, C_SIN:C_SIN + S] = sin[:, f // 2] * (1 if f % 2 else -1)
    t[:, C_DESC:C_DESC + E] = E - np.arange(E)
    t[:, C_TILE:C_TILE + NT] = P * np.arange(NT)
    t[:, C_LE:C_LE + E * E] = (np.arange(E)[None, :] <= np.arange(E)[:, None]).reshape(-1)
    t[:, C_NUM:C_NUM + NR] = np.arange(NR)
    return t


def program(nc, x, const, w_down, w_q, w_kv, w_out, w_router, bias_col, bias_v, bias_o,
            gate_up, down, sh_gate, sh_up, sh_down, out):
    x_tok = nc.dram_tensor("x_tok", [NT * P, D], F32, kind="Internal").ap()
    x_exp = nc.dram_tensor("x_exp", [NR * P, D], F32, kind="Internal").ap()
    y_exp = nc.dram_tensor("y_exp", [NR * P, D], F32, kind="Internal").ap()
    with ExitStack() as ctx:
        def sb(name, shape, dt=F32):
            return ctx.enter_context(nc.sbuf_tensor(name, shape, dt))

        def sem(name):
            return ctx.enter_context(nc.semaphore(name))

        wall = sb("wall", [P, E + 1, WLEN])
        x_sb = sb("x_sb", [P, NT, D])
        cst = sb("cst", [P, C_END])
        wd_sb = sb("wd_sb", [P, KT, D])
        wq_sb = sb("wq_sb", [P, KT, 2 * D])
        wkv_sb = sb("wkv_sb", [P, 3 * D])
        wo_sb = sb("wo_sb", [P, KT, D])
        wr_sb = sb("wr_sb", [P, KT, E])
        bcol = sb("bcol", [P, 12])
        bv_sb = sb("bv_sb", [P, D])
        bo_sb = sb("bo_sb", [P, D])
        stacks = sb("stacks", [P, 2, 2, NH, S], BF16)
        pv = sb("pv", [P, 4096])
        probs = pv[:, 0:2048].rearrange("p (n c) -> p n c", n=4)
        v_aug = pv[:, 2048:4096].rearrange("p (b t h c) -> p b t h c", b=2, t=TB, h=NH)
        spare = wall[:, E - 1, :]
        qf = spare[:, 0:512].rearrange("p (m c) -> p m c", m=2)
        kf = spare[:, 512:1024].rearrange("p (m c) -> p m c", m=2)
        xn = spare[:, 1024:1536].rearrange("p (t c) -> p t c", t=TB)
        xnT = spare[:, 1536:2048].rearrange("p (k c) -> p k c", k=KT)
        ctT = spare[:, 2048:2560].rearrange("p (k c) -> p k c", k=KT)
        a_sb = spare[:, 2560:3072].rearrange("p (t c) -> p t c", t=TB)
        spare2 = wall[:, E - 2, :]
        o_sb = spare2[:, 0:1024].rearrange("p (g c) -> p g c", g=4)
        aT = spare2[:, 1024:1536].rearrange("p (k c) -> p k c", k=KT)
        y_sb = spare2[:, 1536:2048].rearrange("p (t c) -> p t c", t=TB)
        xn2 = spare2[:, 2048:2560].rearrange("p (t c) -> p t c", t=TB)
        xn2T = spare2[:, 2560:3072].rearrange("p (k c) -> p k c", k=KT)
        yr = {"q": sb("yr_q", [P, S]), "k": sb("yr_k", [P, S])}
        swp = {"q": sb("swp_q", [P, S]), "k": sb("swp_k", [P, S])}
        parts = {"q": sb("parts_q", [P, NPART, 2, S], BF16), "k": sb("parts_k", [P, NPART, 2, S], BF16)}
        full = {"q": qf, "k": kf}
        nmax = sb("nmax", [P, 2, TB, NH // 2])
        nres = sb("nres", [P, 2, TB, NH // 2])
        mparts = sb("mparts", [P, TB, NPART, NH // 2], BF16)
        mT = sb("mT", [NPART * NH // 2, S], BF16)
        idb = sb("idb", [P, P], BF16)
        rec = sb("rec", [P, NH])
        stats = {n: sb(f"stats_{n}", [P, TB, 6]) for n in ("in", "at", "ff")}
        mv = {n: sb(f"mv_{n}", [P, TB, 2]) for n in ("in", "at", "ff")}
        mv2 = sb("mv2", [P, NT, 2])
        var = {n: sb(f"var_{n}", [P, TB]) for n in ("in", "at", "ff")}
        rstd = {n: sb(f"rstd_{n}", [P, TB]) for n in ("in", "at")}
        rstd2 = sb("rstd2", [P, NT])
        neg_half = sb("neg_half", [P, 1])
        zero = sb("zero", [P, D])
        logits = sb("logits", [P, NT, E])
        onehot = sb("onehot", [P, NT, E])
        work_r = sb("work_r", [P, NT, E])
        oh_bf = sb("oh_bf", [P, NT, E], BF16)
        tri_bf = sb("tri_bf", [P, P], BF16)
        ones_bf = sb("ones_bf", [P, P], BF16)
        lmax = sb("lmax", [P, NT])
        score = sb("score", [P, NT])
        gain = sb("gain", [P, NT])
        cmp_t = sb("cmp_t", [P, E, NT])
        cnt = sb("cnt", [P, 4, E])
        cmp_e = sb("cmp_e", [P, NR, E])
        eid = sb("eid", [P, NR])
        eid_i = sb("eid_i", [P, NR], I32)
        pos = sb("pos", [P, NT])
        pos_i = sb("pos_i", [P, NT], I32)
        pos_cur = sb("pos_cur", [P, 2], I32)
        ffn = stacks[:, :, :, :, :].rearrange("p a b h c -> p (a b h c)").bitcast(F32)
        xl = ffn[:, 0:512].rearrange("p (n c) -> p n c", n=2)
        xT = ffn[:, 512:1024].rearrange("p (n c) -> p n c", n=2)
        sg = ffn[:, 1024:1536]
        hid = ffn[:, 1536:2048]
        hT = ffn[:, 2048:2560]
        ys = ffn[:, 2560:3072].rearrange("p (n c) -> p n c", n=2)
        z_sb = ffn[:, 3072:4096].rearrange("p (n g c) -> p n g c", n=2, g=2)
        mv_f = ffn[:, 4096:4104].rearrange("p (n g c) -> p n g c", n=2, g=2)
        rstd_f = ffn[:, 4104:4108].rearrange("p (n g) -> p n g", n=2)
        var_f = ffn[:, 4108:4112].rearrange("p (n g) -> p n g", n=2)
        stats_f = ffn[:, 4112:4136].rearrange("p (n g c) -> p n g c", n=2, g=2)
        y_first = ffn[:, 4608:4608 + HALF * D].rearrange("p (n c) -> p n c", n=HALF)
        xr = pv[:, :].rearrange("p (n c) -> p n c", n=NT)
        routed = xr

        bank = [ctx.enter_context(nc.psum_tensor(f"bank{i}", [P, 512], F32)) for i in range(8)]
        st_bank, sm_bank, av_bank, w0, w1, w2 = bank[0:2], bank[2:4], bank[4], bank[5], bank[6], bank[7]
        y_bank = bank[4], bank[6]

        def two(t):
            return t[:, :].rearrange("p (a c) -> p a c", a=2)

        names = """passed x0_in x_in attn_w attn_w2 const_in ones_rows
            xn_ready xnT_ps xnT_sb ct_ps ct_sb k0_ps q0_ps kr_sb qr_sb k_swap q_swap k_mul q_mul k_rot
            q_rot k0_done q0_done qk1_ps qk1_sb v_ps v_ready kh qh k_res q_res km qm kl ql stacked0 stacked1
            sm_ps sm_max m_parts mT_ps mT_sb m_rows0 m_rows1 st_ready exp_done av_done o_copied
            avT_ps rec_ready a_ready aT_ps aT_sb wo_ps y_ready yn_ready x1_ready mv2_kept xn2_ready xn2_out
            xn2T_ps xn2T_sb rt_ps logits_sb setup_pool setup_dve bias_sum id_ready
            in_stats in_aggr in_var in_rstd at_stats at_aggr at_var at_rstd
            ff_stats ff_aggr ff_var ff_rstd out_stats out_aggr out_var out_rstd
            w_in w67_in zeroed
            rt rt_exp oh_ready rank_ps pos_ready xr_ready scattered0
            xl_in0 xl_in1 xT_ps xT_sb g_ps u_ps sg_sb h_sb hT_ps hT_sb y_ps ys_sb y_out0 y_out1
            gathered0 gathered1 gathered2 gathered3 z_ready zn_ready fin_ready out_done0 out_done1""".split()
        sm = {n: sem(n) for n in names}

        def counted(value):
            return not isinstance(value, int) or value > 0

        block = ctx.enter_context(nc.Block())

        NLOAD = 4

        AHEAD = {"A": 2, "N": 1, "M0": 1, "M1": 0, "D": -1, "L": -2}

        PROLOGUE = ((0, "A_stats A_power A_norm M_ones A_xnT A_ct A_ones A_k0 A_kswap A_krot A_q0 A_qswap"),
                    (0, "A_qrot A_kadd A_qadd A_qk1 A_v"),
                    (1, "A_stats A_power A_norm"),
                    (0, "A_khigh A_kres A_qhigh A_qres N_v A_qmid A_kmid A_qlow A_klow A_stack N_stack"),
                    (1, "A_xnT A_ct A_k0 A_kswap A_krot A_q0 A_qswap A_qrot SM0 A_kadd A_qadd A_qk1 A_v"),
                    (0, "M0"),
                    (1, "A_khigh A_kres A_qhigh A_qres A_kmid A_qmid A_klow A_qlow A_stack"))

        def exists(b):
            return not isinstance(b, int) or 0 <= b < B

        def step_of(steps, name, b, par):
            ahead = AHEAD[name.split("_")[0]]
            if exists(b + ahead):
                steps[name](b + ahead, (par + ahead) % 2)

        def units(b, h):
            if not (isinstance(b, int) and b == 0):
                return ((1, h),)
            if h < 4:
                return (0, 2 * h + 8), (0, 2 * h + 9)
            return ((1, h - 4),) if h < 12 else ((1, 2 * h - 16), (1, 2 * h - 15))

        def run_slot(b, par, head, steps, order, behind):
            for h in range(NH):
                head(b, par, h)
                for ahead, u in units(b, h):
                    if exists(b + ahead):
                        steps["SM"](b + ahead, (par + ahead) % 2, u)
                for name in order.get(h, ()):
                    if not (name == "M1" and isinstance(b, int) and b == 0):
                        step_of(steps, name, b, par)
                if h == 4 and isinstance(b, int) and b == 0 and "M1" in steps:
                    steps["M1"](b, par)
                behind(b, par, h)

        def run_attention(eng, head, steps, order, behind=lambda *_: None):
            for n, names in PROLOGUE:
                for name in names.split():
                    if name[0:2] == "SM":
                        for u in range(NH // 2):
                            steps["SM"](0, 0, NH // 2 * int(name[2]) + u)
                    elif name in steps:
                        steps[name](n, n)
            for b in (0, 1):
                run_slot(b, b, head, steps, order, behind)
            with eng.Fori(1, B // 2 - 1) as i:
                for c in range(2):
                    run_slot(2 * i + c, c, head, steps, order, behind)
            for b in (B - 2, B - 1):
                run_slot(b, b % 2, head, steps, order, behind)

        def nothing(*_):
            return None

        LAST = NT + NR - 1
        R0, B0 = HALF, HALF + NR

        def rows_of(seq, kind):
            n = {"A": seq, "R": seq - R0, "B": seq + HALF - B0}[kind]
            return (x_exp if kind == "R" else x_tok)[ds(P * n, P), :]

        def run_ffn(eng, front, body, final=nothing, before_finals=nothing, between=None):
            kinds = "A" * HALF + "R" * NR + "B" * HALF

            def single(s):
                body(s, s // 2, s % 2, kinds[s:s + 3])

            between = between or {}
            front()
            for s in range(HALF):
                between.get(s, nothing)()
                single(s)
            for s in (R0, R0 + 1):
                single(s)
            with eng.Fori(1, (NR - 1) // 2 - 1) as i:
                for c in range(2):
                    body(2 * i + R0 + c, i + R0 // 2, c, "RRR")
            for s in (B0 - 3, B0 - 2, B0 - 1):
                single(s)
            before_finals()
            for c in range(2):
                single(B0 + c)
                final(c, 0, c)
            with eng.Fori(1, (HALF - 2) // 2) as i:
                for c in range(2):
                    body(2 * i + B0 + c, i + (B0 + c) // 2, (B0 + c) % 2, "BBB")
                    final(2 * i + c, i, c)
            single(LAST - 1)
            between.get(LAST, nothing)()
            single(LAST)
            for c in (HALF - 2, HALF - 1):
                final(c, c // 2, c % 2)

        @block.sync
        def _(sp):
            x_t = x.rearrange("(n p) d -> p n d", p=P)
            sp.dma_start(x_sb[:, 0:TB, :], x_t[:, 0:TB, :]).then_inc(sm["x0_in"], 16)
            sp.dma_start(cst[:, :], const).then_inc(sm["const_in"], 16)
            loads = ((wd_sb[:, :, :], w_down.rearrange("(k p) n -> p k n", p=P)),
                     (bcol[:, :], bias_col),
                     (wkv_sb[:, :], w_kv),
                     (wq_sb[:, :, :], w_q.rearrange("(k p) n -> p k n", p=P)),
                     (bv_sb[:, :], bias_v.partition_broadcast(P)[:, 0, :]),
                     (bo_sb[:, :], bias_o.partition_broadcast(P)[:, 0, :]),
                     (wo_sb[:, :, :], w_out.rearrange("(k p) n -> p k n", p=P)),
                     (wr_sb[:, :, :], w_router.rearrange("(k p) n -> p k n", p=P)))
            assert len(loads) == 2 * NLOAD
            for n, (dst, src) in enumerate(loads):
                sp.dma_start(dst, src).then_inc(sm["attn_w" if n < NLOAD else "attn_w2"], 16)
            sp.dma_start(x_sb[:, TB:NT, :], x_t[:, TB:NT, :]).then_inc(sm["x_in"], 16)

            def stack(m):
                def f(b, par):
                    before = NH * (b - 2) + 8 * (m + 1)
                    if counted(before):
                        sp.wait_ge(sm["st_ready"], before)
                        sp.sem_inc(sm["passed"], 1)
                    for side, key, slots, sems in ((1, "k", K_SLOTS, ("kh", "km", "kl")),
                                                   (0, "q", Q_SLOTS, ("qh", "qm", "ql"))):
                        for part in range(NPART):
                            sp.wait_ge(sm[sems[part]], b + 1)
                            for r, slot in enumerate(slots):
                                if slot == part:
                                    sp.dma_start(
                                        stacks[HD * r:HD * r + HD, par, side, 8 * m:8 * m + 8, :],
                                        parts[key][:, part, m, :],
                                    ).then_inc(sm[f"stacked{m}"], 16)
                return f

            def xn2_store(b, par):
                sp.wait_ge(sm["xn2_ready"], TB * (b + 1))
                sp.dma_start(x_tok[ds(S * b, S), :].rearrange("(t p) d -> p t d", p=P),
                             xn2[:, :, :]).then_inc(sm["xn2_out"], 16)

            def weights(e, sig="w_in"):
                one = wall[:, ds(e, 1), :].rearrange("p e w -> p (e w)")
                sp.dma_start(one[:, 0:KT * 2 * I].rearrange("p (k f) -> p k f", k=KT),
                             gate_up[ds(D * e, D), :].rearrange("(k p) f -> p k f", p=P)
                             ).then_inc(sm[sig], 16)
                sp.dma_start(one[:, KT * 2 * I:WLEN].rearrange("p (k n) -> p k n", n=D),
                             down[ds(I * e, I), :].rearrange("(k p) n -> p k n", p=P)
                             ).then_inc(sm[sig], 16)

            def head(b, par, h):
                if h == NH - 1 and isinstance(b, int) and b == 0:
                    sp.wait_ge(sm["setup_pool"], 1)
                    sp.dma_start(x_exp.rearrange("(n p) d -> p n d", p=P),
                                 zero[:, :].unsqueeze(1).to_broadcast([P, NR, D])).then_inc(sm["zeroed"], 16)
                if h == 3:
                    if isinstance(b, int) and b == B - 1:
                        g = wall[:, E, 0:KT * 2 * I].rearrange("p (k f) -> p k f", k=KT)
                        sp.dma_start(g[:, :, 0:I], sh_gate.rearrange("(k p) f -> p k f", p=P)
                                     ).then_inc(sm["w_in"], 16)
                        sp.dma_start(g[:, :, I:2 * I], sh_up.rearrange("(k p) f -> p k f", p=P)
                                     ).then_inc(sm["w_in"], 16)
                        sp.dma_start(wall[:, E, KT * 2 * I:WLEN].rearrange("p (k n) -> p k n", n=D),
                                     sh_down.rearrange("(k p) n -> p k n", p=P)).then_inc(sm["w_in"], 16)
                    elif not (isinstance(b, int) and b == 0):
                        weights(b - 1)

            steps = {"A_stack": stack(0), "N_stack": stack(1), "D_store": xn2_store, "SM": nothing}
            order = {0: ("N_stack",), 5: ("A_stack",), 12: ("D_store",)}

            run_attention(sp, head, steps, order)

            def last_store():
                xn2_store(B - 1, 1)
                sp.wait_ge(sm["rt_ps"], B)
                sp.wait_ge(sm["xn2_out"], 16 * B)
                for e in (E - 2, E - 1):
                    weights(e, "w67_in")

            sp.wait_ge(sm["st_ready"], NH * B)
            if counted(16 * (B // 2)):
                sp.wait_ge(sm["xn2_out"], 16 * (B // 2))

            def load(seq, n, p, kind):
                if counted(seq - 1):
                    sp.wait_ge(sm["xT_ps"], seq - 1)
                if kind == "R" and isinstance(seq, int) and seq == R0:
                    sp.wait_ge(sm["scattered0"], 16 * NT)
                sp.dma_start(xl[:, p, :], rows_of(seq, kind)).then_inc(sm[f"xl_in{p}"], 16)

            def front():
                load(0, 0, 0, "A")
                load(1, 0, 1, "A")

            def body(seq, n, p, kinds):
                if kinds[2:]:
                    load(seq + 2, n + 1, p, kinds[2])

            def store(c, p):
                sp.wait_ge(sm["fin_ready"], c + 1)
                sp.dma_start(out.rearrange("(g r) d -> r g d", g=2)[ds(P * c, P), :, :], z_sb[:, p, :, :]
                             ).then_inc(sm[f"out_done{p}"], 16)

            def final(c, n, p):
                if not (isinstance(c, int) and c < 2):
                    store(c - 2, p)

            run_ffn(sp, front, body, final, between={3: last_store})
            store(HALF - 2, 0)
            store(HALF - 1, 1)
            sp.wait_ge(sm["out_done0"], 16 * HALF // 2)
            sp.wait_ge(sm["out_done1"], 16 * HALF // 2)

        @block.gpsimd
        def _(pool):
            pool.memset(zero[:, :], 0.0).then_inc(sm["setup_pool"], 1)
            pool.memset(neg_half[:, :], -0.5).then_inc(sm["setup_pool"], 1)
            pool.wait_ge(sm["setup_pool"], 2)

            def power(name, count, out_ap, in_ap, n):
                if counted(count):
                    pool.wait_ge(sm[f"{name}_var"], count)
                pool.tensor_tensor(out_ap, in_ap, neg_half[:, 0:1].to_broadcast([P, n]), ALU.pow
                                   ).then_inc(sm[f"{name}_rstd"], 1)

            def rotate(k, b):
                pool.wait_ge(sm[f"{k}_swap"], b + 1)
                pool.tensor_tensor(yr[k][:, :], yr[k][:, :], cst[:, C_COS:C_COS + S],
                                   ALU.mult).then_inc(sm[f"{k}_mul"], 1)
                pool.tensor_tensor(swp[k][:, :], swp[k][:, :], cst[:, C_SIN:C_SIN + S],
                                   ALU.mult).then_inc(sm[f"{k}_mul"], 1)
                pool.wait_ge(sm[f"{k}_mul"], 2 * b + 2)
                pool.tensor_tensor(yr[k][:, :], yr[k][:, :], swp[k][:, :], ALU.add
                                   ).then_inc(sm[f"{k}_rot"], 1)

            def residual(k, b):
                pool.wait_ge(sm[f"{k}h"], b + 1)
                pool.tensor_tensor(full[k], full[k], parts[k][:, 0, :, :], ALU.subtract
                                   ).then_inc(sm[f"{k}_res"], 1)

            def low(k, b):
                pool.wait_ge(sm[f"{k}m"], b + 1)
                pool.tensor_tensor(parts[k][:, 2, :, :], full[k], parts[k][:, 1, :, :], ALU.subtract
                                   ).then_inc(sm[f"{k}l"], 1)

            def rows_of_ones(b, par):
                pool.wait_ge(sm["in_rstd"], 1)
                for p in range(2):
                    pool.memset(stacks[ROWS:MROWS, p, 1, :, :], 1.0).then_inc(sm["ones_rows"], 1)
                    pool.wait_ge(sm["ones_rows"], p + 1)

            def add_x(b, par):
                pool.wait_ge(sm["yn_ready"], TB * (b + 1))
                tile = x_sb[:, ds(TB * b, TB), :]
                pool.tensor_tensor(tile, tile, y_sb[:, :, :], ALU.add).then_inc(sm["x1_ready"], 1)

            steps = {
                "A_power": lambda b, par: power("in", b + 1, rstd["in"][:, :], var["in"][:, :], TB),
                "A_krot": lambda b, par: rotate("k", b), "A_qrot": lambda b, par: rotate("q", b),
                "A_kres": lambda b, par: residual("k", b), "A_qres": lambda b, par: residual("q", b),
                "A_klow": lambda b, par: low("k", b), "A_qlow": lambda b, par: low("q", b),
                "D_power": lambda b, par: power("at", b + 1, rstd["at"][:, :], var["at"][:, :], TB),
                "D_x1": add_x,
                "D_power2": lambda b, par: power("ff", b + 1, rstd2[:, ds(TB * b, TB)], var["ff"][:, :], TB),
                "M_ones": rows_of_ones, "SM": nothing}
            order = {0: ("A_power",), 4: ("A_krot",), 5: ("A_qrot",), 6: ("D_power",),
                     7: ("A_kres", "A_qres", "A_klow",), 8: ("A_qlow",), 10: ("D_x1",),
                     13: ("D_power2",)}

            run_attention(pool, nothing, steps, order)
            for name in ("D_power", "D_x1", "D_power2"):
                steps[name](B - 1, 1)

            pool.wait_ge(sm["pos_ready"], 1)
            pool.wait_ge(sm["zeroed"], 16)
            for j in range(NT):
                pool.wait_ge(sm["xr_ready"], j + 1)
                pool.indirect_dma_start(
                    out=x_exp, out_offset=bass.IndirectOffsetOnAxis(ap=pos_i[:, j:j + 1], axis=0),
                    in_=xr[:, j, :], in_offset=None).then_inc(sm["scattered0"], 16)

            def gather(c, name):
                for j in (HALF + c, c):
                    pool.indirect_dma_start(
                        out=routed[:, j, :], out_offset=None, in_=y_exp,
                        in_offset=bass.IndirectOffsetOnAxis(ap=pos_i[:, j:j + 1], axis=0)).then_inc(sm[name], 16)

            def before_finals():
                pool.wait_ge(sm["scattered0"], 16 * NT)
                pool.wait_ge(sm["y_out0"], 16 * ((NR + 1) // 2))
                pool.wait_ge(sm["y_out1"], 16 * (NR // 2))
                for c, name in ((0, "gathered0"), (1, "gathered1"), (2, "gathered2")):
                    gather(c, name)

            after_power = {0: (3,), 1: (5,)}
            after_sum = {0: (4,), 1: (6, 7)}
            assert HALF == 8

            x_two = x_sb[:, :, :].rearrange("p (g n) d -> p n g d", g=2)

            def final(c, n, p):
                power("out", c + 1, rstd_f[:, p, :], var_f[:, p, :], 2)
                if isinstance(c, int):
                    for rest in after_power.get(c, ()):
                        gather(rest, "gathered2")
                if isinstance(c, int) and c >= HALF - 2:
                    return
                plus_x(c, p)
                if isinstance(c, int):
                    for rest in after_sum.get(c, ()):
                        gather(rest, "gathered2" if rest < HALF - 2 else "gathered3")

            def plus_x(c, p):
                pool.wait_ge(sm["zn_ready"], 2 * c + 2)
                pool.tensor_tensor(z_sb[:, p, :, :], z_sb[:, p, :, :],
                                   x_two[:, ds(c, 1), :, :].rearrange("p a g d -> p (a g) d"), ALU.add
                                   ).then_inc(sm["fin_ready"], 1)

            run_ffn(pool, nothing, nothing, final, before_finals)
            for c in (HALF - 2, HALF - 1):
                plus_x(c, c % 2)

        @block.scalar
        def _(act):
            def xnT_copy(b, par):
                act.wait_ge(sm["xnT_ps"], b + 1)
                act.activation(xnT, two(w0), ACT.Copy).then_inc(sm["xnT_sb"], 1)

            def ct_copy(b, par):
                act.wait_ge(sm["ct_ps"], b + 1)
                if counted(b):
                    act.wait_ge(sm["v_ps"], b)
                for m in range(2):
                    act.activation(ctT[:, m, :], two(w1)[:, m, :], ACT.Identity, bias=bcol[:, m:m + 1]
                                   ).then_inc(sm["ct_sb"], 1)

            def rope_copy(k, bank_, col):
                def f(b, par):
                    act.wait_ge(sm[f"{k}0_ps"], b + 1)
                    if counted(b):
                        act.wait_ge(sm[f"{k}0_done"], b)
                    act.activation(yr[k][:, :], two(bank_)[:, 1, :], ACT.Identity,
                                   bias=bcol[:, col:col + 1]).then_inc(sm[f"{k}r_sb"], 1)
                return f

            def qk1_copy(b, par):
                if isinstance(b, int) and b == 0:
                    act.wait_ge(sm["bias_sum"], 1)
                act.wait_ge(sm["qk1_ps"], b + 1)
                if counted(b):
                    act.wait_ge(sm["kl"], b)
                if counted(b):
                    act.wait_ge(sm["ql"], b)
                act.activation(kf[:, 1, :], two(w0)[:, 1, :], ACT.Identity, bias=bcol[:, 7:8]
                               ).then_inc(sm["qk1_sb"], 1)
                act.activation(qf[:, 1, :], two(w0)[:, 0, :], ACT.Identity, bias=bcol[:, 3:4]
                               ).then_inc(sm["qk1_sb"], 1)

            def first_high(b, par):
                act.wait_ge(sm["qk1_sb"], 2 * b + 2)
                if counted(16 * 2 * NSLOT * b):
                    act.wait_ge(sm["stacked0"], 16 * 2 * NSLOT * b)
                if counted(16 * 2 * NSLOT * b):
                    act.wait_ge(sm["stacked1"], 16 * 2 * NSLOT * b)
                high("k", b)

            def high(k, b):
                act.wait_ge(sm[f"{k}0_done"], b + 1)
                act.activation(parts[k][:, 0, :, :], full[k], ACT.Copy).then_inc(sm[f"{k}h"], 1)

            def mid(k, b):
                act.wait_ge(sm[f"{k}_res"], b + 1)
                act.activation(parts[k][:, 1, :, :], full[k], ACT.Copy).then_inc(sm[f"{k}m"], 1)

            def mT_out(b, par, half):
                act.wait_ge(sm["mT_ps"], 2 * b + half + 1)
                if half:
                    act.wait_ge(sm["m_rows0"], 16 * (b + 1))
                else:
                    if counted(16 * b):
                        act.wait_ge(sm["m_rows1"], 16 * b)
                act.activation(mT[:, :], w2[:, 0:P].bitcast(BF16)[0:NPART * NH // 2, :], ACT.Copy
                               ).then_inc(sm["mT_sb"], 1)
                act.wait_ge(sm["mT_sb"], 2 * b + half + 1)
                act.dma_start(stacks[ROWS:MROWS, par, 0, 8 * half:8 * half + 8, :],
                              mT[:, :]).then_inc(sm[f"m_rows{half}"], 16)

            def o_copy(b, half):
                act.wait_ge(sm["av_done"], NH * b + 8 * half + 8)
                if counted(2 * b):
                    act.wait_ge(sm["avT_ps"], 2 * b)
                act.activation(o_sb[:, 2 * half:2 * half + 2, :], two(av_bank), ACT.Copy
                               ).then_inc(sm["o_copied"], 1)

            def head(b, par, h):
                act.wait_ge(sm["st_ready"], NH * b + h + 1)
                if counted(NH * b + h - 3):
                    act.wait_ge(sm["av_done"], NH * b + h - 3)
                act.activation(probs[:, h % 4, :], st_bank[h % 2][:, :], ACT.Exp, scale=SCALE
                               ).then_inc(sm["exp_done"], 1)

            def aT_copy(b, par):
                act.wait_ge(sm["aT_ps"], b + 1)
                if counted(b):
                    act.wait_ge(sm["wo_ps"], b)
                act.activation(aT[:, :, :], two(w2), ACT.Copy).then_inc(sm["aT_sb"], 1)

            def xn2T_copy(b, par):
                act.wait_ge(sm["xn2T_ps"], b + 1)
                if counted(b):
                    act.wait_ge(sm["rt_ps"], b)
                act.activation(xn2T[:, :, :], two(w2), ACT.Copy).then_inc(sm["xn2T_sb"], 1)

            steps = {
                "A_xnT": xnT_copy, "A_ct": ct_copy, "A_k0": rope_copy("k", w0, 6), "A_q0": rope_copy("q", w1, 4),
                "A_qk1": qk1_copy, "A_khigh": first_high, "A_qhigh": lambda b, par: high("q", b),
                "A_kmid": lambda b, par: mid("k", b), "A_qmid": lambda b, par: mid("q", b),
                "M0": lambda b, par: mT_out(b, par, 0), "M1": lambda b, par: mT_out(b, par, 1),
                "M1_o0": lambda b, par: o_copy(b, 0), "D_o1": lambda b, par: o_copy(b, 1),
                "D_aT": aT_copy, "D_xn2T": xn2T_copy, "SM": nothing}
            order = {0: ("D_o1",), 1: ("M1",), 2: ("A_xnT",), 3: ("A_ct",),
                     4: ("D_aT", "A_k0", "A_q0",), 7: ("A_qk1", "A_khigh", "A_qhigh",),
                     8: ("A_kmid", "M1_o0", "A_qmid",), 12: ("M0",), 15: ("D_xn2T",)}

            run_attention(act, head, steps, order)
            steps["D_o1"](B - 1, 1)

            def last_xn2T():
                steps["D_xn2T"](B - 1, 1)
                act.wait_ge(sm["rt"], 1)
                act.activation(score[:, :], lmax[:, :], ACT.Exp, scale=-1.0).then_inc(sm["rt_exp"], 1)

            def xT_copy(seq, p):
                act.wait_ge(sm["xT_ps"], seq + 1)
                act.activation(xT[:, p, :], bank[0][:, 0:KT * P], ACT.Copy).then_inc(sm["xT_sb"], 1)

            def silu(seq):
                act.wait_ge(sm["g_ps"], seq + 1)
                act.activation(sg, bank[1][:, :], ACT.Silu).then_inc(sm["sg_sb"], 1)

            def front():
                xT_copy(0, 0)
                silu(0)
                xT_copy(1, 1)

            def body(seq, n, p, kinds):
                kind = kinds[0]
                if kinds[1:]:
                    silu(seq + 1)
                if kinds[2:]:
                    xT_copy(seq + 2, p)
                if kind == "B":
                    return
                act.wait_ge(sm["y_ps"], seq + 1)
                if kind == "A":
                    act.activation(y_first[:, ds(seq, 1), :].rearrange("p a c -> p (a c)"), y_bank[p][:, 0:D],
                                   ACT.Copy).then_inc(sm["ys_sb"], 1)
                    return
                if not (isinstance(seq, int) and seq < R0 + 2):
                    if counted(16 * (n - R0 // 2)):
                        act.wait_ge(sm[f"y_out{p}"], 16 * (n - R0 // 2))
                act.activation(ys[:, p, :], y_bank[p][:, 0:D], ACT.Copy).then_inc(sm["ys_sb"], 1)
                act.wait_ge(sm["ys_sb"], seq + 1)
                act.dma_start(y_exp[ds(P * (seq - R0), P), :], ys[:, p, :]).then_inc(sm[f"y_out{p}"], 16)

            run_ffn(act, front, body, between={0: lambda: steps["D_aT"](B - 1, 1), 2: last_xn2T})

        @block.vector
        def _(dve):
            def ones_and_sums(b, par):
                dve.wait_ge(sm["attn_w"], 16 * NLOAD)
                dve.tensor_tensor(wq_sb[:, :, P:2 * P], wq_sb[:, :, P:2 * P], wq_sb[:, :, D + P:D + 2 * P], ALU.add)
                dve.tensor_tensor(wkv_sb[:, P:2 * P], wkv_sb[:, P:2 * P], wkv_sb[:, D + P:D + 2 * P], ALU.add)
                dve.tensor_tensor(bcol[:, 3:4], bcol[:, 8:9], bcol[:, 9:10], ALU.add)
                dve.tensor_tensor(bcol[:, 7:8], bcol[:, 10:11], bcol[:, 11:12], ALU.add
                                  ).then_inc(sm["bias_sum"], 1)
                for p in range(2):
                    dve.memset(v_aug[:, p, :, :, HD:2 * HD], 1.0).then_inc(sm["setup_dve"], 1)
                dve.memset(ones_bf[:, :], 1.0).then_inc(sm["setup_dve"], 1)
                dve.wait_ge(sm["const_in"], 16)
                dve.tensor_copy(idb[:, :], cst[:, C_ID:C_ID + P]).then_inc(sm["setup_dve"], 1)
                dve.tensor_copy(tri_bf[:, :], cst[:, C_TRI:C_TRI + P]).then_inc(sm["setup_dve"], 1)

            def ln_head(name, b, tiles, stat, mean_var, var_ap, n):
                for t in range(n):
                    dve.bn_stats(stat[:, t, :], tiles(t)).then_inc(sm[f"{name}_stats"], 1)
                dve.wait_ge(sm[f"{name}_stats"], n * (b + 1))
                dve.sem_inc(sm["passed"], 1)
                for t in range(n):
                    dve.bn_aggr(mean_var(t), stat[:, t, :]).then_inc(sm[f"{name}_aggr"], 1)
                dve.wait_ge(sm[f"{name}_aggr"], n * (b + 1))

            def a_stats(b, par):
                if isinstance(b, int) and b <= 1:
                    dve.wait_ge(sm["x0_in" if b == 0 else "x_in"], 16)
                tiles = lambda t: x_sb[:, ds(TB * b + t, 1), :].rearrange("p a c -> p (a c)")
                ln_head("in", b, tiles, stats["in"], lambda t: mv["in"][:, t, :], var["in"], TB)
                dve.tensor_scalar(var["in"][:, :], mv["in"][:, :, 1], EPS, None, ALU.add
                                  ).then_inc(sm["in_var"], 1)

            def a_norm(b, par):
                tiles = lambda t: x_sb[:, ds(TB * b + t, 1), :].rearrange("p a c -> p (a c)")
                dve.wait_ge(sm["in_rstd"], b + 1)
                if counted(b):
                    dve.wait_ge(sm["xnT_ps"], b)
                for t in range(TB):
                    dve.tensor_scalar(xn[:, t, :], tiles(t), mv["in"][:, t, 0:1], rstd["in"][:, t:t + 1],
                                      ALU.subtract, ALU.mult).then_inc(sm["xn_ready"], 1)

            SWAP = [i ^ HT for i in range(32)]

            def swap(k, col, bank_):
                def f(b, par):
                    dve.wait_ge(sm[f"{k}r_sb"], b + 1)
                    dve.sem_inc(sm["passed"], 1)
                    dve.stream_shuffle(swp[k][:, :], yr[k][:, :], SWAP).then_inc(sm[f"{k}_swap"], 1)
                return f

            def add0(k, col, bank_):
                def f(b, par):
                    dve.wait_ge(sm[f"{k}_rot"], b + 1)
                    if counted(b):
                        dve.wait_ge(sm[f"{k}l"], b)
                    dve.scalar_tensor_tensor(full[k][:, 0, :], two(bank_)[:, 0, :], bcol[:, col:col + 1],
                                             yr[k][:, :], ALU.add, ALU.add).then_inc(sm[f"{k}0_done"], 1)
                return f

            k_swap, q_swap = swap("k", 5, w0), swap("q", 2, w1)
            k_add, q_add = add0("k", 5, w0), add0("q", 2, w1)

            def v_add(b, par):
                if isinstance(b, int) and b == 0:
                    dve.wait_ge(sm["attn_w2"], 16 * NLOAD)
                dve.wait_ge(sm["v_ps"], b + 1)
                if counted(NH * (b - 1)):
                    dve.wait_ge(sm["av_done"], NH * (b - 1))
                dve.tensor_tensor(v_aug[:, par, :, :, 0:HD],
                                  two(w1).rearrange("p t (h d) -> p t h d", d=HD),
                                  bv_sb[:, :].rearrange("p (h d) -> p h d", d=HD).unsqueeze(1)
                                  .to_broadcast([P, TB, NH, HD]), ALU.add).then_inc(sm["v_ready"], 1)

            def sm_max(b, par, u):
                half, qt, pair = u // 8, (u // 4) % 2, u % 4
                dve.wait_ge(sm["sm_ps"], NH * b + u + 1)
                dve.tensor_reduce(nmax[:, half, qt, 2 * pair:2 * pair + 2], two(sm_bank[u % 2]), AX.X,
                                  ALU.max, negate=True).then_inc(sm["sm_max"], 1)

            def m_split(b, par, half):
                n = 8 * b + 4 * half
                dve.wait_ge(sm["sm_max"], NH * b + 8 * (half + 1))
                if counted(2 * b + half):
                    dve.wait_ge(sm["mT_ps"], 2 * b + half)
                src, res = nmax[:, half, :, :], nres[:, half, :, :]
                dve.tensor_copy(mparts[:, :, 0, :], src).then_inc(sm["m_parts"], 1)
                dve.wait_ge(sm["m_parts"], n + 1)
                dve.tensor_tensor(res, src, mparts[:, :, 0, :], ALU.subtract).then_inc(sm["m_parts"], 1)
                dve.wait_ge(sm["m_parts"], n + 2)
                dve.tensor_copy(mparts[:, :, 1, :], res).then_inc(sm["m_parts"], 1)
                dve.wait_ge(sm["m_parts"], n + 3)
                dve.tensor_tensor(mparts[:, :, 2, :], res, mparts[:, :, 1, :], ALU.subtract
                                  ).then_inc(sm["m_parts"], 1)

            def divide(t):
                def f(b, par):
                    dve.wait_ge(sm["avT_ps"], 2 * b + t + 1)
                    o = w2[:, :].rearrange("p (h c) -> p h c", c=2 * HD)
                    dve.reciprocal(rec[:, :], o[:, :, HD]).then_inc(sm["rec_ready"], 1)
                    dve.wait_ge(sm["rec_ready"], 2 * b + t + 1)
                    if counted(b):
                        dve.wait_ge(sm["aT_ps"], b)
                    dve.tensor_tensor(a_sb[:, t, :].rearrange("p (h c) -> p h c", c=HD), o[:, :, 0:HD],
                                      rec[:, :].unsqueeze(2).to_broadcast([P, NH, HD]), ALU.mult
                                      ).then_inc(sm["a_ready"], 1)
                return f

            def d_wo(b, par):
                dve.wait_ge(sm["wo_ps"], b + 1)
                if counted(b):
                    dve.wait_ge(sm["x1_ready"], b)
                dve.tensor_tensor(y_sb[:, :, :], two(w2), bo_sb[:, :].unsqueeze(1).to_broadcast([P, TB, D]),
                                  ALU.add).then_inc(sm["y_ready"], 1)
                dve.wait_ge(sm["y_ready"], b + 1)
                ln_head("at", b, lambda t: y_sb[:, t, :], stats["at"], lambda t: mv["at"][:, t, :], None, TB)
                dve.tensor_scalar(var["at"][:, :], mv["at"][:, :, 1], EPS, None, ALU.add
                                  ).then_inc(sm["at_var"], 1)

            def d_yn(b, par):
                dve.wait_ge(sm["at_rstd"], b + 1)
                for t in range(TB):
                    dve.tensor_scalar(y_sb[:, t, :], y_sb[:, t, :], mv["at"][:, t, 0:1],
                                      rstd["at"][:, t:t + 1], ALU.subtract, ALU.mult
                                      ).then_inc(sm["yn_ready"], 1)

            def d_stats(b, par):
                dve.wait_ge(sm["x1_ready"], b + 1)
                tiles = lambda t: x_sb[:, ds(TB * b + t, 1), :].rearrange("p a c -> p (a c)")
                ln_head("ff", b, tiles, stats["ff"], lambda t: mv["ff"][:, t, :], None, TB)
                dve.tensor_copy(mv2[:, ds(TB * b, TB), :], mv["ff"][:, :, :]).then_inc(sm["mv2_kept"], 1)
                dve.tensor_scalar(var["ff"][:, :], mv["ff"][:, :, 1], EPS, None, ALU.add
                                  ).then_inc(sm["ff_var"], 1)

            def d_xn2(b, par):
                tiles = lambda t: x_sb[:, ds(TB * b + t, 1), :].rearrange("p a c -> p (a c)")
                dve.wait_ge(sm["ff_rstd"], b + 1)
                if counted(b):
                    dve.wait_ge(sm["xn2T_ps"], b)
                if counted(16 * b):
                    dve.wait_ge(sm["xn2_out"], 16 * b)
                for t in range(TB):
                    dve.tensor_scalar(xn2[:, t, :], tiles(t), mv["ff"][:, t, 0:1],
                                      rstd2[:, ds(TB * b + t, 1)], ALU.subtract, ALU.mult
                                      ).then_inc(sm["xn2_ready"], 1)

            def d_router(b, par):
                dve.wait_ge(sm["rt_ps"], b + 1)
                dve.tensor_copy(logits[:, ds(TB * b, TB), :],
                                w2[:, 0:TB * E].rearrange("p (t e) -> p t e", e=E)).then_inc(sm["logits_sb"], 1)

            steps = {
                "A_ones": ones_and_sums, "A_stats": a_stats, "A_norm": a_norm, "A_kswap": k_swap, "A_kadd": k_add, "A_qswap": q_swap,
                "A_qadd": q_add, "N_v": v_add, "SM": sm_max,
                "M0": lambda b, par: m_split(b, par, 0), "M1": lambda b, par: m_split(b, par, 1),
                "D_div0": divide(0), "D_div1": divide(1), "D_y": d_wo, "D_yn": d_yn, "D_stats": d_stats,
                "D_xn2": d_xn2, "L_router": d_router}
            order = {0: ("M1", "L_router", "A_stats",), 1: ("N_v", "A_norm",),
                     2: ("D_div0", "D_div1",), 5: ("A_kswap", "A_qswap", "A_kadd", "D_y",),
                     7: ("A_qadd",), 8: ("D_yn",), 11: ("M0",), 12: ("D_stats",), 13: ("D_xn2",)}

            run_attention(dve, nothing, steps, order)
            for name, b in (("L_router", B - 2), ("D_div0", B - 1)):
                steps[name](b, b % 2)

            def last_steps(*names):
                return lambda: [steps[name](B - 1, 1) for name in names]

            done = [0]

            def chain(ins):
                done[0] += 1
                ins.then_inc(sm["rt"], 1)
                if counted(done[0]):
                    dve.wait_ge(sm["rt"], done[0])

            def spread(ap, n):
                return ap.unsqueeze(2).to_broadcast([P, NT, n])

            def one_hots():
                steps["L_router"](B - 1, 1)
                dve.wait_ge(sm["logits_sb"], B)
                chain(dve.tensor_reduce(lmax[:, :], logits[:, :, :], AX.X, ALU.max))
                chain(dve.tensor_tensor(work_r[:, :, :], logits[:, :, :], spread(lmax[:, :], E), ALU.is_equal))
                desc = cst[:, C_DESC:C_DESC + E].unsqueeze(1).to_broadcast([P, NT, E])
                chain(dve.tensor_tensor(work_r[:, :, :], work_r[:, :, :], desc, ALU.mult))
                chain(dve.tensor_reduce(pos[:, :], work_r[:, :, :], AX.X, ALU.max))
                chain(dve.tensor_tensor(onehot[:, :, :], work_r[:, :, :], spread(pos[:, :], E), ALU.is_equal))
                dve.tensor_copy(oh_bf[:, :, :], onehot[:, :, :]).then_inc(sm["oh_ready"], 1)
                dve.wait_ge(sm["rt_exp"], 1)
                chain(dve.tensor_scalar(score[:, :], score[:, :], 1.0, None, ALU.add))
                chain(dve.reciprocal(score[:, :], score[:, :]))
                chain(dve.tensor_tensor(gain[:, :], score[:, :], rstd2[:, :], ALU.mult))
            def token_rows():
                dve.wait_ge(sm["rank_ps"], 1)
                chain(dve.tensor_copy(cnt[:, 0, :], bank[5][:, NT * E:NT * E + E]))
                chain(dve.tensor_tensor(cmp_t[:, :, :], cnt[:, 0, :].unsqueeze(2).to_broadcast([P, E, NT]),
                                        cst[:, C_TILE:C_TILE + NT].unsqueeze(1).to_broadcast([P, E, NT]), ALU.is_gt))
                chain(dve.tensor_reduce(cnt[:, 1, :], cmp_t[:, :, :], AX.X, ALU.add))
                le = cst[:, C_LE:C_LE + E * E].rearrange("p (a b) -> p a b", a=E)
                chain(dve.tensor_tensor(cmp_t[:, :, 0:E], le, cnt[:, 1, :].unsqueeze(1).to_broadcast([P, E, E]),
                                        ALU.mult))
                chain(dve.tensor_reduce(cnt[:, 2, :], cmp_t[:, :, 0:E], AX.X, ALU.add))
                chain(dve.tensor_tensor(cnt[:, 3, :], cnt[:, 2, :], cnt[:, 1, :], ALU.subtract))
                chain(dve.tensor_scalar(cnt[:, 3, :], cnt[:, 3, :], float(P), None, ALU.mult))
                chain(dve.tensor_tensor(work_r[:, :, :], bank[5][:, 0:NT * E].rearrange("p (t e) -> p t e", e=E),
                                        cnt[:, 3, :].unsqueeze(1).to_broadcast([P, NT, E]), ALU.add))
                chain(dve.tensor_tensor(work_r[:, :, :], work_r[:, :, :], onehot[:, :, :], ALU.mult))
                chain(dve.tensor_reduce(pos[:, :], work_r[:, :, :], AX.X, ALU.add))
                dve.tensor_copy(pos_i[:, :], pos[:, :]).then_inc(sm["pos_ready"], 1)

            def scaled(*rows):
                dve.wait_ge(sm["mv2_kept"], B)
                for j in range(*rows):
                    dve.tensor_scalar(xr[:, j, :], x_sb[:, j, :], mv2[:, j, 0:1], gain[:, j:j + 1],
                                      ALU.subtract, ALU.mult).then_inc(sm["xr_ready"], 1)

            def tile_experts():
                chain(dve.tensor_tensor(cmp_e[:, :, :], cnt[:, 2, :].unsqueeze(1).to_broadcast([P, NR, E]),
                                        cst[:, C_NUM:C_NUM + NR].unsqueeze(2).to_broadcast([P, NR, E]), ALU.is_le))
                chain(dve.tensor_reduce(eid[:, :], cmp_e[:, :, :], AX.X, ALU.add))
                chain(dve.tensor_scalar(eid[:, :], eid[:, :], float(E - 1), None, ALU.min))
                dve.tensor_copy(eid_i[:, :], eid[:, :]).then_inc(sm["pos_ready"], 1)

            def rows_and_scaled():
                token_rows()
                scaled(0, 4)

            def experts_and_scaled():
                scaled(4, 10)
                tile_experts()

            def hidden(seq):
                dve.wait_ge(sm["sg_sb"], seq + 1)
                dve.wait_ge(sm["u_ps"], seq + 1)
                dve.tensor_tensor(hid, sg, bank[2][:, :], ALU.mult).then_inc(sm["h_sb"], 1)

            def front():
                hidden(0)

            def body(seq, n, p, kinds):
                dve.wait_ge(sm["hT_ps"], seq + 1)
                dve.tensor_copy(hT, bank[3][:, :]).then_inc(sm["hT_sb"], 1)
                if isinstance(seq, int) and seq == 1:
                    last_steps("D_stats", "D_xn2")()
                if kinds[1:]:
                    hidden(seq + 1)

            def normalise(c, p):
                dve.wait_ge(sm["out_rstd"], c + 1)
                for g in range(2):
                    dve.tensor_scalar(z_sb[:, p, g, :], z_sb[:, p, g, :], mv_f[:, p, g, 0:1],
                                      rstd_f[:, p, g:g + 1], ALU.subtract, ALU.mult
                                      ).then_inc(sm["zn_ready"], 1)

            def final(c, n, p):
                if not (isinstance(c, int) and c in (0, HALF - 2, HALF - 1)):
                    normalise(c - 1, 1 - p)
                dve.wait_ge(sm["y_ps"], c + B0 + 1)
                if isinstance(c, int) and c < 2:
                    dve.wait_ge(sm[f"gathered{c}"], 32)
                else:
                    if isinstance(c, int) and c >= HALF - 2:
                        dve.wait_ge(sm["gathered3"], 32 * 2)
                    else:
                        dve.wait_ge(sm["gathered2"], 32 * (HALF - 4))
                    dve.wait_ge(sm[f"out_done{p}"], 16 * n)
                for g, y in ((1, y_bank[(B0 + p) % 2][:, 0:D]),
                             (0, y_first[:, ds(c, 1), :].rearrange("p a d -> p (a d)"))):
                    dve.tensor_tensor(z_sb[:, p, g, :], y,
                                      routed[:, ds(c + HALF * g, 1), :].rearrange("p a d -> p (a d)"), ALU.add
                                      ).then_inc(sm["z_ready"], 1)
                dve.wait_ge(sm["z_ready"], 2 * c + 2)
                dve.sem_inc(sm["passed"], 1)
                for g in range(2):
                    dve.bn_stats(stats_f[:, p, g, :], z_sb[:, p, g, :]).then_inc(sm["out_stats"], 1)
                dve.wait_ge(sm["out_stats"], 2 * c + 2)
                dve.sem_inc(sm["passed"], 1)
                for g in range(2):
                    dve.bn_aggr(mv_f[:, p, g, :], stats_f[:, p, g, :]).then_inc(sm["out_aggr"], 1)
                dve.wait_ge(sm["out_aggr"], 2 * c + 2)
                dve.tensor_scalar(var_f[:, p, :], mv_f[:, p, :, 1], EPS, None, ALU.add
                                  ).then_inc(sm["out_var"], 1)

            between = {0: last_steps("D_div1"), 1: last_steps("D_y", "D_yn"), 2: one_hots,
                       3: rows_and_scaled, 4: experts_and_scaled, 5: lambda: scaled(10, NT),
                       LAST: lambda: normalise(HALF - 3, 1)}
            run_ffn(dve, front, body, final, between=between)
            normalise(HALF - 2, 0)
            normalise(HALF - 1, 1)

        @block.tensor
        def _(pe):
            ident = cst[:, C_ID:C_ID + P]

            def products(out_ap, pairs):
                for n, (lhsT, rhs) in enumerate(pairs):
                    last = pe.matmul(out_ap, lhsT, rhs, start=(n == 0), stop=(n == len(pairs) - 1))
                return last

            def turn(out_ap, in_ap):
                return pe.transpose(out_ap, in_ap, ident)

            def a_xnT(b, par):
                if isinstance(b, int) and b == 0:
                    pe.wait_ge(sm["const_in"], 16)
                pe.wait_ge(sm["xn_ready"], TB * (b + 1))
                if counted(2 * b):
                    pe.wait_ge(sm["qk1_sb"], 2 * b)
                for k in range(KT):
                    for t in range(TB):
                        last = turn(two(w0)[:, k, P * t:P * t + P], xn[:, t, P * k:P * k + P])
                last.then_inc(sm["xnT_ps"], 1)

            def a_ct(b, par):
                if isinstance(b, int) and b == 0:
                    pe.wait_ge(sm["attn_w"], 16 * NLOAD)
                pe.wait_ge(sm["xnT_sb"], b + 1)
                if counted(b):
                    pe.wait_ge(sm["v_ready"], b)
                for m in range(2):
                    last = products(two(w1)[:, m, :], [(wd_sb[:, k, P * m:P * m + P], xnT[:, k, :])
                                                       for k in range(KT)])
                last.then_inc(sm["ct_ps"], 1)

            def a_k0(b, par):
                pe.wait_ge(sm["ct_sb"], 2 * b + 2)
                for r in range(2):
                    last = products(two(w0)[:, r, :], [(wkv_sb[:, D * r:D * r + P], ctT[:, 1, :])])
                last.then_inc(sm["k0_ps"], 1)

            def a_q0(b, par):
                for r in range(2):
                    last = products(two(w1)[:, r, :], [(wq_sb[:, k, D * r:D * r + P], ctT[:, k, :])
                                                       for k in range(KT)])
                last.then_inc(sm["q0_ps"], 1)

            def a_qk1(b, par):
                if isinstance(b, int) and b == 0:
                    pe.wait_ge(sm["bias_sum"], 1)
                pe.wait_ge(sm["kr_sb"], b + 1)
                pe.wait_ge(sm["k0_done"], b + 1)
                products(two(w0)[:, 0, :], [(wq_sb[:, k, P:2 * P], ctT[:, k, :]) for k in range(KT)])
                products(two(w0)[:, 1, :], [(wkv_sb[:, P:2 * P], ctT[:, 1, :])]).then_inc(sm["qk1_ps"], 1)

            def a_v(b, par):
                pe.wait_ge(sm["qr_sb"], b + 1)
                pe.wait_ge(sm["q0_done"], b + 1)
                for t in range(TB):
                    last = products(two(w1)[:, t, :], [(ctT[:, 1, P * t:P * t + P], wkv_sb[:, 2 * D:3 * D])])
                last.then_inc(sm["v_ps"], 1)

            def sm_scores(b, par, u):
                half, qt, pair = u // 8, (u // 4) % 2, u % 4
                if u % 8 == 0:
                    pe.wait_ge(sm[f"stacked{half}"], 16 * 2 * NSLOT * (b + 1))
                if counted(NH * b + u - 1):
                    pe.wait_ge(sm["sm_max"], NH * b + u - 1)
                for c in range(2):
                    h = 8 * half + 2 * pair + c
                    last = pe.matmul(two(sm_bank[u % 2])[:, c, :],
                                     stacks[0:ROWS, par, 0, h, P * qt:P * qt + P],
                                     stacks[0:ROWS, par, 1, h, :], start=True, stop=True)
                last.then_inc(sm["sm_ps"], 1)

            def m_turn(b, par, half):
                if isinstance(b, int) and b == 0 and half == 0:
                    pe.wait_ge(sm["setup_dve"], 5)
                pe.wait_ge(sm["m_parts"], 8 * b + 4 * half + 4)
                if half:
                    pe.wait_ge(sm["mT_sb"], 2 * b + 1)
                    if counted(b - 1):
                        pe.wait_ge(sm["logits_sb"], b - 1)
                else:
                    if counted(b - 1):
                        pe.wait_ge(sm["y_ready"], b - 1)
                    if counted(2 * b):
                        pe.wait_ge(sm["mT_sb"], 2 * b)
                for t in range(TB):
                    last = pe.transpose(w2[:, 0:P].bitcast(BF16)[0:NPART * NH // 2, P * t:P * t + P],
                                        mparts[:, t, :, :].rearrange("p a h -> p (a h)"), idb[:, :])
                last.then_inc(sm["mT_ps"], 1)

            def probs_v(b, par, h):
                pe.wait_ge(sm["exp_done"], NH * b + h + 1)
                if h % 8 == 0:
                    if counted(2 * b + h // 8):
                        pe.wait_ge(sm["o_copied"], 2 * b + h // 8)
                if h == 0:
                    pe.wait_ge(sm["v_ready"], b + 1)
                c = h % 4
                for k in range(TB):
                    last = pe.matmul(two(av_bank)[32 * c:32 * c + 32, (h % 8) // 4, :],
                                     v_aug[:, par, k, h, :], probs[:, h % 4, S * k:S * k + S],
                                     start=(k == 0), stop=(k == TB - 1))
                last.then_inc(sm["av_done"], 1)

            def head(b, par, h):
                if h == 0 and isinstance(b, int) and b < 2:
                    pe.wait_ge(sm["ones_rows"], b + 1)
                if h == 0:
                    pe.wait_ge(sm["m_rows0"], 16 * (b + 1))
                if h == 8:
                    pe.wait_ge(sm["m_rows1"], 16 * (b + 1))
                if counted(NH * b + h - 1):
                    pe.wait_ge(sm["exp_done"], NH * b + h - 1)
                for k in range(TB):
                    last = pe.matmul(two(st_bank[h % 2])[:, k, :],
                                     stacks[0:MROWS, par, 1, h, P * k:P * k + P],
                                     stacks[0:MROWS, par, 0, h, :], start=True, stop=True)
                last.then_inc(sm["st_ready"], 1)

            def behind(b, par, h):
                if h > 0:
                    probs_v(b, par, h - 1)
                elif exists(b - 1):
                    probs_v(b - 1, 1 - par, NH - 1)

            def av_turn(t):
                def f(b, par):
                    if t == 0:
                        pe.wait_ge(sm["o_copied"], 2 * b + 2)
                        if isinstance(b, int) and b == B - 1:
                            if counted(b):
                                pe.wait_ge(sm["logits_sb"], b)
                        else:
                            pe.wait_ge(sm["mT_sb"], 2 * b + 4)
                    else:
                        pe.wait_ge(sm["a_ready"], 2 * b + 1)
                    for g in range(4):
                        last = turn(w2[:, P * g:P * g + P], o_sb[:, g, P * t:P * t + P])
                    last.then_inc(sm["avT_ps"], 1)
                return f

            def a_turn(b, par):
                pe.wait_ge(sm["a_ready"], 2 * b + 2)
                for k in range(KT):
                    for t in range(TB):
                        last = turn(two(w2)[:, k, P * t:P * t + P], a_sb[:, t, P * k:P * k + P])
                last.then_inc(sm["aT_ps"], 1)

            def d_wo(b, par):
                pe.wait_ge(sm["aT_sb"], b + 1)
                for t in range(TB):
                    last = products(two(w2)[:, t, :], [(aT[:, k, P * t:P * t + P], wo_sb[:, k, :])
                                                       for k in range(KT)])
                last.then_inc(sm["wo_ps"], 1)

            def d_xn2T(b, par):
                pe.wait_ge(sm["xn2_ready"], TB * (b + 1))
                if exists(b + 2):
                    pe.wait_ge(sm["mT_sb"], 2 * b + 5)
                for k in range(KT):
                    for t in range(TB):
                        last = turn(two(w2)[:, k, P * t:P * t + P], xn2[:, t, P * k:P * k + P])
                last.then_inc(sm["xn2T_ps"], 1)

            def d_router(b, par):
                pe.wait_ge(sm["xn2T_sb"], b + 1)
                for t in range(TB):
                    last = products(w2[:, E * t:E * t + E], [(xn2T[:, k, P * t:P * t + P], wr_sb[:, k, :])
                                                             for k in range(KT)])
                last.then_inc(sm["rt_ps"], 1)

            steps = {"A_xnT": a_xnT, "A_ct": a_ct, "A_k0": a_k0, "A_q0": a_q0, "A_qk1": a_qk1, "A_v": a_v,
                     "SM": sm_scores, "M0": lambda b, par: m_turn(b, par, 0),
                     "M1": lambda b, par: m_turn(b, par, 1), "D_avT0": av_turn(0), "D_avT1": av_turn(1),
                     "D_aT": a_turn, "D_wo": d_wo, "D_xn2T": d_xn2T, "L_router": d_router}
            order = {0: ("L_router",), 1: ("M1",), 2: ("A_xnT", "D_avT0",), 3: ("A_ct", "D_avT1",),
                     4: ("D_aT", "A_k0",), 5: ("A_q0", "D_wo",), 7: ("A_qk1", "A_v",), 12: ("M0",),
                     15: ("D_xn2T",)}

            run_attention(pe, head, steps, order, behind)
            probs_v(B - 1, 1, NH - 1)
            for name, b in (("L_router", B - 2), ("D_avT0", B - 1)):
                steps[name](b, b % 2)

            def last_steps(*names):
                return lambda: [steps[name](B - 1, 1) for name in names]

            def ranks():
                pe.wait_ge(sm["oh_ready"], 1)
                flat = oh_bf[:, :, :].rearrange("p t e -> p (t e)")
                rank = bank[5][:, 0:NT * E].rearrange("p (t e) -> p t e", e=E)
                pe.matmul(bank[5][:, 0:NT * E], tri_bf[:, :], flat, start=True, stop=False,
                          skip_group_check=True)
                for j in range(NT - 1):
                    pe.matmul(rank[:, j + 1:NT, :], ones_bf[:, :],
                              oh_bf[:, j:j + 1, :].to_broadcast([P, NT - 1 - j, E]),
                              start=False, stop=(j == NT - 2), skip_group_check=True)
                for j in range(NT):
                    last = pe.matmul(bank[5][:, NT * E:NT * E + E], ones_bf[:, :], oh_bf[:, j, :],
                                     start=(j == 0), stop=(j == NT - 1))
                last.then_inc(sm["rank_ps"], 1)

            pe.wait_ge(sm["w_in"], 16 * (2 * (E - 2) + 3))

            def gate_up_of(kind, seq):
                if kind != "R":
                    return lambda k, r: wall[:, E, 2 * I * k + I * r:2 * I * k + I * r + I], \
                           lambda k: wall[:, E, KT * 2 * I + D * k:KT * 2 * I + D * k + D]
                e = pe.value_load(eid_i[0:1, ds(seq - R0, 1)], min_val=0, max_val=E - 1)
                flat_w = wall[:, :, :].rearrange("p e w -> p (e w)")
                return lambda k, r: flat_w[:, ds(e * WLEN + 2 * I * k + I * r, I)], \
                       lambda k: flat_w[:, ds(e * WLEN + KT * 2 * I + D * k, D)]

            def x_turn(seq, n, p):
                pe.wait_ge(sm[f"xl_in{p}"], 16 * (n + 1))
                for k in range(KT):
                    last = turn(bank[0][:, P * k:P * k + P], xl[:, p, P * k:P * k + P])
                last.then_inc(sm["xT_ps"], 1)

            def gate_and_up(seq, p, kind):
                w, _ = gate_up_of(kind, seq)
                pe.wait_ge(sm["xT_sb"], seq + 1)
                for r, sig in ((0, "g_ps"), (1, "u_ps")):
                    products(bank[1 + r][:, :], [(xT[:, p, P * k:P * k + P], w(k, r)) for k in range(KT)]
                             ).then_inc(sm[sig], 1)

            def front():
                x_turn(0, 0, 0)
                gate_and_up(0, 0, "A")
                x_turn(1, 0, 1)

            def body(seq, n, p, kinds):
                kind, then = kinds[0], kinds[1:2]
                pe.wait_ge(sm["h_sb"], seq + 1)
                for k in range(I // P):
                    last = turn(bank[3][:, P * k:P * k + P], hid[:, P * k:P * k + P])
                last.then_inc(sm["hT_ps"], 1)
                if then == "R" and kind == "A":
                    pe.wait_ge(sm["pos_ready"], 2)
                    pe.wait_ge(sm["w67_in"], 64)
                if then:
                    gate_and_up(seq + 1, 1 - p, then)
                if kinds[2:]:
                    x_turn(seq + 2, n + 1, p)
                _, w = gate_up_of(kind, seq)
                pe.wait_ge(sm["hT_sb"], seq + 1)
                if kind == "B" and not (isinstance(seq, int) and seq < B0 + 2):
                    pe.wait_ge(sm["z_ready"], 2 * (seq - B0) - 3)
                else:
                    if counted(seq - 1):
                        pe.wait_ge(sm["ys_sb"], seq - 1)
                products(y_bank[p][:, 0:D], [(hT[:, P * k:P * k + P], w(k)) for k in range(I // P)]
                         ).then_inc(sm["y_ps"], 1)

            between = {0: last_steps("D_avT1", "D_aT"), 1: last_steps("D_wo"),
                       2: last_steps("D_xn2T", "L_router"), 3: ranks}
            run_ffn(pe, front, body, between=between)


def kernel(**inputs):
    import concourse.bacc as bacc
    from concourse.bass_utils import run_bass_kernel_spmd

    g = {k: np.asarray(v) for k, v in inputs.items()}
    f = np.float32

    def padded(a, rows):
        return np.concatenate([np.zeros((rows, a.shape[1]), f), a], 0)

    wq = np.zeros((D, 2 * D), f)
    wq[0:DQ, 0:D] = head_minor(g["L0_attn_w_up_q"].T)
    wq[0:DQ, D:2 * D] = head_minor(g["L0_attn_wq_r"].T)
    wkv = np.concatenate([padded(head_minor(g["L0_attn_w_up_k"].T), P - DKV),
                          padded(head_minor(g["L0_attn_wk_r"].T), P - DKV),
                          padded(g["L0_attn_w_up_v"].T, P - DKV)], 1)
    col = np.zeros((P, 12), f)
    bd = np.concatenate([g["L0_attn_b_down_q"], g["L0_attn_b_down_kv"]]).reshape(2, P)
    bq, bqr, bk, bkr = (head_minor(g[f"L0_attn_{n}"]).reshape(2, P) for n in ("b_up_q", "bq_r", "b_up_k", "bk_r"))
    for c, v in ((0, bd[0]), (1, bd[1]), (2, bq[0]), (4, bqr[0]), (5, bk[0]), (6, bkr[0]),
                 (8, bq[1]), (9, bqr[1]), (10, bk[1]), (11, bkr[1])):
        col[:, c] = v
    arrays = {
        "x": g["L0_attn_x"].reshape(B * S, D),
        "const": constants(),
        "w_down": np.concatenate([g["L0_attn_w_down_q"].T, g["L0_attn_w_down_kv"].T], 1),
        "w_q": wq, "w_kv": wkv,
        "w_out": g["L0_attn_wo"].T, "w_router": g["L0_ffn_router_w"].T,
        "bias_col": col,
        "bias_v": np.zeros(0), "bias_o": np.zeros(0),
        "gate_up": g["L0_ffn_gate_up_proj"].reshape(E * D, 2 * I),
        "down": g["L0_ffn_down_proj"].reshape(E * I, D),
        "sh_gate": g["L0_ffn_shared_gate_w"], "sh_up": g["L0_ffn_shared_up_w"],
        "sh_down": g["L0_ffn_shared_down_w"],
    }
    arrays["bias_v"] = g["L0_attn_b_up_v"].reshape(1, D)
    arrays["bias_o"] = g["L0_attn_bo"].reshape(1, D)
    nc = bacc.Bacc("TRN2", target_bir_lowering=False, num_devices=1)
    aps = []
    for n in list(arrays):
        arrays[n] = np.ascontiguousarray(arrays[n])
        aps.append(nc.dram_tensor(n, list(arrays[n].shape), F32, kind="ExternalInput").ap())
    out = nc.dram_tensor("out", [B * S, D], F32, kind="ExternalOutput").ap()
    program(nc, *aps, out)
    r = run_bass_kernel_spmd(nc, [arrays], core_ids=[0])
    return r.results[0]["out"].reshape(B, S, D)
```
